# Optimizing a Trainium2 kernel written in Bass

```python
import numpy as np
import jax
import jax.numpy as jnp

def _softmax(x, axis=-1):
    return jax.nn.softmax(x, axis=axis)

def _gelu(x):
    return jax.nn.gelu(x, approximate=True)

def _silu(x):
    return jax.nn.silu(x)

def _sigmoid(x):
    return jax.nn.sigmoid(x)

def _layernorm(x, axis=-1, eps=1e-05):
    m = jnp.mean(x, axis=axis, keepdims=True)
    v = jnp.var(x, axis=axis, keepdims=True)
    return (x - m) / jnp.sqrt(v + eps)

def _scatter_add(tgt, idx, src, axis=0):
    return tgt.at[idx].add(src)

def _segment_sum(src, seg, n):
    return jax.ops.segment_sum(src, seg, n)
kernel_name = 'mk_flamingo_gated_d4_seqx_r4_8a89f1'

def setup_inputs(seed: int=0):
    np.random.seed(seed)
    _w = jnp.asarray

    def _rec_inputs():
        import jax
        import jax.numpy as jnp
        _rk = jax.random.key(seed)
        x = -0.0003929 + 0.9999 * jax.random.normal(jax.random.fold_in(_rk, 1), (8, 256, 256), jnp.float32)
        _lenS = 256 - jax.random.randint(jax.random.fold_in(_rk, 7), (8,), 0, max(1, 256 // 4) + 1, jnp.int32)
        _lenS2 = 256 - jax.random.randint(jax.random.fold_in(_rk, 8), (8,), 0, max(1, 256 // 4) + 1, jnp.int32)
        _ctx_768P = jax.random.normal(jax.random.fold_in(_rk, 11), (8, 16, 192), jnp.float32)
        _ctx_768c = jax.random.dirichlet(jax.random.fold_in(_rk, 511), 0.3 * jnp.ones((16,), jnp.float32), (8, 256))
        _ctx_768t = jnp.einsum('bsk,bkd->bsd', _ctx_768c, _ctx_768P)
        _ctx_768t = _ctx_768t * jax.lax.rsqrt(jnp.mean(jnp.square(_ctx_768t)) + 1e-12) * 0.953939
        ctx_768 = -7.36909e-05 + 0.999899 * (_ctx_768t + 0.3 * jax.random.normal(jax.random.fold_in(_rk, 611), (8, 256, 192), jnp.float32))
        _validS = jnp.arange(256)[None, :] < _lenS[:, None]
        _validS2 = jnp.arange(256)[None, :] < _lenS2[:, None]
        _causal = jnp.tril(jnp.ones((256, 256), dtype=bool))
        mask_BxS_bk0 = jnp.logical_not(jnp.broadcast_to(_validS[:, :], (8, 256)))
        _g = jax.random.normal(jax.random.fold_in(_rk, 9001), (2, 4), jnp.float32)
        _g = jnp.sign(_g) * jnp.maximum(jnp.abs(_g), 1.0) + (_g == 0) * 1.0
        g_xattn = _g[0]
        g_ffn = _g[1]
        return (x, ctx_768, mask_BxS_bk0, g_xattn, g_ffn)
    x, ctx_768, mask_BxS_bk0, g_xattn, g_ffn = _rec_inputs()

    def _L0_xattn_setup():
        import jax, jax.numpy as jnp
        import numpy as np
        EPS = 1e-08
        key = jax.random.key(seed)
        kv, kt, k1, k2, k3, k4 = jax.random.split(key, 6)
        B, S = (16, 256)
        VD, TD, H = (256, 192, 128)
        visual_features = jax.random.normal(kv, (B, S, VD), dtype=jnp.float32)
        text_features = jax.random.normal(kt, (B, S, TD), dtype=jnp.float32)
        Wv = jax.random.normal(k1, (H, VD), dtype=jnp.float32) * (1.0 / np.sqrt(VD))
        bv = jax.random.normal(k2, (H,), dtype=jnp.float32) * 0.01
        Wt = jax.random.normal(k3, (H, TD), dtype=jnp.float32) * (1.0 / np.sqrt(TD))
        bt = jax.random.normal(k4, (H,), dtype=jnp.float32) * 0.01
        return {'visual_features': visual_features, 'text_features': text_features, 'Wv': Wv, 'bv': bv, 'Wt': Wt, 'bt': bt}
    _L0_xattn_all = _L0_xattn_setup()
    _L0_xattn_in = {k: v for k, v in _L0_xattn_all.items() if k in ('Wv', 'bv', 'Wt', 'bt')}
    del _L0_xattn_all

    def _L0_ffn_setup():
        import jax, jax.numpy as jnp
        import numpy as np
        B, S, D, F, E = (2, 512, 256, 1024, 8)
        LN_EPS = 1e-05

        def _xavier(key, shape, fan_in, fan_out):
            a = np.sqrt(6.0 / (fan_in + fan_out))
            return jax.random.uniform(key, shape, jnp.float32, -a, a)
        key = jax.random.key(seed)
        ks = jax.random.split(key, 8)
        tgt = jax.random.normal(ks[0], (B, S, D), jnp.float32)
        router_w = _xavier(ks[1], (E, D), D, E)
        router_b = jnp.zeros((E,), jnp.float32)
        w1 = _xavier(ks[2], (E, D, F), D, F)
        b1 = jnp.zeros((E, F), jnp.float32)
        w2 = _xavier(ks[3], (E, F, D), F, D)
        b2 = jnp.zeros((E, D), jnp.float32)
        gamma = jnp.ones((D,), jnp.float32)
        beta = jnp.zeros((D,), jnp.float32)
        return {'tgt': tgt, 'router_w': router_w, 'router_b': router_b, 'w1': w1, 'b1': b1, 'w2': w2, 'b2': b2, 'gamma': gamma, 'beta': beta}
    _L0_ffn_all = _L0_ffn_setup()
    _L0_ffn_in = {k: v for k, v in _L0_ffn_all.items() if k in ('router_w', 'router_b', 'w1', 'b1', 'w2', 'b2', 'gamma', 'beta')}
    del _L0_ffn_all

    def _L1_xattn_setup():
        import jax, jax.numpy as jnp
        import numpy as np
        NUM_HEADS = 16
        key = jax.random.key(seed)
        k1, k2, k3, k4, k5 = jax.random.split(key, 5)
        B, N, C = (4, 512, 256)
        N2, Cy = (256, 192)
        x = jax.random.normal(k1, (B, N, C), dtype=jnp.float32)
        y = jax.random.normal(k2, (B, N2, Cy), dtype=jnp.float32)
        pad_mask = jax.random.randint(k3, (B, N), 0, 2).astype(jnp.bool_)
        Wq = jax.random.normal(k4, (C, C), dtype=jnp.float32) * C ** (-0.5)
        Wkv = jax.random.normal(k5, (2 * C, Cy), dtype=jnp.float32) * Cy ** (-0.5)
        return {'x': x, 'y': y, 'pad_mask': pad_mask, 'Wq': Wq, 'Wkv': Wkv}
    _L1_xattn_all = _L1_xattn_setup()
    _L1_xattn_in = {k: v for k, v in _L1_xattn_all.items() if k in ('Wq', 'Wkv')}
    del _L1_xattn_all

    def _L1_ffn_setup():
        import jax, jax.numpy as jnp
        import numpy as np
        EMB_DIM = 256
        HIDDEN = int(2 / 3 * 4 * EMB_DIM)
        NUM_EXPERTS = 8
        TOP_K = 2
        B, S = (4, 256)
        key = jax.random.key(seed)
        ks = jax.random.split(key, 5)
        sc = 1.0 / np.sqrt(EMB_DIM)
        sh = 1.0 / np.sqrt(HIDDEN)
        return {'x': jax.random.normal(ks[0], (B, S, EMB_DIM), dtype=jnp.float32), 'Wg': jax.random.normal(ks[1], (NUM_EXPERTS, EMB_DIM), dtype=jnp.float32) * sc, 'W1': jax.random.normal(ks[2], (NUM_EXPERTS, HIDDEN, EMB_DIM), dtype=jnp.float32) * sc, 'W2': jax.random.normal(ks[3], (NUM_EXPERTS, HIDDEN, EMB_DIM), dtype=jnp.float32) * sc, 'W3': jax.random.normal(ks[4], (NUM_EXPERTS, EMB_DIM, HIDDEN), dtype=jnp.float32) * sh}
    _L1_ffn_all = _L1_ffn_setup()
    _L1_ffn_in = {k: v for k, v in _L1_ffn_all.items() if k in ('Wg', 'W1', 'W2', 'W3')}
    del _L1_ffn_all

    def _L2_xattn_setup():
        import jax, jax.numpy as jnp
        import numpy as np
        HEADS = 16
        DIM_HEAD = 64
        QUERY_DIM = 256
        CONTEXT_DIM = 192
        INNER = HEADS * DIM_HEAD
        SCALE = DIM_HEAD ** (-0.5)
        key = jax.random.key(seed)
        ks = jax.random.split(key, 7)
        B, Sq, Skv = (4, 512, 512)
        x = jax.random.normal(ks[0], (B, Sq, QUERY_DIM), dtype=jnp.float32)
        context = jax.random.normal(ks[1], (B, Skv, CONTEXT_DIM), dtype=jnp.float32)
        w_q = jax.random.normal(ks[2], (QUERY_DIM, INNER), dtype=jnp.float32) / np.sqrt(QUERY_DIM)
        w_k = jax.random.normal(ks[3], (CONTEXT_DIM, INNER), dtype=jnp.float32) / np.sqrt(CONTEXT_DIM)
        w_v = jax.random.normal(ks[4], (CONTEXT_DIM, INNER), dtype=jnp.float32) / np.sqrt(CONTEXT_DIM)
        w_o = jax.random.normal(ks[5], (INNER, QUERY_DIM), dtype=jnp.float32) / np.sqrt(INNER)
        b_o = jax.random.normal(ks[6], (QUERY_DIM,), dtype=jnp.float32) * 0.02
        return {'x': x, 'context': context, 'w_q': w_q, 'w_k': w_k, 'w_v': w_v, 'w_o': w_o, 'b_o': b_o}
    _L2_xattn_all = _L2_xattn_setup()
    _L2_xattn_in = {k: v for k, v in _L2_xattn_all.items() if k in ('w_q', 'w_k', 'w_v', 'w_o', 'b_o')}
    del _L2_xattn_all

    def _L2_ffn_setup():
        import jax, jax.numpy as jnp
        import numpy as np
        DIM = 256
        INTER = 256
        N_EXPERTS = 8
        TOPK = 2
        N_SHARED = 2
        key = jax.random.key(seed)
        ks = jax.random.split(key, 10)
        s = 0.02
        return {'x': jax.random.normal(ks[0], (4, 512, DIM), dtype=jnp.float32), 'gate_w': jax.random.normal(ks[1], (N_EXPERTS, DIM), dtype=jnp.float32) * s, 'gate_bias': jax.random.normal(ks[2], (N_EXPERTS,), dtype=jnp.float32) * s, 'w1': jax.random.normal(ks[3], (N_EXPERTS, INTER, DIM), dtype=jnp.float32) * s, 'w3': jax.random.normal(ks[4], (N_EXPERTS, INTER, DIM), dtype=jnp.float32) * s, 'w2': jax.random.normal(ks[5], (N_EXPERTS, DIM, INTER), dtype=jnp.float32) * s, 'sw1': jax.random.normal(ks[6], (N_SHARED * INTER, DIM), dtype=jnp.float32) * s, 'sw3': jax.random.normal(ks[7], (N_SHARED * INTER, DIM), dtype=jnp.float32) * s, 'sw2': jax.random.normal(ks[8], (DIM, N_SHARED * INTER), dtype=jnp.float32) * s}
    _L2_ffn_all = _L2_ffn_setup()
    _L2_ffn_in = {k: v for k, v in _L2_ffn_all.items() if k in ('gate_w', 'gate_bias', 'w1', 'w3', 'w2', 'sw1', 'sw3', 'sw2')}
    del _L2_ffn_all

    def _L3_xattn_setup():
        import jax, jax.numpy as jnp
        import numpy as np
        NUM_HEADS = 16
        CLAMP = 10000.0
        key = jax.random.key(seed)
        ks = jax.random.split(key, 8)
        B, Nq, Nkv, Cq, Ckv = (4, 512, 512, 256, 192)
        s_q = 1.0 / np.sqrt(Cq)
        s_kv = 1.0 / np.sqrt(Ckv)
        return {'query': jax.random.normal(ks[0], (B, Nq, Cq), jnp.float32), 'key_value': jax.random.normal(ks[1], (B, Nkv, Ckv), jnp.float32), 'Wq': jax.random.normal(ks[2], (Cq, Cq), jnp.float32) * s_q, 'bq': jnp.zeros((Cq,), jnp.float32), 'Wk': jax.random.normal(ks[3], (Ckv, Cq), jnp.float32) * s_kv, 'bk': jnp.zeros((Cq,), jnp.float32), 'Wv': jax.random.normal(ks[4], (Ckv, Cq), jnp.float32) * s_kv, 'bv': jnp.zeros((Cq,), jnp.float32), 'Wo': jax.random.normal(ks[5], (Cq, Cq), jnp.float32) * s_q, 'bo': jnp.zeros((Cq,), jnp.float32)}
    _L3_xattn_all = _L3_xattn_setup()
    _L3_xattn_in = {k: v for k, v in _L3_xattn_all.items() if k in ('Wq', 'bq', 'Wk', 'bk', 'Wv', 'bv', 'Wo', 'bo')}
    del _L3_xattn_all

    def _L3_ffn_setup():
        import jax, jax.numpy as jnp
        import numpy as np
        B, N, C, H, REG = (1, 2309, 256, 16, 5)
        D = C // H
        key = jax.random.key(seed)
        k0, k1, k2, k3 = jax.random.split(key, 4)
        x = jax.random.normal(k0, (B, N, C), dtype=jnp.float32)
        g_info = jax.random.normal(k1, (12, 2, C), dtype=jnp.float32)
        W_qkv = jax.random.normal(k2, (C, 3 * C), dtype=jnp.float32) * 0.02
        W_proj = jax.random.normal(k3, (C, C), dtype=jnp.float32) * 0.02
        b_proj = jnp.zeros((C,), dtype=jnp.float32)
        return {'x': x, 'g_info': g_info, 'W_qkv': W_qkv, 'W_proj': W_proj, 'b_proj': b_proj}
    _L3_ffn_all = _L3_ffn_setup()
    _L3_ffn_in = {k: v for k, v in _L3_ffn_all.items() if k in ('g_info', 'W_qkv', 'W_proj', 'b_proj')}
    del _L3_ffn_all
    return {'x': x, 'ctx_768': ctx_768, 'mask_BxS_bk0': mask_BxS_bk0, 'g_xattn': g_xattn, 'g_ffn': g_ffn, 'L0_xattn_Wv': _L0_xattn_in['Wv'], 'L0_xattn_bv': _L0_xattn_in['bv'], 'L0_xattn_Wt': _L0_xattn_in['Wt'], 'L0_xattn_bt': _L0_xattn_in['bt'], 'L0_ffn_router_w': _L0_ffn_in['router_w'], 'L0_ffn_router_b': _L0_ffn_in['router_b'], 'L0_ffn_w1': _L0_ffn_in['w1'], 'L0_ffn_b1': _L0_ffn_in['b1'], 'L0_ffn_w2': _L0_ffn_in['w2'], 'L0_ffn_b2': _L0_ffn_in['b2'], 'L0_ffn_gamma': _L0_ffn_in['gamma'], 'L0_ffn_beta': _L0_ffn_in['beta'], 'L1_xattn_Wq': _L1_xattn_in['Wq'], 'L1_xattn_Wkv': _L1_xattn_in['Wkv'], 'L1_ffn_Wg': _L1_ffn_in['Wg'], 'L1_ffn_W1': _L1_ffn_in['W1'], 'L1_ffn_W2': _L1_ffn_in['W2'], 'L1_ffn_W3': _L1_ffn_in['W3'], 'L2_xattn_w_q': _L2_xattn_in['w_q'], 'L2_xattn_w_k': _L2_xattn_in['w_k'], 'L2_xattn_w_v': _L2_xattn_in['w_v'], 'L2_xattn_w_o': _L2_xattn_in['w_o'], 'L2_xattn_b_o': _L2_xattn_in['b_o'], 'L2_ffn_gate_w': _L2_ffn_in['gate_w'], 'L2_ffn_gate_bias': _L2_ffn_in['gate_bias'], 'L2_ffn_w1': _L2_ffn_in['w1'], 'L2_ffn_w3': _L2_ffn_in['w3'], 'L2_ffn_w2': _L2_ffn_in['w2'], 'L2_ffn_sw1': _L2_ffn_in['sw1'], 'L2_ffn_sw3': _L2_ffn_in['sw3'], 'L2_ffn_sw2': _L2_ffn_in['sw2'], 'L3_xattn_Wq': _L3_xattn_in['Wq'], 'L3_xattn_bq': _L3_xattn_in['bq'], 'L3_xattn_Wk': _L3_xattn_in['Wk'], 'L3_xattn_bk': _L3_xattn_in['bk'], 'L3_xattn_Wv': _L3_xattn_in['Wv'], 'L3_xattn_bv': _L3_xattn_in['bv'], 'L3_xattn_Wo': _L3_xattn_in['Wo'], 'L3_xattn_bo': _L3_xattn_in['bo'], 'L3_ffn_g_info': _L3_ffn_in['g_info'], 'L3_ffn_W_qkv': _L3_ffn_in['W_qkv'], 'L3_ffn_W_proj': _L3_ffn_in['W_proj'], 'L3_ffn_b_proj': _L3_ffn_in['b_proj']}

def reference(x, ctx_768, mask_BxS_bk0, g_xattn, g_ffn, L0_xattn_Wv, L0_xattn_bv, L0_xattn_Wt, L0_xattn_bt, L0_ffn_router_w, L0_ffn_router_b, L0_ffn_w1, L0_ffn_b1, L0_ffn_w2, L0_ffn_b2, L0_ffn_gamma, L0_ffn_beta, L1_xattn_Wq, L1_xattn_Wkv, L1_ffn_Wg, L1_ffn_W1, L1_ffn_W2, L1_ffn_W3, L2_xattn_w_q, L2_xattn_w_k, L2_xattn_w_v, L2_xattn_w_o, L2_xattn_b_o, L2_ffn_gate_w, L2_ffn_gate_bias, L2_ffn_w1, L2_ffn_w3, L2_ffn_w2, L2_ffn_sw1, L2_ffn_sw3, L2_ffn_sw2, L3_xattn_Wq, L3_xattn_bq, L3_xattn_Wk, L3_xattn_bk, L3_xattn_Wv, L3_xattn_bv, L3_xattn_Wo, L3_xattn_bo, L3_ffn_g_info, L3_ffn_W_qkv, L3_ffn_W_proj, L3_ffn_b_proj):
    import jax
    import jax.numpy as jnp

    def _L0_xattn_ref(visual_features, text_features, Wv, bv, Wt, bt):
        import jax, jax.numpy as jnp
        import numpy as np
        EPS = 1e-08
        v = jnp.einsum('bsd,hd->bsh', visual_features, Wv) + bv
        t = jnp.einsum('bsd,hd->bsh', text_features, Wt) + bt
        dots = jnp.einsum('bih,bjh->bij', v, t)
        vn = jnp.linalg.norm(v, axis=-1)
        tn = jnp.linalg.norm(t, axis=-1)
        denom = jnp.maximum(vn[:, :, None] * tn[:, None, :], EPS)
        return dots / denom

    def _L0_ffn_ref(tgt, router_w, router_b, w1, b1, w2, b2, gamma, beta):
        import jax, jax.numpy as jnp
        import numpy as np
        B, S, D, F, E = (2, 512, 256, 1024, 8)
        LN_EPS = 1e-05

        def _xavier(key, shape, fan_in, fan_out):
            a = np.sqrt(6.0 / (fan_in + fan_out))
            return jax.random.uniform(key, shape, jnp.float32, -a, a)
        logits = jnp.einsum('bsd,ed->bse', tgt, router_w) + router_b
        rw = jax.nn.softmax(logits, axis=-1)
        rw = jnp.zeros_like(rw).at[..., 0].set(1.0)
        h = jax.nn.relu(jnp.einsum('bsd,edf->besf', tgt, w1) + b1[None, :, None, :])
        eo = jnp.einsum('besf,efd->besd', h, w2) + b2[None, :, None, :]
        tgt2 = jnp.einsum('besd,bse->bsd', eo, rw)
        x = tgt + tgt2
        mean = jnp.mean(x, axis=-1, keepdims=True)
        var = jnp.mean(jnp.square(x - mean), axis=-1, keepdims=True)
        return (x - mean) * jax.lax.rsqrt(var + LN_EPS) * gamma + beta

    def _L1_xattn_ref(x, y, pad_mask, Wq, Wkv):
        import jax, jax.numpy as jnp
        import numpy as np
        NUM_HEADS = 16
        B, N, C = x.shape
        N2 = y.shape[1]
        H = NUM_HEADS
        d = C // H
        scale = d ** (-0.5)
        q = (x @ Wq.T).reshape(B, N, H, d).transpose(0, 2, 1, 3)
        kv = (y @ Wkv.T).reshape(B, N2, 2, H, d).transpose(2, 0, 3, 1, 4)
        k, v = (kv[0], kv[1])
        attn = jnp.einsum('bhnd,bhmd->bhnm', q * scale, k)
        attn = jnp.where(pad_mask[:, None, :, None], attn, jnp.float32(-1000000000.0))
        attn = jax.nn.softmax(attn, axis=-1)
        out = jnp.einsum('bhnm,bhmd->bhnd', attn, v)
        return out.transpose(0, 2, 1, 3).reshape(B, N, C)

    def _L1_ffn_ref(x, Wg, W1, W2, W3):
        import jax, jax.numpy as jnp
        import numpy as np
        EMB_DIM = 256
        HIDDEN = int(2 / 3 * 4 * EMB_DIM)
        NUM_EXPERTS = 8
        TOP_K = 2
        B, S = (4, 256)
        gate_logits = jnp.einsum('bsd,ed->bse', x, Wg)
        top_v, top_i = jax.lax.top_k(gate_logits, TOP_K)
        mask = jnp.any(top_i[..., :, None] == jnp.arange(NUM_EXPERTS), axis=-2)
        sparse_logits = jnp.where(mask, gate_logits, -jnp.inf)
        gating = jax.nn.softmax(sparse_logits, axis=-1)
        h1 = jnp.einsum('bsd,ehd->bseh', x, W1)
        h2 = jnp.einsum('bsd,ehd->bseh', x, W2)
        hidden = jax.nn.silu(h1) * h2
        expert_out = jnp.einsum('bseh,edh->bsed', hidden, W3)
        return jnp.einsum('bsed,bse->bsd', expert_out, gating)

    def _L2_xattn_ref(x, context, w_q, w_k, w_v, w_o, b_o):
        import jax, jax.numpy as jnp
        import numpy as np
        HEADS = 16
        DIM_HEAD = 64
        QUERY_DIM = 256
        CONTEXT_DIM = 192
        INNER = HEADS * DIM_HEAD
        SCALE = DIM_HEAD ** (-0.5)
        B, Sq, _ = x.shape
        Skv = context.shape[1]
        q = (x @ w_q).reshape(B, Sq, HEADS, DIM_HEAD).transpose(0, 2, 1, 3)
        k = (context @ w_k).reshape(B, Skv, HEADS, DIM_HEAD).transpose(0, 2, 1, 3)
        v = (context @ w_v).reshape(B, Skv, HEADS, DIM_HEAD).transpose(0, 2, 1, 3)
        sim = jnp.einsum('bhid,bhjd->bhij', q, k) * SCALE
        attn = jax.nn.softmax(sim, axis=-1)
        out = jnp.einsum('bhij,bhjd->bhid', attn, v)
        out = out.transpose(0, 2, 1, 3).reshape(B, Sq, INNER)
        return out @ w_o + b_o

    def _L2_ffn_ref(x, gate_w, gate_bias, w1, w3, w2, sw1, sw3, sw2):
        import jax, jax.numpy as jnp
        import numpy as np
        DIM = 256
        INTER = 256
        N_EXPERTS = 8
        TOPK = 2
        N_SHARED = 2
        shape = x.shape
        xt = x.reshape(-1, shape[-1])
        scores = jax.nn.softmax((xt @ gate_w.T).astype(jnp.float32), axis=-1)
        _, idx = jax.lax.top_k(scores + gate_bias, TOPK)
        weights = jnp.take_along_axis(scores, idx, axis=1).astype(x.dtype)
        y = jnp.zeros_like(xt)
        for e in range(N_EXPERTS):
            gate_e = jnp.sum(jnp.where(idx == e, weights, 0.0), axis=1)
            h = jax.nn.silu(xt @ w1[e].T) * (xt @ w3[e].T)
            y = y + gate_e[:, None] * (h @ w2[e].T)
        z = jax.nn.silu(xt @ sw1.T) * (xt @ sw3.T) @ sw2.T
        return (y + z).reshape(shape)

    def _L3_xattn_ref(query, key_value, Wq, bq, Wk, bk, Wv, bv, Wo, bo):
        import jax, jax.numpy as jnp
        import numpy as np
        NUM_HEADS = 16
        CLAMP = 10000.0
        B, Nq, Cq = query.shape
        Nkv = key_value.shape[1]
        H = NUM_HEADS
        D = Cq // H
        scale = D ** (-0.5)
        q = (query @ Wq + bq).reshape(B, Nq, H, D).transpose(0, 2, 1, 3)
        k = (key_value @ Wk + bk).reshape(B, Nkv, H, D).transpose(0, 2, 1, 3)
        v = (key_value @ Wv + bv).reshape(B, Nkv, H, D).transpose(0, 2, 1, 3)
        attn = jnp.einsum('bhqd,bhkd->bhqk', q, k) * scale
        attn = jnp.clip(attn, -CLAMP, CLAMP)
        attn = jax.nn.softmax(attn, axis=-1)
        attn = jnp.where(jnp.any(jnp.isnan(attn)), jnp.asarray(1.0 / Nkv, attn.dtype), attn)
        x = jnp.einsum('bhqk,bhkd->bqhd', attn, v).reshape(B, Nq, Cq)
        return x @ Wo + bo

    def _L3_ffn_ref(x, g_info, W_qkv, W_proj, b_proj):
        import jax, jax.numpy as jnp
        import numpy as np
        B, N, C, H, REG = (1, 2309, 256, 16, 5)
        D = C // H
        Bx, Nx, Cx = x.shape
        scale = D ** (-0.5)
        qkv = (x @ W_qkv).reshape(Bx, Nx, 3, H, D)
        q, k, v = (qkv[:, :, 0], qkv[:, :, 1], qkv[:, :, 2])
        g_layer = g_info[0].reshape(-1, H, D)
        q_g = g_layer[0]
        q_pure = q[:, REG:]
        q_n = q_pure / jnp.linalg.norm(q_pure, axis=-1, keepdims=True)
        qg_n = q_g / jnp.linalg.norm(q_g, axis=-1, keepdims=True)
        sim = (qg_n[None, None] * q_n).sum(-1).mean(-1)
        sim = (sim - sim.min()) / (sim.max() - sim.min())
        pos = sim > 0.9
        logits = jnp.einsum('bqhd,bkhd->bhqk', q * scale, k)

        def masked_attn(tok_mask):
            key_mask = jnp.concatenate([jnp.ones((Bx, REG), bool), tok_mask], axis=1)
            l = jnp.where(key_mask[:, None, None, :], logits, -jnp.inf)
            a = jax.nn.softmax(l, axis=-1)
            return jnp.einsum('bhqk,bkhd->bqhd', a, v)
        x_pos = masked_attn(pos)
        x_neg = masked_attn(~pos)
        reg_out = (x_pos[:, :REG] + x_neg[:, :REG]) * 0.5
        tok_out = jnp.where(pos[:, :, None, None], x_pos[:, REG:], x_neg[:, REG:])
        out = jnp.concatenate([reg_out, tok_out], axis=1).reshape(Bx, Nx, Cx)
        return out @ W_proj + b_proj
    x = x + jnp.tanh(g_xattn[0]) * _L0_xattn_ref(_layernorm(x, axis=-1), ctx_768, L0_xattn_Wv, L0_xattn_bv, L0_xattn_Wt, L0_xattn_bt)
    x = x + jnp.tanh(g_ffn[0]) * _L0_ffn_ref(_layernorm(x, axis=-1), L0_ffn_router_w, L0_ffn_router_b, L0_ffn_w1, L0_ffn_b1, L0_ffn_w2, L0_ffn_b2, L0_ffn_gamma, L0_ffn_beta)
    x = x + jnp.tanh(g_xattn[1]) * _L1_xattn_ref(_layernorm(x, axis=-1), ctx_768, mask_BxS_bk0, L1_xattn_Wq, L1_xattn_Wkv)
    x = x + jnp.tanh(g_ffn[1]) * _L1_ffn_ref(_layernorm(x, axis=-1), L1_ffn_Wg, L1_ffn_W1, L1_ffn_W2, L1_ffn_W3)
    x = x + jnp.tanh(g_xattn[2]) * _L2_xattn_ref(_layernorm(x, axis=-1), ctx_768, L2_xattn_w_q, L2_xattn_w_k, L2_xattn_w_v, L2_xattn_w_o, L2_xattn_b_o)
    x = x + jnp.tanh(g_ffn[2]) * _L2_ffn_ref(_layernorm(x, axis=-1), L2_ffn_gate_w, L2_ffn_gate_bias, L2_ffn_w1, L2_ffn_w3, L2_ffn_w2, L2_ffn_sw1, L2_ffn_sw3, L2_ffn_sw2)
    x = x + jnp.tanh(g_xattn[3]) * _L3_xattn_ref(_layernorm(x, axis=-1), ctx_768, L3_xattn_Wq, L3_xattn_bq, L3_xattn_Wk, L3_xattn_bk, L3_xattn_Wv, L3_xattn_bv, L3_xattn_Wo, L3_xattn_bo)
    x = x + jnp.tanh(g_ffn[3]) * _L3_ffn_ref(_layernorm(x, axis=-1), L3_ffn_g_info, L3_ffn_W_qkv, L3_ffn_W_proj, L3_ffn_b_proj)
    return x

_drawn_inputs = setup_inputs


def setup_inputs(seed=0):
    import zlib

    import numpy as np

    out = dict(_drawn_inputs(seed))
    spreads = {'L0_ffn_router_b': (0.0, 0.1),
     'L0_ffn_b1': (0.0, 0.1),
     'L0_ffn_b2': (0.0, 0.1),
     'L0_ffn_gamma': (1.0, 0.2),
     'L0_ffn_beta': (0.0, 0.1),
     'L3_xattn_bq': (0.0, 2.0),
     'L3_xattn_bk': (0.0, 2.0),
     'L3_xattn_bv': (0.0, 0.8),
     'L3_xattn_bo': (0.0, 0.8),
     'L3_ffn_b_proj': (0.0, 0.723)}
    factors = {'g_ffn': 26.168,
     'L0_xattn_bv': 8.0,
     'L0_xattn_bt': 62.838,
     'L2_xattn_b_o': 3.555,
     'L2_ffn_gate_w': 8.0,
     'L2_ffn_gate_bias': 8.0,
     'L2_ffn_w1': 8.0,
     'L2_ffn_w3': 8.0,
     'L2_ffn_w2': 8.0,
     'L2_ffn_sw1': 3.139,
     'L2_ffn_sw3': 3.044,
     'L2_ffn_sw2': 3.068,
     'L3_ffn_g_info': 64.0,
     'L3_xattn_Wq': 2.889,
     'L3_ffn_W_qkv': 8.0,
     'L3_ffn_W_proj': 8.0}
    for name, (base, spread) in spreads.items():
        noise = np.random.default_rng([zlib.crc32(name.encode()), seed]).standard_normal(out[name].shape)
        drawn = base * np.exp(spread * noise) if base else spread * noise
        out[name] = jnp.asarray(drawn.astype(out[name].dtype))
    for name, factor in factors.items():
        out[name] = (out[name] * factor).astype(out[name].dtype)
    return out
```

```python
from contextlib import ExitStack

import concourse.bass as bass
from concourse import mybir

F32 = mybir.dt.float32
U8 = mybir.dt.uint8
ALU = mybir.AluOpType
ACT = mybir.ActivationFunctionType
AXX = mybir.AxisListType.X
RMAX = bass.bass_isa.ReduceOp.max

P = 128
B, S, D = 8, 256, 256
T = S // P
NT = B * T
DC = D // P
CTX, CK = 192, 96
NH = 16
HV = 128
F0 = 1024
F1 = 682
F1T = -(-F1 // P)
F2 = 256
NE = 8
NREG = 5
NX = NREG * NH
LN_EPS = 1e-5
COS_EPS = 1e-8
CLAMP = 10000.0
FAR = 1e30


class Attn:

    def __init__(self, name, d, qscale, proj=False, bias=False, mask=False, clip=False, split=False):
        self.name, self.d, self.qscale = name, d, qscale
        self.proj, self.bias, self.mask, self.clip, self.split = proj, bias, mask, clip, split
        self.rows = 32 if d == 16 else 64
        self.per = P // self.rows
        self.groups = NH // self.per
        self.width = NH * d
        self.vs = d + 1 if d == 16 else d
        self.ones = self.vs > d
        self.kdim, self.kt = (P, DC) if split else (CK, 2)
        self.units = NH + (1 if split else 0)
        self.qjobs = self.groups // 2
        self.vjobs = T * self.width // 512


L1X = Attn("l1x", 16, 0.25, mask=True)
L2X = Attn("l2x", 64, 0.125, proj=True, bias=False)
L3X = Attn("l3x", 16, 0.25, proj=True, bias=True, clip=True)
L3F = Attn("l3f", 16, 0.25, proj=True, split=True)


class Chain:

    def __init__(self, eng, sem):
        self.eng, self.sem, self.base, self.k, self.total = eng, sem, 0, 0, 0

    def loop(self, i, per):
        self.total = self.base = self.total + self.k
        self.base = self.total + i * per
        self.k, self.per = 0, per

    def leave(self, n):
        assert self.k == self.per, f"{self.sem}: {self.k} increments in the body, {self.per} said"
        self.total += n * self.per
        self.base, self.k = self.total, 0

    def link(self, ins):
        self.k += 1
        ins.then_inc(self.sem, 1)
        self.eng.wait_ge(self.sem, self.base + self.k)


def build(nc, a, out, layers=8):
    ctx = ExitStack()
    with ctx:
        def sb(name, shape, dt=F32):
            return ctx.enter_context(nc.sbuf_tensor(name, shape, dt))

        def sem(name):
            return ctx.enter_context(nc.semaphore(name))

        bank = [ctx.enter_context(nc.psum_tensor(f"bank{k}", [P, 512], F32)) for k in range(8)]

        x = sb("x", [P, NT, D])
        ident = sb("ident", [P, P])
        ones = sb("ones", [P, P])
        gates_x = sb("gates_x", [P, 4])
        gates_f = sb("gates_f", [P, 4])
        tgx = sb("tgx", [P, 4])
        tgf = sb("tgf", [P, 4])
        mask_u8 = sb("mask_u8", [P, B * S], U8)
        w0v = sb("w0v", [P, DC, HV]); w0t = sb("w0t", [CK, 2, HV])
        b0v = sb("b0v", [P, 1]); b0t = sb("b0t", [P, 1])
        wq = {s.name: sb(f"wq_{s.name}", [P, DC, s.groups * P]) for s in (L1X, L2X, L3X, L3F)}
        wk = {s.name: sb(f"wk_{s.name}", [s.kdim, s.kt, s.groups * P]) for s in (L1X, L2X, L3X, L3F)}
        wv = {s.name: sb(f"wv_{s.name}", [s.kdim, s.kt, s.width]) for s in (L1X, L2X, L3X, L3F)}
        wo = {s.name: sb(f"wo_{s.name}", [P, s.width // P, D]) for s in (L2X, L3X, L3F)}
        bo = {s.name: sb(f"bo_{s.name}", [P, D]) for s in (L2X, L3X, L3F)}
        bq3 = sb("bq3", [P, 4]); bk3 = sb("bk3", [P, 4]); bv3 = sb("bv3", [P, D])
        b01 = sb("b01", [P, F0 // P]); b02 = sb("b02", [P, D])
        gam = sb("gam", [P, D]); bet = sb("bet", [P, D])
        wg1 = sb("wg1", [P, DC, NE]); wg2 = sb("wg2", [P, DC, NE]); gb2 = sb("gb2", [P, NE])
        wqs = sb("wqs", [P, DC, D]); qg = sb("qg", [P, D])
        EW = 2 * DC * F1 + F1T * D
        ew = sb("ew", [P, 2, EW])
        w01 = ew[:, 0, 0:DC * F0 // 2 * 2].rearrange("p (c f) -> p c f", c=DC)
        w02 = ew[:, 1, 0:F0 // P * D].rearrange("p (c f) -> p c f", c=F0 // P)

        def expert(u, f):
            ft = -(-f // P)
            n = DC * f
            return (ew[:, u, 0:n].rearrange("p (c f) -> p c f", c=DC),
                    ew[:, u, n:2 * n].rearrange("p (c f) -> p c f", c=DC),
                    ew[:, u, 2 * n:2 * n + ft * D].rearrange("p (c f) -> p c f", c=ft))

        xn = sb("xn", [P, T, D])
        xt = sb("xt", [P, DC, S])
        ct = sb("ct", [CK, 2, S])
        bst = sb("bst", [P, T, 6]); mv = sb("mv", [P, T, 2]); rstd = sb("rstd", [P, T])
        ARENA = 8 * S * 2 + T * NH * 64 + 4 * 512 + 2 * D
        arena = sb("arena", [P, ARENA + 4096])
        o = [0]

        def cut(n):
            o[0] += n
            return arena[:, o[0] - n:o[0]]

        qT = cut(8 * S).rearrange("p (g s) -> p g s", g=8)
        kT = cut(8 * S).rearrange("p (g s) -> p g s", g=8)
        v = cut(T * NH * 64).rearrange("p (t n) -> p t n", t=T)
        prob = [cut(512) for _ in range(2)]
        probT = [cut(512) for _ in range(2)]
        on = cut(NH * 64)
        oT = cut(NH * 64).rearrange("p (c s) -> p c s", c=8)
        hid0 = arena[:, 0:F0 // P * S].rearrange("p (c s) -> p c s", s=S)
        o[0] = 0
        xt_all = cut(DC * NT * P).rearrange("p (c s) -> p c s", c=DC)
        hid = [cut(F1T * 512).rearrange("p (c s) -> p c s", c=F1T) for _ in range(2)]
        assert o[0] <= ARENA + 4096, (o[0], ARENA)
        sil = [sb(f"sil{k}", [P, 512]) for k in range(2)]
        sc = sil
        scr = sb("scr", [P, NT * NE * NE])
        tmp = scr[:, 0:D]
        z = scr[:, D:2 * D]
        nmax = sb("nmax", [P, NH + 1, T])
        esum = sb("esum", [P, NH, T])
        rec = sb("rec", [P, NH])
        idle = sb("idle", [P, 1])
        norms = sb("norms", [P, 2 * T])
        diag = sb("diag", [P, T, P])
        mhalf = sb("mhalf", [P, 2 * NH])
        gate = sb("gate", [P, NT, 10])
        lg = sb("lg", [P, NT, NE]); sel = sb("sel", [P, NT, NE]); gm = sb("gm", [P, NT])
        larger = sb("larger", [P, NT, NE])
        tri = sb("tri", [P, NE, NE])
        sim = sb("sim", [P, NT]); regm = sb("regm", [P, NT]); ss = sb("ss", [P, 4 * NH])
        qp = sb("qp", [P, NT, 2]); kp = sb("kp", [P, NT, 2]); qk2 = sb("qk2", [P, T, 4])
        mrow = sb("mrow", [P, 2, S]); mregq = sb("mregq", [P, NREG]); selw = sb("selw", [P, P])
        qxs = sb("qxs", [P, 4 * NREG]); qx = sb("qx", [P, 4, NX])
        hm = sb("hm", [P, 4, NH]); bm = sb("bm", [P, NH]); rsel = sb("rsel", [P, P]); wcol = sb("wcol", [P, 1])
        onx = sb("onx", [P, D])

        names = ("x_in", "w0_in", "w0f_in", "att_in", "consts", "tanh", "phase", "out_done",
                 "xn", "xnT", "xt")
        g = {n: sem(n) for n in names}

        def group(p, *ns):
            return {n: sem(f"{p}_{n}") for n in ns}

        ph = {}
        for s in (L1X, L2X, L3X, L3F):
            ph[s.name] = group(s.name, "ct", "q", "k", "v", "qc", "kc", "vc",
                               "s", "mx", "e", "pT", "pTc", "pv", "dve", "rq", "rd",
                               *(("on", "onT", "oT", "y") if s.proj else ()), *(("x2",) if s.split else ()))
        l0x = group("l0x", "rq", "rd", "ct", "vt", "vtc", "dots", "dg", "rows", "dve", "act")
        l0f = group("l0f", "rq", "rd", "h", "hc", "y", "dve")
        moe = {}
        for n in ("l1f", "l2f"):
            moe[n] = group(n, "rq", "rd", "lg", "gd", "ga", "w0", "w1",
                           "a", "sil", "hid", "y", "yc", "dve")
        sm = group("sim", "rq", "rd", "q", "dve", "pool")

        block = ctx.enter_context(nc.Block())
        n_phase = {"l0x": 1, "l0f": 2, "l1x": 3, "l1f": 4, "l2x": 5, "l2f": 6, "l3x": 7, "sim": 8, "l3f": 9}
        order = [["l0x"], ["l0f"], ["l1x"], ["l1f"], ["l2x"], ["l2f"], ["l3x"], ["sim", "l3f"]]
        run = [n for l in order[:layers] for n in l]
        attn = {s.name: s for s in (L1X, L2X, L3X, L3F)}

        def entries(name, n):
            return n + (n_phase[name] - 1) * B

        @block.sync
        def _(sp):
            sp.dma_start(x[:, :, :], a["x"].rearrange("b (t p) d -> p (b t) d", p=P)).then_inc(g["x_in"], 16)
            for dst, src in ((w0v[:, :, :], a["w0v"]), (w0t[:, :, :], a["w0t"]), (b0v[:, :], a["b0v"]),
                             (b0t[:, :], a["b0t"]), (gates_x[:, :], a["g_xattn"].partition_broadcast(P)),
                             (gates_f[:, :], a["g_ffn"].partition_broadcast(P))):
                sp.dma_start(dst, src).then_inc(g["w0_in"], 16)

            def contexts(name, sem_in, sem_used, per):
                if n_phase[name] > 1:
                    sp.wait_ge(g["phase"], n_phase[name] - 1)
                sp.dma_start(ct[:, :, :], a["ctxT"][0, :, :, :]).then_inc(sem_in, 16)
                with sp.Fori(1, B) as n:
                    sp.wait_ge(sem_used, n * per)
                    sp.dma_start(ct[:, :, :], a["ctxT"][n, :, :, :]).then_inc(sem_in, 16)

            contexts("l0x", l0x["ct"], l0x["vt"], 1)
            def expert_size(f):
                return 2 * DC * f + -(-f // P) * D

            def first_experts(name, f, src):
                sp.wait_ge(g["phase"], 2 if name == "l1f" else 4)
                for u in range(2):
                    sp.dma_start(ew[:, u, 0:expert_size(f)], src[u, :, :]).then_inc(moe[name][f"w{u}"], 16)

            def more_experts(name, f, src, ne):
                with sp.Fori(1, ne // 2) as i:
                    for u in range(2):
                        sp.wait_ge(moe[name]["y"], (i * 2 + u - 1) * NT)
                        sp.dma_start(ew[:, u, 0:expert_size(f)], src[i * 2 + u, :, :])\
                            .then_inc(moe[name][f"w{u}"], 16)

            if "l1f" in run:
                first_experts("l1f", F1, a["we1"])
            if "l1x" in run:
                contexts("l1x", ph["l1x"]["ct"], ph["l1x"]["v"], L1X.vjobs)
            if "l1f" in run:
                more_experts("l1f", F1, a["we1"], NE)
            if "l2f" in run:
                first_experts("l2f", F2, a["we2"])
            if "l2x" in run:
                contexts("l2x", ph["l2x"]["ct"], ph["l2x"]["v"], L2X.vjobs)
            if "l2f" in run:
                more_experts("l2f", F2, a["we2"], NE + 2)
            if "l3x" in run:
                contexts("l3x", ph["l3x"]["ct"], ph["l3x"]["v"], L3X.vjobs)
            sp.wait_ge(g["phase"], len(run))
            sp.dma_start(out.rearrange("b (t p) d -> p (b t) d", p=P), x[:, :, :]).then_inc(g["out_done"], 16)
            sp.wait_ge(g["out_done"], 16)

        @block.gpsimd
        def _(pool):
            nc.gpsimd.memset(ident[:, :], 0.0).then_inc(g["consts"], 1)
            nc.gpsimd.memset(ones[:, :], 1.0).then_inc(g["consts"], 1)
            nc.gpsimd.memset(tri[:, :, :], 1.0).then_inc(g["consts"], 1)
            nc.gpsimd.memset(regm[:, :], 0.0).then_inc(g["consts"], 1)
            nc.gpsimd.memset(mrow[:, :, :], 0.0).then_inc(g["consts"], 1)
            nc.gpsimd.memset(mregq[:, :], 0.0).then_inc(g["consts"], 1)
            nc.gpsimd.memset(selw[:, :], 0.0).then_inc(g["consts"], 1)
            nc.gpsimd.memset(hm[:, :, :], 0.0).then_inc(g["consts"], 1)
            nc.gpsimd.memset(bm[:, :], 0.0).then_inc(g["consts"], 1)
            nc.gpsimd.memset(rsel[:, :], 0.5).then_inc(g["consts"], 1)
            nc.gpsimd.memset(wcol[:, :], 1.0).then_inc(g["consts"], 1)
            nc.gpsimd.memset(mhalf[:, :], -0.5).then_inc(g["consts"], 1)
            done = [12]

            def select(t, fill, base, pattern, cm, op=ALU.not_equal):
                pool.wait_ge(g["consts"], done[0])
                nc.gpsimd.affine_select(out=t, in_=t, compare_op=op, fill=fill, base=base,
                                        pattern=pattern, channel_multiplier=cm).then_inc(g["consts"], 1)
                done[0] += 1

            select(ident[:, :], 1.0, 0, [[-1, P]], 1)
            select(tri[:, :, :], 0.0, 0, [[1, NE], [-1, NE]], 0, ALU.is_gt)
            reg = regm[:, :].rearrange("p (b t) -> p b t", t=T)[:, :, 0:1]
            select(reg, 1.0, -NREG, [[0, B], [0, 1]], 1, ALU.is_ge)
            select(mregq[:, :], 1.0, -1, [[0, NREG]], 1)
            select(selw[:, :].rearrange("p (h r) -> p h r", r=32), 1.0, -16, [[0, 4], [1, 32]], -1)
            select(selw[:, :], 0.0, 1, [[0, P]], -1, ALU.is_ge)
            pool.wait_ge(g["consts"], done[0])
            nc.gpsimd.memset(hm[:, :, :], 1.0).then_inc(g["consts"], 1)
            done[0] += 1
            select(hm[:, :, :], 0.0, 0, [[128, 4], [-32, NH]], 1, ALU.is_ge)
            select(hm[:, :, :], 0.0, 31, [[-128, 4], [32, NH]], -1, ALU.is_ge)
            for r in range(NREG):
                select(bm[:, :], 1.0, -NH * r, [[-1, NH]], 1)
            select(rsel[:, :], 0.0, 0, [[-NH, P]], 1, ALU.is_ge)
            select(rsel[:, :], 0.0, NH - 1, [[NH, P]], -1, ALU.is_ge)
            select(wcol[:, :], 0.5, -NREG, [[0, 1]], 1, ALU.is_ge)
            g["n_consts"] = done[0]

            pool.dma_start(w01, a["w01"]).then_inc(g["w0f_in"], 16)
            pool.dma_start(w02, a["w02"]).then_inc(g["w0f_in"], 16)
            loads = [(b01[:, :], a["b01"]), (b02[:, :], a["b02"].partition_broadcast(P)),
                     (gam[:, :], a["gamma"].partition_broadcast(P)), (bet[:, :], a["beta"].partition_broadcast(P)),
                     (mask_u8[:, :], a["mask"].partition_broadcast(P))]
            for s in (L1X, L2X, L3X, L3F):
                loads += [(wq[s.name][:, :, :], a[f"wq_{s.name}"]), (wk[s.name][:, :, :], a[f"wk_{s.name}"]),
                          (wv[s.name][:, :, :], a[f"wv_{s.name}"])]
                if s.proj:
                    loads += [(wo[s.name][:, :, :], a[f"wo_{s.name}"]),
                              (bo[s.name][:, :], a[f"bo_{s.name}"].partition_broadcast(P))]
            loads += [(bq3[:, :], a["bq3"]), (bk3[:, :], a["bk3"]), (bv3[:, :], a["bv3"].partition_broadcast(P)),
                      (wg1[:, :, :], a["wg1"]), (wg2[:, :, :], a["wg2"]), (gb2[:, :], a["gb2"].partition_broadcast(P)),
                      (wqs[:, :, :], a["wqs"]), (qg[:, :], a["qg"].partition_broadcast(P))]
            for dst, src in loads:
                pool.dma_start(dst, src).then_inc(g["att_in"], 16)
            g["n_loads"] = len(loads)

            def root(m, k, out_, in_, power):
                pool.wait_ge(m["rq"], k)
                nc.gpsimd.tensor_tensor(out_, in_, power, ALU.pow).then_inc(m["rd"], 1)

            for name in run:
                if name == "l0x":
                    with pool.Fori(0, B) as n:
                        root(l0x, n * 2 + 1, rstd[:, :], rstd[:, :], mhalf[:, 0:T])
                        root(l0x, n * 2 + 2, norms[:, :], norms[:, :], mhalf[:, 0:2 * T])
                elif name == "l0f":
                    with pool.Fori(0, B) as n:
                        for k in range(2):
                            root(l0f, n * 2 + k + 1, rstd[:, :], rstd[:, :], mhalf[:, 0:T])
                elif name == "sim":
                    root(sm, 1, ss[:, 0:NH], ss[:, 0:NH], mhalf[:, 0:NH])
                    with pool.Fori(0, B) as n:
                        root(sm, n * 2 + 2, rstd[:, :], rstd[:, :], mhalf[:, 0:T])
                        root(sm, n * 2 + 3, ss[:, 0:2 * NH], ss[:, 0:2 * NH], mhalf[:, :])
                    pool.wait_ge(sm["dve"], SIM_STEPS_BEFORE)
                    nc.gpsimd.partition_all_reduce(ss[:, 2:4], ss[:, 0:2], P, RMAX).then_inc(sm["pool"], 1)
                else:
                    m = ph[name] if name in ph else moe[name]
                    with pool.Fori(0, B) as n:
                        root(m, n + 1, rstd[:, :], rstd[:, :], mhalf[:, 0:T])

        @block.vector
        def _(dve):
            V = nc.vector
            stt, ts, tt = V.scalar_tensor_tensor, V.tensor_scalar, V.tensor_tensor

            def root(m, k, ins):
                ins.then_inc(m["rq"], 1)
                dve.wait_ge(m["rd"], k)

            def stats(ch, m, k, srcs):
                for t, src in enumerate(srcs):
                    ins = V.bn_stats(bst[:, t, :], src)
                ch.link(ins)
                V.memset(idle[:, 0:1], 0.0)
                for t in range(T):
                    ins = V.bn_aggr(mv[:, t, :], bst[:, t, :])
                ch.link(ins)
                root(m, k, ts(rstd[:, :], mv[:, :, 1], LN_EPS, None, ALU.add))

            def layernorm(ch, m, n, k):
                stats(ch, m, k, [x[:, n * T + t, :] for t in range(T)])
                for t in range(T):
                    ts(xn[:, t, :], x[:, n * T + t, :], mv[:, t, 0:1], rstd[:, t:t + 1],
                       ALU.subtract, ALU.mult).then_inc(g["xn"], 1)
            LN = 2

            def add_to_x(n, t, branch, scalar):
                return stt(x[:, n * T + t, :], branch, scalar, x[:, n * T + t, :], ALU.mult, ALU.add)

            def similarity():
                ch = Chain(dve, l0x["dve"])
                with dve.Fori(0, B) as n:
                    ch.loop(n, LN + 1 + 3 * T)
                    layernorm(ch, l0x, n, n * 2 + 1)
                    dve.wait_ge(l0x["dots"], n + 1)
                    root(l0x, n * 2 + 2, V.tensor_copy(norms[:, :], bank[4][:, 0:2 * T]))
                    ch.link(ts(norms[:, :], norms[:, :], FAR, None, ALU.min))
                    for t in range(T):
                        ins = ts(diag[:, t, :], ident[:, :], norms[:, T + t:T + t + 1], None, ALU.mult)
                    ins.then_inc(l0x["dg"], 1)
                    dve.wait_ge(l0x["rows"], n + 1)
                    for t in range(T):
                        ch.link(ts(tmp, bank[3][:, 0:S], norms[:, t:t + 1], 1.0 / COS_EPS, ALU.mult, ALU.min))
                        ch.link(tt(tmp, bank[2][:, t * S:(t + 1) * S], tmp, ALU.mult))
                        ch.link(add_to_x(n, t, tmp, tgx[:, 0:1]))
                ch.leave(B)
                V.memset(idle[:, 0:1], 0.0).then_inc(g["phase"], 1)

            def feed_forward():
                ch = Chain(dve, l0f["dve"])
                with dve.Fori(0, B) as n:
                    ch.loop(n, 2 * LN + T * 6)
                    layernorm(ch, l0f, n, n * 2 + 1)
                    zs = [scr[:, (1 + t) * D:(2 + t) * D] for t in range(T)]
                    for t in range(T):
                        dve.wait_ge(l0f["y"], n * T + t + 1)
                        ch.link(tt(zs[t], bank[6 + t][:, 0:D], b02[:, :], ALU.add))
                        ch.link(tt(zs[t], zs[t], xn[:, t, :], ALU.add))
                    stats(ch, l0f, n * 2 + 2, zs)
                    for t in range(T):
                        ch.link(ts(zs[t], zs[t], mv[:, t, 0:1], rstd[:, t:t + 1], ALU.subtract, ALU.mult))
                        ch.link(tt(zs[t], zs[t], gam[:, :], ALU.mult))
                        ch.link(tt(zs[t], zs[t], bet[:, :], ALU.add))
                        ch.link(add_to_x(n, t, zs[t], tgf[:, 0:1]))
                ch.leave(B)
                V.memset(idle[:, 0:1], 0.0).then_inc(g["phase"], 1)

            def attention(s, gi):
                m = ph[s.name]
                ch = Chain(dve, m["dve"])
                vh = v[:, :, 0:NH * s.vs].rearrange("p t (h e) -> p t h e", h=NH)
                if s.ones:
                    for t in range(T):
                        ch.link(V.memset(vh[:, t, :, s.d:s.d + 1], 1.0))
                per = (LN + T * (4 if s.proj else 3) + (1 if s.bias else 0) + (2 * NH if s.clip else 0)
                       + (6 + NREG if s.split else 0))
                with dve.Fori(0, B) as n:
                    ch.loop(n, per)
                    layernorm(ch, m, n, n + 1)
                    if s.split:
                        ch.link(V.tensor_copy(qk2[:, :, 0:2], qp[:, bass.ds(n * T, T), :]))
                        V.tensor_copy(qk2[:, :, 2:4], kp[:, bass.ds(n * T, T), :]).then_inc(m["x2"], 1)
                        dve.wait_ge(m["x2"], n * 4 + 2)
                        V.tensor_copy(mrow[0:2, :, :], bank[7][0:2, :].rearrange("p (k s) -> p k s", k=2))\
                            .then_inc(m["x2"], 1)
                    for j in range(s.qjobs):
                        dve.wait_ge(m["q"], n * s.qjobs + j + 1)
                        dst = qT[:, 2 * j:2 * j + 2, :]
                        src = bank[j][:, :].rearrange("p (k s) -> p k s", k=2)
                        if s.mask:
                            for k in range(2):
                                ins = stt(dst[:, k, :], src[:, k, :], s.qscale, mask_u8[:, bass.ds(n * S, S)],
                                          ALU.mult, ALU.mult)
                        elif s.bias:
                            for k in range(2):
                                ins = ts(dst[:, k, :], src[:, k, :], bq3[:, 2 * j + k:2 * j + k + 1], s.qscale,
                                         ALU.add, ALU.mult)
                        else:
                            ins = ts(dst, src, s.qscale, None, ALU.mult)
                        ins.then_inc(m["qc"], 1)
                    if s.bias:
                        dve.wait_ge(m["v"], n + 1)
                        for t in range(T):
                            ins = tt(vh[:, t, :, 0:s.d],
                                     bank[4][:, t * D:(t + 1) * D].rearrange("p (h e) -> p h e", h=NH),
                                     bv3[:, :].rearrange("p (h e) -> p h e", h=NH), ALU.add)
                            if t == 0:
                                ch.link(ins)
                        ins.then_inc(m["vc"], 1)
                    if s.split:
                        dve.wait_ge(m["k"], n * (s.qjobs + 1) + s.qjobs + 1)
                        ch.link(ts(qxs[:, :], bank[5][:, 0:4 * NREG], s.qscale, None, ALU.mult))
                        qv = qxs[:, :].rearrange("p (g r) -> p g r", g=4)
                        for r in range(NREG):
                            ch.link(tt(qx[:, :, r * NH:(r + 1) * NH], hm[:, :, :],
                                       qv[:, :, r:r + 1].broadcast_to([P, 4, NH]), ALU.mult))
                        V.memset(idle[:, 0:1], 0.0).then_inc(m["vc"], 1)
                    U = s.units
                    for h in range(U + 1):
                        if h < U:
                            dve.wait_ge(m["s"], n * U + h + 1)
                            if h == NH:
                                V.tensor_reduce(nmax[0:NX, h, 0:1], bank[h % 2][0:NX, 0:S], AXX, ALU.max, negate=True)\
                                    .then_inc(m["mx"], 1)
                            else:
                                src = bank[h % 2][:, :]
                                if s.clip:
                                    if h >= 2:
                                        dve.wait_ge(m["e"], n * NH + h - 1)
                                    ch.link(ts(sc[h % 2][:, :], src, CLAMP, -CLAMP, ALU.min, ALU.max))
                                    src = sc[h % 2][:, :]
                                ins = V.tensor_reduce(nmax[:, h, :], src.rearrange("p (t k) -> p t k", t=T),
                                                      AXX, ALU.max, negate=True)
                                if s.clip:
                                    ch.link(ins)
                                    V.memset(idle[:, 0:1], 0.0).then_inc(m["mx"], 1)
                                else:
                                    ins.then_inc(m["mx"], 1)
                        if h >= 1 and not s.clip:
                            k = h - 1
                            dve.wait_ge(m["pT"], n * U + k + 1)
                            if k >= 2:
                                dve.wait_ge(m["pv"], n * U + k - 1)
                            w = 2 * NX if k == NH else 512
                            V.tensor_copy(probT[k % 2][:, 0:w], bank[2 + k % 2][:, 0:w]).then_inc(m["pTc"], 1)
                    dve.wait_ge(m["pv"], (n + 1) * U)
                    if s.split:
                        ov = bank[5][0:NX, 0:NH * s.vs].rearrange("p (h e) -> p h e", h=NH)
                        ch.link(V.reciprocal(rec[0:NX, :], ov[:, :, s.d]))
                        ch.link(tt(rec[0:NX, :], rec[0:NX, :], bm[0:NX, :], ALU.mult))
                        ch.link(tt(onx[0:NX, :].rearrange("p (h e) -> p h e", h=NH), ov[:, :, 0:s.d],
                                   rec[0:NX, :].rearrange("p (h o) -> p h o", o=1).broadcast_to([NX, NH, s.d]),
                                   ALU.mult))
                        V.memset(idle[:, 0:1], 0.0).then_inc(m["x2"], 1)
                    for t in range(T):
                        if s.ones:
                            ov = bank[4 + 2 * t][:, 0:NH * s.vs].rearrange("p (h e) -> p h e", h=NH)
                            ch.link(V.reciprocal(rec[:, :], ov[:, :, s.d]))
                            halves = [(ov[:, :, 0:s.d], 0, NH)]
                        else:
                            ch.link(V.reciprocal(rec[:, :], esum[:, :, t]))
                            halves = [(bank[4 + 2 * t + k][:, :].rearrange("p (h e) -> p h e", h=NH // 2),
                                       k * NH // 2, NH // 2) for k in range(2)]
                        if s.proj and t >= 1:
                            dve.wait_ge(m["onT"], n * T + t)
                        dst = (on if s.proj else tmp)[:, 0:NH * s.d].rearrange("p (h e) -> p h e", h=NH)
                        for src, h0, hn in halves:
                            ins = tt(dst[:, h0:h0 + hn, :], src,
                                     rec[:, h0:h0 + hn].rearrange("p (h o) -> p h o", o=1)
                                     .broadcast_to([P, hn, s.d]), ALU.mult)
                        ch.link(ins)
                        if s.split and t == 0:
                            dve.wait_ge(m["y"], n * (T + 1) + 1)
                            ch.link(stt(on[:, 0:D], on[:, 0:D], wcol[:, 0:1], bank[7][:, 0:D], ALU.mult, ALU.add))
                        if s.proj:
                            V.memset(idle[:, 0:1], 0.0).then_inc(m["on"], 1)
                        else:
                            ch.link(add_to_x(n, t, tmp, tgx[:, gi:gi + 1]))
                    if s.proj:
                        e = 1 if s.split else 0
                        for t in range(T):
                            dve.wait_ge(m["y"], n * (T + e) + e + t + 1)
                            ch.link(tt(tmp, bank[4 + 2 * t][:, 0:D], bo[s.name][:, :], ALU.add))
                            ins = add_to_x(n, t, tmp, (tgf if s.split else tgx)[:, gi:gi + 1])
                            ch.link(ins)
                ch.leave(B)
                V.memset(idle[:, 0:1], 0.0).then_inc(g["phase"], 1)

            def mixture(name, gi, ne):
                m = moe[name]
                ch = Chain(dve, m["dve"])
                with dve.Fori(0, B) as n:
                    ch.loop(n, LN)
                    dve.wait_ge(g["xnT"], entries(name, n))
                    layernorm(ch, m, n, n + 1)
                ch.leave(B)
                dve.wait_ge(m["lg"], 1)
                full = [P, NT, NE]
                per_tok = [P, NT, 1]
                gmv = gm[:, :].rearrange("p (t o) -> p t o", o=1)
                ch.link(V.tensor_copy(lg[:, :, :], bank[0][:, 0:NT * NE].rearrange("p (t e) -> p t e", t=NT)))
                ch.link(V.tensor_reduce(gm[:, :], lg[:, :, :], AXX, ALU.max))
                ch.link(tt(sel[:, :, :], lg[:, :, :], gmv.broadcast_to(full), ALU.subtract))
                V.memset(idle[:, 0:1], 0.0).then_inc(m["gd"], 1)
                dve.wait_ge(m["ga"], 1)
                if name == "l2f":
                    ch.link(V.tensor_reduce(gm[:, :], sel[:, :, :], AXX, ALU.add))
                    ch.link(V.reciprocal(gm[:, :], gm[:, :]))
                    ch.link(tt(sel[:, :, :], sel[:, :, :], gmv.broadcast_to(full), ALU.mult))
                    ch.link(tt(lg[:, :, :], sel[:, :, :],
                               gb2[:, :].rearrange("p (o e) -> p o e", o=1).broadcast_to(full), ALU.add))
                rank = scr[:, 0:NT * NE * NE].rearrange("p (t e j) -> p t e j", e=NE, j=NE)
                for e in range(NE):
                    ch.link(tt(rank[:, :, e, :], lg[:, :, :], lg[:, :, e:e + 1].broadcast_to(full), ALU.is_equal))
                    ch.link(tt(rank[:, :, e, :], rank[:, :, e, :],
                               tri[:, e:e + 1, :].broadcast_to(full), ALU.mult))
                    ch.link(tt(larger[:, :, :], lg[:, :, :], lg[:, :, e:e + 1].broadcast_to(full), ALU.is_gt))
                    ch.link(tt(rank[:, :, e, :], rank[:, :, e, :], larger[:, :, :], ALU.add))
                ch.link(V.tensor_reduce(lg[:, :, :], rank, AXX, ALU.add))
                ch.link(ts(lg[:, :, :], lg[:, :, :], 1.5, None, ALU.is_lt))
                ch.link(tt(sel[:, :, :], sel[:, :, :], lg[:, :, :], ALU.mult))
                if name == "l1f":
                    ch.link(V.tensor_reduce(gm[:, :], sel[:, :, :], AXX, ALU.add))
                    ch.link(V.reciprocal(gm[:, :], gm[:, :]))
                    ch.link(tt(sel[:, :, :], sel[:, :, :], gmv.broadcast_to(full), ALU.mult))
                else:
                    ch.link(V.memset(gate[:, :, NE:NE + 2], 1.0))
                    ch.link(ts(gate[:, :, NE:NE + 2], gate[:, :, NE:NE + 2], tgf[:, gi:gi + 1], None, ALU.mult))
                ch.link(ts(gate[:, :, 0:NE], sel[:, :, :], tgf[:, gi:gi + 1], None, ALU.mult))
                ft = -(-(F1 if name == "l1f" else F2) // P)
                f = F1 if name == "l1f" else F2
                NBLK = NT * P // 512
                V.memset(idle[:, 0:1], 0.0).then_inc(m["yc"], 1)
                with dve.Fori(0, ne // 2) as i:
                    for u in range(2):
                        for blk in range(NBLK + 1):
                            blocks = (i * 2 + u) * NBLK + blk
                            if blk < NBLK:
                                for h in range(ft):
                                    if h == 1 and blk >= 1:
                                        expert_out(m, i, u, blk - 1, 4 * (blocks - 1))
                                    r = min(P, f - h * P)
                                    dve.wait_ge(m["sil"], blocks * ft + h + 1)
                                    tt(hid[blk % 2][0:r, h, :], sil[h % 2][0:r, :], bank[2 + h % 2][0:r, :], ALU.mult)\
                                        .then_inc(m["hid"], 1)
                            else:
                                expert_out(m, i, u, blk - 1, 4 * (blocks - 1))
                dve.wait_ge(m["hid"], ne * NBLK * ft)
                dve.wait_ge(m["yc"], ne * NBLK * 4 + 1)
                V.memset(idle[:, 0:1], 0.0).then_inc(g["phase"], 1)

            def expert_out(m, i, u, blk, before):
                for k in range(4):
                    t = blk * 4 + k
                    dve.wait_ge(m["y"], before + k + 1)
                    stt(x[:, t, :], bank[4 + k % 4][:, 0:D], gate[:, t, bass.ds(i * 2 + u, 1)], x[:, t, :],
                        ALU.mult, ALU.add).then_inc(m["yc"], 1)


            def guide():
                ch = Chain(dve, sm["dve"])
                q16 = lambda t: t.rearrange("p (h e) -> p h e", h=NH)
                ch.link(tt(tmp, qg[:, :], qg[:, :], ALU.mult))
                root(sm, 1, V.tensor_reduce(ss[:, 0:NH], q16(tmp), AXX, ALU.add))
                ch.link(tt(q16(qg[:, :]), q16(qg[:, :]),
                           ss[:, 0:NH].rearrange("p (h o) -> p h o", o=1).broadcast_to([P, NH, 16]), ALU.mult))
                with dve.Fori(0, B) as n:
                    ch.loop(n, LN + T * 5 + 2)
                    layernorm(ch, sm, n, n * 2 + 2)
                    for t in range(T):
                        dve.wait_ge(sm["q"], n * T + t + 1)
                        ch.link(V.tensor_copy(z, bank[t][:, 0:D]))
                        ch.link(tt(tmp, z, z, ALU.mult))
                        ins = V.tensor_reduce(ss[:, t * NH:(t + 1) * NH], q16(tmp), AXX, ALU.add)
                        ch.link(ins)
                        ch.link(tt(tmp, z, qg[:, :], ALU.mult))
                        ch.link(V.tensor_reduce(ss[:, (2 + t) * NH:(3 + t) * NH], q16(tmp), AXX, ALU.add))
                    root(sm, n * 2 + 3, V.memset(idle[:, 0:1], 0.0))
                    ch.link(tt(ss[:, 2 * NH:4 * NH], ss[:, 0:2 * NH], ss[:, 2 * NH:4 * NH], ALU.mult))
                    ch.link(V.tensor_reduce(sim[:, bass.ds(n * T, T)],
                                            ss[:, 2 * NH:4 * NH].rearrange("p (t h) -> p t h", h=NH), AXX, ALU.add))
                ch.leave(B)
                ch.link(ts(sim[:, :], sim[:, :], 1.0 / NH, None, ALU.mult))
                nreg = scr[:, 0:NT]
                t0 = scr[:, NT:2 * NT]
                t1 = scr[:, 2 * NT:3 * NT]
                ch.link(ts(nreg, regm[:, :], -1.0, 1.0, ALU.mult, ALU.add))
                ch.link(tt(t0, sim[:, :], nreg, ALU.mult))
                ch.link(stt(t1, regm[:, :], -FAR, t0, ALU.mult, ALU.add))
                ch.link(V.tensor_reduce(ss[:, 0:1], t1, AXX, ALU.max))
                ch.link(stt(t1, regm[:, :], FAR, t0, ALU.mult, ALU.add))
                ch.link(ts(t1, t1, -1.0, None, ALU.mult))
                ch.link(V.tensor_reduce(ss[:, 1:2], t1, AXX, ALU.max))
                assert ch.base + ch.k == SIM_STEPS_BEFORE, ch.base + ch.k
                dve.wait_ge(sm["pool"], 1)
                ch.link(ts(t0, sim[:, :], ss[:, 3:4], None, ALU.add))
                ch.link(tt(ss[:, 4:5], ss[:, 2:3], ss[:, 3:4], ALU.add))
                ch.link(V.reciprocal(ss[:, 4:5], ss[:, 4:5]))
                ch.link(ts(t0, t0, ss[:, 4:5], None, ALU.mult))
                ch.link(ts(t0, t0, 0.9, None, ALU.is_gt))
                ch.link(tt(qp[:, :, 0], t0, regm[:, :], ALU.max))
                ch.link(ts(qp[:, :, 1], qp[:, :, 0], -1.0, 1.0, ALU.mult, ALU.add))
                ch.link(ts(t1, t0, -1.0, 1.0, ALU.mult, ALU.add))
                ch.link(stt(kp[:, :, 0], t1, -FAR, nreg, ALU.mult, ALU.mult))
                ch.link(stt(kp[:, :, 1], t0, -FAR, nreg, ALU.mult, ALU.mult))
                V.memset(idle[:, 0:1], 0.0).then_inc(g["phase"], 1)

            dve.wait_ge(g["x_in"], 16)
            dve.wait_ge(g["tanh"], 2)
            dve.wait_ge(g["consts"], g["n_consts"])
            similarity()
            dve.wait_ge(g["att_in"], 16 * g["n_loads"])
            for name in run[1:]:
                if name == "l0f":
                    feed_forward()
                elif name == "l1x":
                    attention(L1X, 1)
                elif name == "l1f":
                    mixture("l1f", 1, NE)
                elif name == "l2x":
                    attention(L2X, 2)
                elif name == "l2f":
                    mixture("l2f", 2, NE + 2)
                elif name == "l3x":
                    attention(L3X, 3)
                elif name == "sim":
                    guide()
                else:
                    attention(L3F, 3)

        @block.scalar
        def _(act):
            A = nc.scalar.activation

            def copy(dst, src):
                return A(dst, src, ACT.Copy)

            def turned(name, n):
                act.wait_ge(g["xnT"], entries(name, n) + 1)
                copy(xt[:, :, :], bank[6][:, :].rearrange("p (c s) -> p c s", c=DC)).then_inc(g["xt"], 1)

            def similarity():
                with act.Fori(0, B) as n:
                    turned("l0x", n)
                    act.wait_ge(l0x["vt"], n + 1)
                    A(qT[:, 0, :], bank[0][:, 0:S], ACT.Identity, bias=b0v[:, 0:1]).then_inc(l0x["act"], 1)
                    A(qT[:, 1, :], bank[1][:, 0:S], ACT.Identity, bias=b0t[:, 0:1]).then_inc(l0x["act"], 1)
                    act.wait_ge(l0x["act"], n * 2 + 2)
                    A(kT[:, 0, :], qT[:, 0, :], ACT.Square)
                    A(kT[:, 1, :], qT[:, 1, :], ACT.Square).then_inc(l0x["vtc"], 1)

            def feed_forward():
                with act.Fori(0, B) as n:
                    turned("l0f", n)
                    for j in range(F0 // P):
                        act.wait_ge(l0f["h"], n * (F0 // P) + j + 1)
                        A(hid0[:, j, :], bank[j % 4][:, 0:S], ACT.Relu, bias=b01[:, j:j + 1]).then_inc(l0f["hc"], 1)

            def attention(s):
                m = ph[s.name]
                U = s.units
                vh = v[:, :, 0:NH * s.vs].rearrange("p t (h e) -> p t h e", h=NH)
                if s.ones:
                    act.wait_ge(m["dve"], T)
                with act.Fori(0, B) as n:
                    turned(s.name, n)
                    kj = s.qjobs + (1 if s.split else 0)
                    for j in range(s.qjobs):
                        act.wait_ge(m["k"], n * kj + j + 1)
                        dst = kT[:, 2 * j:2 * j + 2, :]
                        src = bank[s.qjobs + j][:, :].rearrange("p (k s) -> p k s", k=2)
                        if s.bias:
                            for k in range(2):
                                ins = A(dst[:, k, :], src[:, k, :], ACT.Identity, bias=bk3[:, 2 * j + k:2 * j + k + 1])
                        else:
                            ins = copy(dst, src)
                        ins.then_inc(m["kc"], 1)
                    if not s.bias:
                        for j in range(s.vjobs):
                            act.wait_ge(m["v"], n * s.vjobs + j + 1)
                            if s.ones:
                                for t in range(T):
                                    ins = copy(vh[:, t, :, 0:s.d],
                                               bank[4][:, t * D:(t + 1) * D].rearrange("p (h e) -> p h e", h=NH))
                            else:
                                ins = copy(v[:, j // 2, (j % 2) * 512:(j % 2 + 1) * 512], bank[j][:, :])
                            ins.then_inc(m["vc"], 1)
                    for h in range(U + (1 if s.clip else 0)):
                        if h < U:
                            act.wait_ge(m["mx"], n * U + h + 1)
                            if h >= 2:
                                act.wait_ge(m["pT"], n * U + h - 1)
                        if h < NH:
                            src = (sc[h % 2] if s.clip else bank[h % 2])
                            for t in range(T):
                                kw = {} if s.ones else {"accum_out": esum[:, h, t:t + 1]}
                                ins = A(prob[h % 2][:, t * S:(t + 1) * S], src[:, t * S:(t + 1) * S], ACT.Exp,
                                        bias=nmax[:, h, t:t + 1], **kw)
                            ins.then_inc(m["e"], 1)
                        elif h < U:
                            A(prob[h % 2][0:NX, 0:S], bank[h % 2][0:NX, 0:S], ACT.Exp, bias=nmax[0:NX, h, 0:1])\
                                .then_inc(m["e"], 1)
                        if s.clip and h >= 1:
                            k = h - 1
                            act.wait_ge(m["pT"], n * U + k + 1)
                            if k >= 2:
                                act.wait_ge(m["pv"], n * U + k - 1)
                            copy(probT[k % 2][:, :], bank[2 + k % 2][:, :]).then_inc(m["pTc"], 1)
                    if s.proj:
                        nb = -(-s.width // 512)
                        for t in range(T):
                            act.wait_ge(m["onT"], n * T + t + 1)
                            for k in range(nb):
                                w = min(512, s.width - 512 * k)
                                ins = copy(oT[:, 4 * k:4 * k + w // P, :],
                                           bank[2 * t + k][:, 0:w].rearrange("p (c s) -> p c s", s=P))
                            ins.then_inc(m["oT"], 1)
                            if t < T - 1:
                                act.wait_ge(m["y"], n * (T + (1 if s.split else 0)) + (1 if s.split else 0) + t + 1)

            def mixture(name, ne):
                m = moe[name]
                f = F1 if name == "l1f" else F2
                ft = -(-f // P)
                with act.Fori(0, B) as n:
                    act.wait_ge(g["xnT"], entries(name, n) + 1)
                    copy(xt_all[:, :, bass.ds(n * S, S)], bank[6][:, :].rearrange("p (c s) -> p c s", c=DC))\
                        .then_inc(g["xt"], 1)
                act.wait_ge(m["gd"], 1)
                A(sel[:, :, :], sel[:, :, :], ACT.Exp).then_inc(m["ga"], 1)
                NBLK = NT * P // 512
                with act.Fori(0, ne // 2) as i:
                    for u in range(2):
                        for blk in range(NBLK):
                            blocks = (i * 2 + u) * NBLK + blk
                            for h in range(ft):
                                r = min(P, f - h * P)
                                act.wait_ge(m["a"], blocks * ft + h + 1)
                                if h >= 2:
                                    act.wait_ge(m["hid"], blocks * ft + h - 1)
                                A(sil[h % 2][0:r, :], bank[h % 2][0:r, :], ACT.Silu).then_inc(m["sil"], 1)

            def guide():
                with act.Fori(0, B) as n:
                    turned("sim", n)

            act.wait_ge(g["w0_in"], 16 * 6)
            A(tgx[:, :], gates_x[:, :], ACT.Tanh).then_inc(g["tanh"], 1)
            A(tgf[:, :], gates_f[:, :], ACT.Tanh).then_inc(g["tanh"], 1)
            similarity()
            act.wait_ge(g["att_in"], 16 * g["n_loads"])
            for name in run[1:]:
                if name == "l0f":
                    feed_forward()
                elif name in attn:
                    attention(attn[name])
                elif name == "l1f":
                    mixture("l1f", NE)
                elif name == "l2f":
                    mixture("l2f", NE + 2)
                else:
                    guide()

        @block.tensor
        def _(pe):
            mm, tr = nc.tensor.matmul, nc.tensor.transpose

            def turn(name, n):
                pe.wait_ge(g["xn"], entries(name, n) * T + T)
                for t in range(T):
                    for c in range(DC):
                        ins = tr(bank[6][:, c * S + t * P:c * S + (t + 1) * P], xn[:, t, c * P:(c + 1) * P], ident[:, :])
                ins.then_inc(g["xnT"], 1)

            def similarity():
                with pe.Fori(0, B) as n:
                    turn("l0x", n)
                    pe.wait_ge(g["xt"], entries("l0x", n) + 1)
                    pe.wait_ge(l0x["ct"], n * 16 + 16)
                    for c in range(DC):
                        mm(bank[0][:, 0:S], w0v[:, c, :], xt[:, c, :], start=c == 0, stop=c == DC - 1)
                    for c in range(2):
                        ins = mm(bank[1][:, 0:S], w0t[:, c, :], ct[:, c, :], start=c == 0, stop=c == 1)
                    ins.then_inc(l0x["vt"], 1)
                    pe.wait_ge(l0x["vtc"], n + 1)
                    for t in range(T):
                        mm(bank[2][:, t * S:(t + 1) * S], qT[:, 0, t * P:(t + 1) * P], qT[:, 1, :], start=True, stop=True)
                    for k in range(2):
                        for t in range(T):
                            c = k * T + t
                            ins = mm(bank[4][:, c:c + 1], kT[:, k, t * P:(t + 1) * P], ones[:, 0:1], start=True, stop=True)
                    ins.then_inc(l0x["dots"], 1)
                    pe.wait_ge(l0x["dg"], n + 1)
                    for t in range(T):
                        ins = mm(bank[3][:, t * P:(t + 1) * P], ones[:, :], diag[:, t, :], start=True, stop=True)
                    ins.then_inc(l0x["rows"], 1)

            def feed_forward():
                nj = F0 // P
                with pe.Fori(0, B) as n:
                    turn("l0f", n)
                    pe.wait_ge(g["xt"], entries("l0f", n) + 1)
                    for j in range(nj):
                        if j >= 4:
                            pe.wait_ge(l0f["hc"], n * nj + j - 3)
                        for c in range(DC):
                            ins = mm(bank[j % 4][:, 0:S], w01[:, c, j * P:(j + 1) * P], xt[:, c, :],
                                     start=c == 0, stop=c == DC - 1)
                        ins.then_inc(l0f["h"], 1)
                    pe.wait_ge(l0f["hc"], n * nj + nj)
                    for t in range(T):
                        for j in range(nj):
                            ins = mm(bank[6 + t][:, 0:D], hid0[:, j, t * P:(t + 1) * P], w02[:, j, :],
                                     start=j == 0, stop=j == nj - 1)
                        ins.then_inc(l0f["y"], 1)

            def attention(s):
                m = ph[s.name]
                U, d, R = s.units, s.d, s.rows
                W = {k: t[s.name] for k, t in (("q", wq), ("k", wk), ("v", wv))}
                src = xt if s.split else ct
                with pe.Fori(0, B) as n:
                    turn(s.name, n)
                    if s.split:
                        pe.wait_ge(m["x2"], n * 4 + 1)
                        for k in range(2):
                            for t in range(T):
                                ins = mm(bank[7][0:2, k * S + t * P:k * S + (t + 1) * P],
                                         qk2[:, t, 2 * k:2 * k + 2], ident[:, :], start=True, stop=True)
                        ins.then_inc(m["x2"], 1)
                        pe.wait_ge(m["x2"], n * 4 + 3)
                    pe.wait_ge(g["xt"], entries(s.name, n) + 1)
                    if not s.split:
                        pe.wait_ge(m["ct"], n * 16 + 16)
                    for j in range(s.qjobs):
                        for k in range(2):
                            gr = 2 * j + k
                            dst = bank[j][:, k * S:(k + 1) * S]
                            for c in range(DC):
                                ins = mm(dst, W["q"][:, c, gr * P:(gr + 1) * P], xt[:, c, :], start=c == 0,
                                         stop=c == DC - 1 and not s.split)
                            if s.split:
                                ins = mm(dst, selw[:, :], mrow[:, 0, :], start=False, stop=True)
                        ins.then_inc(m["q"], 1)
                    for j in range(s.qjobs):
                        for k in range(2):
                            gr = 2 * j + k
                            dst = bank[s.qjobs + j][:, k * S:(k + 1) * S]
                            for c in range(s.kt):
                                ins = mm(dst, W["k"][:, c, gr * P:(gr + 1) * P], src[:, c, :], start=c == 0,
                                         stop=c == s.kt - 1 and not s.split)
                            if s.split:
                                ins = mm(dst, selw[:, :], mrow[:, 1, :], start=False, stop=True)
                        ins.then_inc(m["k"], 1)
                    if s.split:
                        for gr in range(4):
                            dst = bank[5][:, gr * NREG:(gr + 1) * NREG]
                            for c in range(DC):
                                mm(dst, W["q"][:, c, gr * P:(gr + 1) * P], xt[:, c, 0:NREG], start=c == 0, stop=False)
                            ins = mm(dst, selw[:, :], mregq[:, :], start=False, stop=True)
                        ins.then_inc(m["k"], 1)
                    for j in range(s.vjobs):
                        if s.ones:
                            parts = [(bank[4][:, t * D:(t + 1) * D], t, 0, D) for t in range(T)]
                        else:
                            pe.wait_ge(m["qc"], n * s.qjobs + j + 1)
                            parts = [(bank[j][:, :], j // 2, (j % 2) * 512, 512)]
                        for dst, t, c0, w in parts:
                            for c in range(s.kt):
                                ins = mm(dst, src[:, c, t * P:(t + 1) * P], W["v"][:, c, c0:c0 + w],
                                         start=c == 0, stop=c == s.kt - 1)
                        ins.then_inc(m["v"], 1)
                    pe.wait_ge(m["qc"], n * s.qjobs + s.qjobs)
                    pe.wait_ge(m["kc"], n * s.qjobs + s.qjobs)
                    nv = s.vjobs + (1 if s.split else 0)
                    if not s.ones:
                        pe.wait_ge(m["vc"], n * nv + nv)
                    for h in range(U + 2):
                        if h < U:
                            if h >= 2:
                                pe.wait_ge(m["e"], n * U + h - 1)
                            if h < NH:
                                r0 = (h % s.per) * R
                                kr = slice(r0, r0 + (R if s.split else d))
                                for t in range(T):
                                    ins = mm(bank[h % 2][:, t * S:(t + 1) * S],
                                             qT[kr, h // s.per, t * P:(t + 1) * P],
                                             kT[kr, h // s.per, :], start=True, stop=True)
                            else:
                                if h == NH:
                                    pe.wait_ge(m["vc"], n * nv + nv)
                                for gr in range(4):
                                    ins = mm(bank[h % 2][0:NX, 0:S], qx[:, gr, :], kT[:, gr, :],
                                             start=gr == 0, stop=gr == 3)
                            ins.then_inc(m["s"], 1)
                        if 1 <= h <= U:
                            k = h - 1
                            pe.wait_ge(m["e"], n * U + k + 1)
                            if k >= 2:
                                pe.wait_ge(m["pTc"], n * U + k - 1)
                            if k < NH:
                                for kt in range(T):
                                    for t in range(T):
                                        c0 = (kt * T + t) * P
                                        ins = tr(bank[2 + k % 2][:, c0:c0 + P],
                                                 prob[k % 2][:, t * S + kt * P:t * S + (kt + 1) * P], ident[:, :])
                            else:
                                for kt in range(T):
                                    ins = tr(bank[2 + k % 2][:, kt * NX:(kt + 1) * NX],
                                             prob[k % 2][0:NX, kt * P:(kt + 1) * P], ident[0:NX, 0:NX])
                            ins.then_inc(m["pT"], 1)
                        if h >= 2:
                            k = h - 2
                            if k == 0 and s.ones:
                                pe.wait_ge(m["vc"], n * nv + nv)
                            pe.wait_ge(m["pTc"], n * U + k + 1)
                            if k < NH:
                                for t in range(T):
                                    for kt in range(T):
                                        c0 = (kt * T + t) * P
                                        if s.ones:
                                            dst = bank[4 + 2 * t][:, k * s.vs:(k + 1) * s.vs]
                                        else:
                                            dst = bank[4 + 2 * t + k // 8][:, (k % 8) * 64:(k % 8 + 1) * 64]
                                        ins = mm(dst, probT[k % 2][:, c0:c0 + P], v[:, kt, k * s.vs:(k + 1) * s.vs],
                                                 start=kt == 0, stop=kt == T - 1)
                            else:
                                for kt in range(T):
                                    ins = mm(bank[5][0:NX, 0:NH * s.vs], probT[k % 2][:, kt * NX:(kt + 1) * NX],
                                             v[:, kt, 0:NH * s.vs], start=kt == 0, stop=kt == T - 1)
                            ins.then_inc(m["pv"], 1)
                    if s.split:
                        pe.wait_ge(m["x2"], n * 4 + 4)
                        mm(bank[7][:, 0:D], rsel[0:NX, :], onx[0:NX, :], start=True, stop=True).then_inc(m["y"], 1)
                    if s.proj:
                        nc_ = s.width // P
                        for t in range(T):
                            pe.wait_ge(m["on"], n * T + t + 1)
                            for c in range(nc_):
                                ins = tr(bank[2 * t + c // 4][:, (c % 4) * P:(c % 4 + 1) * P],
                                         on[:, c * P:(c + 1) * P], ident[:, :])
                            ins.then_inc(m["onT"], 1)
                            pe.wait_ge(m["oT"], n * T + t + 1)
                            for c in range(nc_):
                                ins = mm(bank[4 + 2 * t][:, 0:D], oT[:, c, :], wo[s.name][:, c, :],
                                         start=c == 0, stop=c == nc_ - 1)
                            ins.then_inc(m["y"], 1)

            def mixture(name, wg, ne):
                m = moe[name]
                f = F1 if name == "l1f" else F2
                ft = -(-f // P)
                with pe.Fori(0, B) as n:
                    pe.wait_ge(g["xt"], entries(name, n))
                    turn(name, n)
                pe.wait_ge(g["xt"], entries(name, B))
                for t in range(NT):
                    for c in range(DC):
                        ins = mm(bank[0][:, t * NE:(t + 1) * NE], xt_all[:, c, t * P:(t + 1) * P], wg[:, c, :],
                                 start=c == 0, stop=c == DC - 1)
                ins.then_inc(m["lg"], 1)
                pe.wait_ge(m["gd"], 1)
                NBLK = NT * P // 512

                def down(u, w3, blk, before):
                    pe.wait_ge(m["yc"], before + 1)
                    for k in range(4):
                        for h in range(ft):
                            r = min(P, f - h * P)
                            ins = mm(bank[4 + k][:, 0:D], hid[blk % 2][0:r, h, k * P:(k + 1) * P], w3[0:r, h, :],
                                     start=h == 0, stop=h == ft - 1)
                        ins.then_inc(m["y"], 1)

                with pe.Fori(0, ne // 2) as i:
                    for u in range(2):
                        w1, w2, w3 = expert(u, f)
                        pe.wait_ge(m[f"w{u}"], i * 16 + 16)
                        for blk in range(NBLK + 1):
                            blocks = (i * 2 + u) * NBLK + blk
                            if blk == NBLK:
                                pe.wait_ge(m["hid"], blocks * ft)
                                down(u, w3, blk - 1, 4 * (blocks - 1))
                                break
                            for h in range(ft):
                                if h == 1 and blk >= 1:
                                    pe.wait_ge(m["hid"], blocks * ft)
                                    down(u, w3, blk - 1, 4 * (blocks - 1))
                                r = min(P, f - h * P)
                                if h >= 2:
                                    pe.wait_ge(m["hid"], blocks * ft + h - 1)
                                elif blk >= 1:
                                    pe.wait_ge(m["hid"], blocks * ft + h - 1)
                                for c in range(DC):
                                    mm(bank[h % 2][0:r, :], w1[:, c, h * P:h * P + r],
                                       xt_all[:, c, blk * 512:(blk + 1) * 512], start=c == 0, stop=c == DC - 1)
                                for c in range(DC):
                                    ins = mm(bank[2 + h % 2][0:r, :], w2[:, c, h * P:h * P + r],
                                             xt_all[:, c, blk * 512:(blk + 1) * 512], start=c == 0, stop=c == DC - 1)
                                ins.then_inc(m["a"], 1)

            def guide():
                with pe.Fori(0, B) as n:
                    turn("sim", n)
                    pe.wait_ge(g["xt"], entries("sim", n) + 1)
                    for t in range(T):
                        for c in range(DC):
                            ins = mm(bank[t][:, 0:D], xt[:, c, t * P:(t + 1) * P], wqs[:, c, :],
                                     start=c == 0, stop=c == DC - 1)
                        ins.then_inc(sm["q"], 1)

            pe.wait_ge(g["consts"], g["n_consts"])
            pe.wait_ge(g["w0_in"], 16 * 6)
            similarity()
            pe.wait_ge(g["w0f_in"], 32)
            pe.wait_ge(g["att_in"], 16 * g["n_loads"])
            for name in run[1:]:
                if name == "l0f":
                    feed_forward()
                elif name in attn:
                    attention(attn[name])
                elif name == "l1f":
                    mixture("l1f", wg1, NE)
                elif name == "l2f":
                    mixture("l2f", wg2, NE + 2)
                else:
                    guide()


SIM_STEPS_BEFORE = 2 + B * (2 + T * 5 + 2) + 8


def kernel(**inputs):
    import numpy as np
    import concourse.bacc as bacc
    from concourse.bass_utils import run_bass_kernel_spmd

    def rows(w, k):
        return w.reshape(k, w.shape[0] // k, w.shape[1]).transpose(1, 0, 2)

    def heads32(w):
        r = np.zeros((w.shape[0], NH, 32), w.dtype)
        r[:, :, 0:16] = w.reshape(w.shape[0], NH, 16)
        return r.reshape(w.shape[0], NH * 32)

    def columns(b):
        return heads32(b.reshape(1, D)).reshape(4, P).T

    def per_expert(w1, w2, w3):
        f = w1.shape[0]
        ft = -(-f // P)
        down = np.zeros((ft * P, D), w1.dtype)
        down[0:f] = w3.T
        return np.concatenate([rows(w1.T, DC).reshape(P, -1), rows(w2.T, DC).reshape(P, -1),
                               rows(down, ft).reshape(P, -1)], axis=1)

    n = {k: np.asarray(v) for k, v in inputs.items()}
    wkv = n["L1_xattn_Wkv"].T
    qkv = n["L3_ffn_W_qkv"]
    we1 = np.stack([per_expert(n["L1_ffn_W1"][e], n["L1_ffn_W2"][e], n["L1_ffn_W3"][e]) for e in range(NE)])
    shared = [(n["L2_ffn_sw1"][F2 * e:F2 * e + F2], n["L2_ffn_sw3"][F2 * e:F2 * e + F2],
               n["L2_ffn_sw2"][:, F2 * e:F2 * e + F2]) for e in range(2)]
    we2 = np.stack([per_expert(n["L2_ffn_w1"][e], n["L2_ffn_w3"][e], n["L2_ffn_w2"][e]) for e in range(NE)]
                   + [per_expert(*t) for t in shared])
    arrays = {
        "x": n["x"],
        "ctxT": n["ctx_768"].reshape(B, S, 2, CK).transpose(0, 3, 2, 1),
        "mask": n["mask_BxS_bk0"].reshape(B * S),
        "g_xattn": n["g_xattn"], "g_ffn": n["g_ffn"],
        "w0v": rows(n["L0_xattn_Wv"].T, DC), "w0t": rows(n["L0_xattn_Wt"].T, 2),
        "b0v": n["L0_xattn_bv"].reshape(P, 1), "b0t": n["L0_xattn_bt"].reshape(P, 1),
        "w01": rows(n["L0_ffn_w1"][0], DC), "w02": rows(n["L0_ffn_w2"][0], F0 // P),
        "b01": n["L0_ffn_b1"][0].reshape(F0 // P, P).T, "b02": n["L0_ffn_b2"][0],
        "gamma": n["L0_ffn_gamma"], "beta": n["L0_ffn_beta"],
        "wq_l1x": rows(heads32(n["L1_xattn_Wq"].T), DC),
        "wk_l1x": rows(heads32(wkv[:, 0:D]), 2), "wv_l1x": rows(wkv[:, D:2 * D], 2),
        "wg1": rows(n["L1_ffn_Wg"].T, DC), "we1": we1,
        "wq_l2x": rows(n["L2_xattn_w_q"], DC), "wk_l2x": rows(n["L2_xattn_w_k"], 2),
        "wv_l2x": rows(n["L2_xattn_w_v"], 2), "wo_l2x": rows(n["L2_xattn_w_o"], 8), "bo_l2x": n["L2_xattn_b_o"],
        "wg2": rows(n["L2_ffn_gate_w"].T, DC), "gb2": n["L2_ffn_gate_bias"], "we2": we2,
        "wq_l3x": rows(heads32(n["L3_xattn_Wq"]), DC), "bq3": columns(n["L3_xattn_bq"]),
        "wk_l3x": rows(heads32(n["L3_xattn_Wk"]), 2), "bk3": columns(n["L3_xattn_bk"]),
        "wv_l3x": rows(n["L3_xattn_Wv"], 2), "bv3": n["L3_xattn_bv"],
        "wo_l3x": rows(n["L3_xattn_Wo"], DC), "bo_l3x": n["L3_xattn_bo"],
        "qg": n["L3_ffn_g_info"][0, 0],
        "wqs": rows(qkv[:, 0:D], DC), "wq_l3f": rows(heads32(qkv[:, 0:D]), DC),
        "wk_l3f": rows(heads32(qkv[:, D:2 * D]), DC), "wv_l3f": rows(qkv[:, 2 * D:3 * D], DC),
        "wo_l3f": rows(n["L3_ffn_W_proj"], DC), "bo_l3f": n["L3_ffn_b_proj"],
    }
    arrays = {k: np.ascontiguousarray(v) for k, v in arrays.items()}
    nc = bacc.Bacc("TRN2", target_bir_lowering=False, num_devices=1)
    aps = {k: nc.dram_tensor(f"in_{k}", v.shape, mybir.dt.from_np(v.dtype), kind="ExternalInput").ap()
           for k, v in arrays.items()}
    out = nc.dram_tensor("out", (B, S, D), F32, kind="ExternalOutput").ap()
    build(nc, aps, out)
    r = run_bass_kernel_spmd(nc, [{f"in_{k}": v for k, v in arrays.items()}], core_ids=[0])
    return r.results[0]["out"]
```

```python
from contextlib import ExitStack

import concourse.bass as bass
from concourse import mybir

F32 = mybir.dt.float32
U8 = mybir.dt.uint8
F32R = mybir.dt.float32r
ALU = mybir.AluOpType
ACT = mybir.ActivationFunctionType
AXX = mybir.AxisListType.X
RMAX = bass.bass_isa.ReduceOp.max

P = 128
B, S, D = 8, 256, 256
T = S // P
NT = B * T
DC = D // P
CTX, CK = 192, 96
NH = 16
HV = 128
F0 = 1024
F1 = 682
NBLK = NT * P // 512
HS = {"l1f": 8, "l2f": 4}
F1T = -(-F1 // P)
F2 = 256
NE = 8
NREG = 5
NX = NREG * NH
LN_EPS = 1e-5
COS_EPS = 1e-8
CLAMP = 10000.0
FAR = 1e30


FRONT = 5
LAG = 2


class Attn:

    def __init__(self, name, d, qscale, proj=False, bias=False, mask=False, clip=False, split=False):
        self.name, self.d, self.qscale = name, d, qscale
        self.proj, self.bias, self.mask, self.clip, self.split = proj, bias, mask, clip, split
        self.rows = 32 if d == 16 else 64
        self.per = P // self.rows
        self.groups = NH // self.per
        self.width = NH * d
        self.vs = d + 1 if d == 16 else d
        self.ones = self.vs > d
        self.kdim, self.kt = (P, DC) if split else (CK, 2)
        self.units = NH + (1 if split else 0)
        self.qjobs = self.groups // 2
        self.vjobs = T * self.width // 512
        self.kjobs = self.qjobs + (1 if split else 0)
        self.jobs = [0, 1, 2, 5, 6] if d == 16 else [j % 7 for j in range(12)]
        self.fills = self.groups // 2


L1X = Attn("l1x", 16, 0.25, mask=True)
L2X = Attn("l2x", 64, 0.125, proj=True, bias=False)
L3X = Attn("l3x", 16, 0.25, proj=True, bias=True, clip=True)
L3F = Attn("l3f", 16, 0.25, proj=True, split=True)


class Chain:

    def __init__(self, eng, sem):
        self.eng, self.sem, self.base, self.k, self.total = eng, sem, 0, 0, 0

    def loop(self, i, per):
        self.total = self.base = self.total + self.k
        self.base = self.total + i * per
        self.k, self.per = 0, per

    def leave(self, n):
        assert self.k == self.per, f"{self.sem}: {self.k} increments in the body, {self.per} said"
        self.total += n * self.per
        self.base, self.k = self.total, 0

    def link(self, ins):
        self.k += 1
        ins.then_inc(self.sem, 1)
        self.eng.wait_ge(self.sem, self.base + self.k)


def build(nc, a, out, layers=8):
    ctx = ExitStack()
    with ctx:
        def sb(name, shape, dt=F32):
            return ctx.enter_context(nc.sbuf_tensor(name, shape, dt))

        def under(name, shape, dt=F32):
            with nc.sbuf_tensor(name, shape, dt) as t:
                return t

        def sem(name):
            return ctx.enter_context(nc.semaphore(name))

        bank = [ctx.enter_context(nc.psum_tensor(f"bank{k}", [P, 512], F32)) for k in range(8)]

        x = sb("x", [P, NT, D])
        ident = sb("ident", [P, P])
        ones = sb("ones", [P, P])
        gates_x = sb("gates_x", [P, 4])
        gates_f = sb("gates_f", [P, 4])
        tgx = sb("tgx", [P, 4])
        tgf = sb("tgf", [P, 4])
        mask_u8 = sb("mask_u8", [P, B * S], U8)
        w0v = sb("w0v", [P, DC, HV]); w0t = sb("w0t", [CK, 2, HV])
        b0v = sb("b0v", [P, 1]); b0t = sb("b0t", [P, 1])
        n1q, n1k, n1v = DC * L1X.groups * P, L1X.kt * L1X.groups * P, L1X.kt * L1X.width
        w13 = under("w13", [P, n1q + n1k + n1v])
        rows13 = sb("rows13", [P, n1q + n1k + n1v], F32R)
        wq = {"l1x": w13[:, 0:n1q].rearrange("p (c f) -> p c f", c=DC), "l3f": sb("wq_l3f", [P, DC, L3F.groups * P])}
        wk = {"l1x": w13[0:L1X.kdim, n1q:n1q + n1k].rearrange("p (c f) -> p c f", c=L1X.kt),
              "l3f": sb("wk_l3f", [L3F.kdim, L3F.kt, L3F.groups * P])}
        wv = {"l1x": w13[0:L1X.kdim, n1q + n1k:n1q + n1k + n1v].rearrange("p (c f) -> p c f", c=L1X.kt),
              "l3f": sb("wv_l3f", [L3F.kdim, L3F.kt, L3F.width])}
        for w in (wq, wk, wv):
            w["l3x"] = w["l1x"]
        wo = {s.name: sb(f"wo_{s.name}", [P, s.width // P, D]) for s in (L3X, L3F)}
        bo = {s.name: sb(f"bo_{s.name}", [P, D]) for s in (L2X, L3X, L3F)}
        bq3 = sb("bq3", [P, 4]); bk3 = sb("bk3", [P, 4]); bv3 = sb("bv3", [P, D])
        b01 = sb("b01", [P, F0 // P]); b02 = sb("b02", [P, D])
        gam = sb("gam", [P, D]); bet = sb("bet", [P, D])
        wg1 = sb("wg1", [P, DC, NE]); wg2 = sb("wg2", [P, DC, NE]); gb2 = sb("gb2", [P, NE])
        wqs = sb("wqs", [P, DC, D]); qg = sb("qg", [P, D])
        EW = 2 * DC * F1 + F1T * D
        ew = under("ew", [P, 2, EW])
        ewl = sb("ewl", [P, 2, EW], F32R)
        w2 = under("w2", [P, 2, EW])
        ewh = sb("ewh", [P, 2, EW], F32R)
        n2q, n2k = DC * L2X.groups * P, L2X.kt * L2X.groups * P
        n2v, n2o = L2X.kt * L2X.width, L2X.width // P * D
        wq["l2x"] = w2[:, 0, 0:n2q].rearrange("p (c f) -> p c f", c=DC)
        wk["l2x"] = w2[0:L2X.kdim, 0, n2q:n2q + n2k].rearrange("p (c f) -> p c f", c=L2X.kt)
        wv["l2x"] = w2[0:L2X.kdim, 1, 0:n2v].rearrange("p (c f) -> p c f", c=L2X.kt)
        wo["l2x"] = w2[:, 1, n2v:n2v + n2o].rearrange("p (c f) -> p c f", c=L2X.width // P)
        w01 = ew[:, 0, 0:DC * F0 // 2 * 2].rearrange("p (c f) -> p c f", c=DC)
        w02 = ew[:, 1, 0:F0 // P * D].rearrange("p (c f) -> p c f", c=F0 // P)

        def expert_size(f):
            return 2 * DC * f + -(-f // P) * D

        def expert(u, f):
            ft = -(-f // P)
            n = DC * f
            return [(e[:, u, 0:n].rearrange("p (c f) -> p c f", c=DC),
                     e[:, u, n:2 * n].rearrange("p (c f) -> p c f", c=DC),
                     e[:, u, 2 * n:2 * n + ft * D].rearrange("p (c f) -> p c f", c=ft)) for e in (ewh, ewl)]

        xn = sb("xn", [P, T, D])
        xt = sb("xt", [P, DC, S])
        ct = sb("ct", [CK, 2, S])
        bst = sb("bst", [P, T, 6]); mv = sb("mv", [P, T, 2]); rstd = sb("rstd", [P, T])
        ARENA = 16 * S + T * NH * 64 + (3 + 8) * 512 + 8 * S
        arena = under("arena", [P, ARENA])
        split = sb("split", [P, ARENA], F32R)
        o = [0]

        def cut(n):
            o[0] += n
            return arena[:, o[0] - n:o[0]]

        q8 = cut(8 * S).rearrange("p (g s) -> p g s", g=8)
        qT = [q8, q8[:, 4:8, :]]
        kT = cut(8 * S).rearrange("p (g s) -> p g s", g=8)
        v = cut(T * NH * 64).rearrange("p (t n) -> p t n", t=T)
        prob = [cut(512) for _ in range(3)]
        probT = [cut(512) for _ in range(8)]
        oTs = cut(8 * S).rearrange("p (g s) -> p g s", g=8)
        on = [sb(f"on{t}", [P, D]) for t in range(T)]
        oT = [sb(f"oT{t}", [P, DC, P]) for t in range(T)]
        hid0 = arena[:, 0:F0 // P * S].rearrange("p (c s) -> p c s", s=S)
        n_xt = DC * NT * P
        xth, xtl, xtw = (t[:, c:c + n_xt].rearrange("p (c s) -> p c s", c=DC)
                         for t, c in ((split, 0), (split, n_xt), (arena, n_xt)))
        tiles = [(split, arena, c) for c in range(2 * n_xt, ARENA - 511, 512)]
        tiles += [(rows13, w13, k * 512) for k in range(2 * HS["l1f"] - len(tiles))]
        hid = {}
        for n, hs in HS.items():
            high, low, whole = ([t[k][:, t[2]:t[2] + 512] for t in tiles[c:c + hs]]
                                for k, c in ((0, 0), (0, hs), (1, hs)))
            hid[n] = (high, low, whole)
        assert o[0] <= ARENA, (o[0], ARENA)
        scr = sb("scr", [P, NT * NE * NE])
        sil = [sb(f"sil{k}", [P, 512]) for k in range(2)]
        sc = sil + [scr[:, 512:1024]]
        evens = sb("evens", [P, 2])
        even = sb("even", [P, 2])
        tmp = scr[:, 0:D]
        z = scr[:, D:2 * D]
        nmax = sb("nmax", [P, NH + 1, T])
        esum = sb("esum", [P, NH, T])
        rec = sb("rec", [P, NH])
        recs = sb("recs", [P, T, NH])
        idle = sb("idle", [P, 1])
        pidle = sb("pidle", [P, 1])
        norms = sb("norms", [P, 2 * T])
        diag = probT[0][:, 0:T * P].rearrange("p (t q) -> p t q", t=T)
        mhalf = sb("mhalf", [P, 2 * NH]); minus1 = sb("minus1", [P, T])
        gate = sb("gate", [P, NT, 10])
        lg = sb("lg", [P, NT, NE]); sel = sb("sel", [P, NT, NE]); gm = sb("gm", [P, NT])
        larger = sb("larger", [P, NT, NE])
        bsta = sb("bsta", [P, NT, 6]); mva = sb("mva", [P, NT, 2]); rstda = sb("rstda", [P, NT])
        tri = sb("tri", [P, NE, NE])
        sim = sb("sim", [P, NT]); regm = sb("regm", [P, NT]); ss = sb("ss", [P, 4 * NH])
        qp = sb("qp", [P, NT, 2]); kp = sb("kp", [P, NT, 2]); qk2 = sb("qk2", [P, T, 4])
        mrow = sb("mrow", [P, 2, S]); mregq = sb("mregq", [P, NREG]); selw = sb("selw", [P, P])
        qxs = sb("qxs", [P, 4 * NREG]); qx = sb("qx", [P, 4, NX])
        hm = sb("hm", [P, 4, NH]); bm = sb("bm", [P, NH]); rsel = sb("rsel", [P, P]); wcol = sb("wcol", [P, 1])
        onx = sb("onx", [P, D])

        def xnb(b, t):
            return xn[:, t, :] if b == 0 else on[t][:, :]

        names = ("x_in", "w0_in", "w0f_in", "att_in", "consts", "tanh", "phase", "out_done", "w3_in", "w2a_in", "w2b_in",
                 "xn", "xnT", "xt")
        g = {n: sem(n) for n in names}

        def group(p, *ns):
            return {n: sem(f"{p}_{n}") for n in ns}

        ph = {}
        for s in (L1X, L2X, L3X, L3F):
            ph[s.name] = group(s.name, "ct", "q", "k", "v", "qc", "kc", "vc", "s", "mx", "e", "pT", "pTc", "pv",
                               "oc", "dve", "rq", "rd",
                               *(("y",) if s.proj else ()),
                               *(("z",) if s.ones else ("pn", "psum")),
                               *(("on", "onT", "oT") if s.ones and s.proj else ()),
                               *(("cols", "mrow", "mrowc", "xs", "reg") if s.split else ()))
        l0x = group("l0x", "rq", "rd", "ct", "vt", "vtc", "dots", "dg", "rows", "dve", "act")
        l0f = group("l0f", "rq", "rd", "h", "hc", "y", "dve")
        moe = {}
        for n in ("l1f", "l2f"):
            moe[n] = group(n, "rq", "rd", "lg", "gd", "ga", "w0", "w1", "wh", "ws", "xh", "xs",
                           "a", "sil", "hid", "y", "yc", "dve")
        sm = group("sim", "rq", "rd", "q", "dve", "pool")

        block = ctx.enter_context(nc.Block())
        n_phase = {"l0x": 1, "l0f": 2, "l1x": 3, "l1f": 4, "l2x": 5, "l2f": 6, "l3x": 7, "sim": 8, "l3f": 9}
        order = [["l0x"], ["l0f"], ["l1x"], ["l1f"], ["l2x"], ["l2f"], ["l3x"], ["sim", "l3f"]]
        run = [n for l in order[:layers] for n in l]
        attn = {s.name: s for s in (L1X, L2X, L3X, L3F)}

        def entries(name, n):
            return n + (n_phase[name] - 1) * B

        @block.sync
        def _(sp):
            sp.dma_start(x[:, :, :], a["x"].rearrange("b (t p) d -> p (b t) d", p=P)).then_inc(g["x_in"], 16)
            for dst, src in ((w0v[:, :, :], a["w0v"]), (w0t[:, :, :], a["w0t"]), (b0v[:, :], a["b0v"]),
                             (b0t[:, :], a["b0t"]), (gates_x[:, :], a["g_xattn"].partition_broadcast(P)),
                             (gates_f[:, :], a["g_ffn"].partition_broadcast(P))):
                sp.dma_start(dst, src).then_inc(g["w0_in"], 16)

            def contexts(name, sem_in, sem_used, per):
                if n_phase[name] > 1:
                    sp.wait_ge(g["phase"], n_phase[name] - 1)
                sp.dma_start(ct[:, :, :], a["ctxT"][0, :, :, :]).then_inc(sem_in, 16)
                with sp.Fori(1, B) as n:
                    sp.wait_ge(sem_used, n * per)
                    sp.dma_start(ct[:, :, :], a["ctxT"][n, :, :, :]).then_inc(sem_in, 16)

            contexts("l0x", l0x["ct"], l0x["vt"], 1)
            def first_experts(name, f, src):
                sp.wait_ge(g["phase"], 2 if name == "l1f" else 4)
                for u in range(2):
                    sp.dma_start(ew[:, u, 0:expert_size(f)], src[u, :, :]).then_inc(moe[name][f"w{u}"], 16)

            def more_experts(name, f, src, ne):
                with sp.Fori(1, ne // 2) as i:
                    for u in range(2):
                        sp.wait_ge(moe[name]["y"], (i * 2 + u - 1) * NT)
                        sp.dma_start(ew[:, u, 0:expert_size(f)], src[i * 2 + u, :, :])\
                            .then_inc(moe[name][f"w{u}"], 16)

            if "l1f" in run:
                first_experts("l1f", F1, a["we1"])
            if "l1x" in run:
                contexts("l1x", ph["l1x"]["ct"], ph["l1x"]["v"], L1X.vjobs)
            if "l1f" in run:
                more_experts("l1f", F1, a["we1"], NE)
            if "l2f" in run:
                first_experts("l2f", F2, a["we2"])
            if "l2x" in run:
                contexts("l2x", ph["l2x"]["ct"], ph["l2x"]["v"], L2X.vjobs)
            if "l2f" in run:
                more_experts("l2f", F2, a["we2"], NE + 2)
            if "l3x" in run:
                contexts("l3x", ph["l3x"]["ct"], ph["l3x"]["v"], L3X.vjobs)
            sp.wait_ge(g["phase"], len(run))
            sp.dma_start(out.rearrange("b (t p) d -> p (b t) d", p=P), x[:, :, :]).then_inc(g["out_done"], 16)
            sp.wait_ge(g["out_done"], 16)

        @block.gpsimd
        def _(pool):
            nc.gpsimd.memset(ident[:, :], 0.0).then_inc(g["consts"], 1)
            nc.gpsimd.memset(ones[:, :], 1.0).then_inc(g["consts"], 1)
            nc.gpsimd.memset(tri[:, :, :], 1.0).then_inc(g["consts"], 1)
            nc.gpsimd.memset(regm[:, :], 0.0).then_inc(g["consts"], 1)
            nc.gpsimd.memset(mrow[:, :, :], 0.0).then_inc(g["consts"], 1)
            nc.gpsimd.memset(mregq[:, :], 0.0).then_inc(g["consts"], 1)
            nc.gpsimd.memset(selw[:, :], 0.0).then_inc(g["consts"], 1)
            nc.gpsimd.memset(hm[:, :, :], 0.0).then_inc(g["consts"], 1)
            nc.gpsimd.memset(bm[:, :], 0.0).then_inc(g["consts"], 1)
            nc.gpsimd.memset(rsel[:, :], 0.5).then_inc(g["consts"], 1)
            nc.gpsimd.memset(wcol[:, :], 1.0).then_inc(g["consts"], 1)
            nc.gpsimd.memset(mhalf[:, :], -0.5).then_inc(g["consts"], 1)
            nc.gpsimd.memset(even[:, :], 0.0).then_inc(g["consts"], 1)
            nc.gpsimd.memset(minus1[:, :], -1.0).then_inc(g["consts"], 1)
            pool.wait_ge(g["consts"], 14)
            for k in range(2):
                for base in (0, 64):
                    r0 = base + 32 * k
                    nc.gpsimd.memset(even[r0:r0 + 32, k:k + 1], 1.0).then_inc(g["consts"], 1)
            done = [18]

            def select(t, fill, base, pattern, cm, op=ALU.not_equal):
                pool.wait_ge(g["consts"], done[0])
                nc.gpsimd.affine_select(out=t, in_=t, compare_op=op, fill=fill, base=base,
                                        pattern=pattern, channel_multiplier=cm).then_inc(g["consts"], 1)
                done[0] += 1

            select(ident[:, :], 1.0, 0, [[-1, P]], 1)
            select(tri[:, :, :], 0.0, 0, [[1, NE], [-1, NE]], 0, ALU.is_gt)
            reg = regm[:, :].rearrange("p (b t) -> p b t", t=T)[:, :, 0:1]
            select(reg, 1.0, -NREG, [[0, B], [0, 1]], 1, ALU.is_ge)
            select(mregq[:, :], 1.0, -1, [[0, NREG]], 1)
            select(selw[:, :].rearrange("p (h r) -> p h r", r=32), 1.0, -16, [[0, 4], [1, 32]], -1)
            select(selw[:, :], 0.0, 1, [[0, P]], -1, ALU.is_ge)
            pool.wait_ge(g["consts"], done[0])
            nc.gpsimd.memset(hm[:, :, :], 1.0).then_inc(g["consts"], 1)
            done[0] += 1
            select(hm[:, :, :], 0.0, 0, [[128, 4], [-32, NH]], 1, ALU.is_ge)
            select(hm[:, :, :], 0.0, 31, [[-128, 4], [32, NH]], -1, ALU.is_ge)
            for r in range(NREG):
                select(bm[:, :], 1.0, -NH * r, [[-1, NH]], 1)
            select(rsel[:, :], 0.0, 0, [[-NH, P]], 1, ALU.is_ge)
            select(rsel[:, :], 0.0, NH - 1, [[NH, P]], -1, ALU.is_ge)
            select(wcol[:, :], 0.5, -NREG, [[0, 1]], 1, ALU.is_ge)
            g["n_consts"] = done[0]

            pool.dma_start(w01, a["w01"]).then_inc(g["w0f_in"], 16)
            pool.dma_start(w02, a["w02"]).then_inc(g["w0f_in"], 16)
            loads = [(b01[:, :], a["b01"]), (b02[:, :], a["b02"].partition_broadcast(P)),
                     (gam[:, :], a["gamma"].partition_broadcast(P)), (bet[:, :], a["beta"].partition_broadcast(P)),
                     (mask_u8[:, :], a["mask"].partition_broadcast(P))]
            for s in (L1X, L2X, L3X, L3F):
                qkv = [(wq[s.name][:, :, :], a[f"wq_{s.name}"]), (wk[s.name][:, :, :], a[f"wk_{s.name}"]),
                       (wv[s.name][:, :, :], a[f"wv_{s.name}"])]
                if s is L3X:
                    later = qkv
                elif s is L2X:
                    later2 = qkv + [(wo["l2x"], a["wo_l2x"])]
                    loads += [(bo["l2x"][:, :], a["bo_l2x"].partition_broadcast(P))]
                    continue
                else:
                    loads += qkv
                if s.proj:
                    loads += [(wo[s.name][:, :, :], a[f"wo_{s.name}"]),
                              (bo[s.name][:, :], a[f"bo_{s.name}"].partition_broadcast(P))]
            loads += [(bq3[:, :], a["bq3"]), (bk3[:, :], a["bk3"]), (bv3[:, :], a["bv3"].partition_broadcast(P)),
                      (wg1[:, :, :], a["wg1"]), (wg2[:, :, :], a["wg2"]), (gb2[:, :], a["gb2"].partition_broadcast(P)),
                      (wqs[:, :, :], a["wqs"]), (qg[:, :], a["qg"].partition_broadcast(P))]
            for dst, src in loads:
                pool.dma_start(dst, src).then_inc(g["att_in"], 16)
            g["n_loads"] = len(loads)

            def root(m, k, out_, in_, power):
                pool.wait_ge(m["rq"], k)
                nc.gpsimd.tensor_tensor(out_, in_, power, ALU.pow).then_inc(m["rd"], 1)

            for name in run:
                if name == "l0x":
                    with pool.Fori(0, B) as n:
                        root(l0x, n * 2 + 1, rstd[:, :], rstd[:, :], mhalf[:, 0:T])
                        root(l0x, n * 2 + 2, norms[:, :], norms[:, :], mhalf[:, 0:2 * T])
                elif name == "l0f":
                    with pool.Fori(0, B) as n:
                        for k in range(2):
                            root(l0f, n * 2 + k + 1, rstd[:, :], rstd[:, :], mhalf[:, 0:T])
                elif name == "sim":
                    root(sm, 1, ss[:, 0:NH], ss[:, 0:NH], mhalf[:, 0:NH])
                    with pool.Fori(0, B) as n:
                        root(sm, n * 2 + 2, rstd[:, :], rstd[:, :], mhalf[:, 0:T])
                        root(sm, n * 2 + 3, ss[:, 0:2 * NH], ss[:, 0:2 * NH], mhalf[:, :])
                    pool.wait_ge(sm["dve"], SIM_STEPS_BEFORE)
                    nc.gpsimd.partition_all_reduce(ss[:, 2:4], ss[:, 0:2], P, RMAX).then_inc(sm["pool"], 1)
                else:
                    m = ph[name] if name in ph else moe[name]
                    if name in moe:
                        ne, f = (NE, F1) if name == "l1f" else (NE + 2, F2)
                        size = expert_size(f)
                        root(m, 1, rstda[:, :], rstda[:, :], mhalf[:, 0:NT])

                        def split_weights(u, expert_no, rounds):
                            pool.wait_ge(m[f"w{u}"], rounds * 16)
                            w, wl, wh = (t[:, u, 0:size] for t in (ew, ewl, ewh))
                            nc.gpsimd.tensor_tensor(pidle[:, :], minus1[:, 0:1], minus1[:, 0:1], ALU.mult)
                            nc.gpsimd.tensor_copy(wh, w).then_inc(m["wh"], 1)
                            pool.wait_ge(m["wh"], expert_no + 1)
                            nc.gpsimd.tensor_tensor(wl, w, wh, ALU.subtract).then_inc(m["ws"], 1)

                        split_weights(0, 0, 1)
                        for c in range(NBLK):
                            pool.wait_ge(m["xh"], c + 1)
                            if c == 0:
                                pool.wait_ge(m["lg"], 1)
                            cols = slice(c * 512, c * 512 + 512)
                            nc.gpsimd.tensor_tensor(xtl[:, :, cols], xtw[:, :, cols], xth[:, :, cols],
                                                    ALU.subtract).then_inc(m["xs"], 1)
                        with pool.Fori(0, ne // 2 - 1) as i:
                            split_weights(1, i * 2 + 1, i + 1)
                            split_weights(0, i * 2 + 2, i + 2)
                        split_weights(1, ne - 1, ne // 2)
                        if name == "l1f":
                            for sem_, y, pairs in (("w2a_in", (NE - 1) * NT, later2[0:2]),
                                                   ("w2b_in", NE * NT, later2[2:4]), ("w3_in", NE * NT, later)):
                                pool.wait_ge(m["y"], y)
                                for dst, src in pairs:
                                    pool.dma_start(dst, src).then_inc(g[sem_], 16)
                        continue
                    if name != "l2x":
                        with pool.Fori(0, B) as n:
                            root(m, n + 1, rstd[:, :], rstd[:, :], mhalf[:, 0:T])
                        continue

                    def normalise(n, ahead):
                        for h in range(NH):
                            pool.wait_ge(m["e"], n * NH + h + 1)
                            nc.gpsimd.tensor_tensor(esum[:, h, :], esum[:, h, :], minus1[:, 0:T], ALU.pow)\
                                .then_inc(m["psum"], 1)
                            pool.wait_ge(m["psum"], n * NH + h + 1)
                            p3 = prob[h % 3].rearrange("p (t k) -> p t k", t=T)
                            nc.gpsimd.tensor_tensor(p3, p3, esum[:, h, :].rearrange("p (t o) -> p t o", o=1)
                                                    .broadcast_to([P, T, S]), ALU.mult).then_inc(m["pn"], 1)
                            if h == FRONT and ahead:
                                root(m, n + 2, rstd[:, :], rstd[:, :], mhalf[:, 0:T])

                    root(m, 1, rstd[:, :], rstd[:, :], mhalf[:, 0:T])
                    with pool.Fori(0, B - 1) as n:
                        normalise(n, True)
                    normalise(B - 1, False)

        @block.vector
        def _(dve):
            V = nc.vector
            stt, ts, tt = V.scalar_tensor_tensor, V.tensor_scalar, V.tensor_tensor

            def root(m, k, ins):
                ins.then_inc(m["rq"], 1)
                dve.wait_ge(m["rd"], k)

            def stats(ch, m, k, srcs):
                for t, src in enumerate(srcs):
                    ins = V.bn_stats(bst[:, t, :], src)
                ch.link(ins)
                V.memset(idle[:, 0:1], 0.0)
                for t in range(T):
                    ins = V.bn_aggr(mv[:, t, :], bst[:, t, :])
                ch.link(ins)
                root(m, k, ts(rstd[:, :], mv[:, :, 1], LN_EPS, None, ALU.add))

            def layernorm(ch, m, n, k):
                stats(ch, m, k, [x[:, n * T + t, :] for t in range(T)])
                for t in range(T):
                    ts(xn[:, t, :], x[:, n * T + t, :], mv[:, t, 0:1], rstd[:, t:t + 1],
                       ALU.subtract, ALU.mult).then_inc(g["xn"], 1)
            LN = 2

            def all_stats(ch, m):
                for t in range(NT):
                    ins = V.bn_stats(bsta[:, t, :], x[:, t, :])
                ch.link(ins)
                V.memset(idle[:, 0:1], 0.0)
                for t in range(NT):
                    ins = V.bn_aggr(mva[:, t, :], bsta[:, t, :])
                ch.link(ins)
                root(m, 1, ts(rstda[:, :], mva[:, :, 1], LN_EPS, None, ALU.add))

            def normalise(n, b):
                for t in range(T):
                    r = bass.ds(n * T + t, 1)
                    ts(xnb(b, t), x[:, n * T + t, :], mva[:, r, 0], rstda[:, r],
                       ALU.subtract, ALU.mult).then_inc(g["xn"], 1)

            def add_to_x(n, t, branch, scalar):
                return stt(x[:, n * T + t, :], branch, scalar, x[:, n * T + t, :], ALU.mult, ALU.add)

            def similarity():
                ch = Chain(dve, l0x["dve"])
                with dve.Fori(0, B) as n:
                    ch.loop(n, LN + 1 + 3 * T)
                    layernorm(ch, l0x, n, n * 2 + 1)
                    dve.wait_ge(l0x["dots"], n + 1)
                    root(l0x, n * 2 + 2, V.tensor_copy(norms[:, :], bank[4][:, 0:2 * T]))
                    ch.link(ts(norms[:, :], norms[:, :], FAR, None, ALU.min))
                    for t in range(T):
                        ins = ts(diag[:, t, :], ident[:, :], norms[:, T + t:T + t + 1], None, ALU.mult)
                    ins.then_inc(l0x["dg"], 1)
                    dve.wait_ge(l0x["rows"], n + 1)
                    for t in range(T):
                        ch.link(ts(tmp, bank[3][:, 0:S], norms[:, t:t + 1], 1.0 / COS_EPS, ALU.mult, ALU.min))
                        ch.link(tt(tmp, bank[2][:, t * S:(t + 1) * S], tmp, ALU.mult))
                        ch.link(add_to_x(n, t, tmp, tgx[:, 0:1]))
                ch.leave(B)
                V.memset(idle[:, 0:1], 0.0).then_inc(g["phase"], 1)

            def feed_forward():
                ch = Chain(dve, l0f["dve"])
                with dve.Fori(0, B) as n:
                    ch.loop(n, 2 * LN + T * 6)
                    layernorm(ch, l0f, n, n * 2 + 1)
                    zs = [scr[:, (1 + t) * D:(2 + t) * D] for t in range(T)]
                    for t in range(T):
                        dve.wait_ge(l0f["y"], n * T + t + 1)
                        ch.link(tt(zs[t], bank[6 + t][:, 0:D], b02[:, :], ALU.add))
                        ch.link(tt(zs[t], zs[t], xn[:, t, :], ALU.add))
                    stats(ch, l0f, n * 2 + 2, zs)
                    for t in range(T):
                        ch.link(ts(zs[t], zs[t], mv[:, t, 0:1], rstd[:, t:t + 1], ALU.subtract, ALU.mult))
                        ch.link(tt(zs[t], zs[t], gam[:, :], ALU.mult))
                        ch.link(tt(zs[t], zs[t], bet[:, :], ALU.add))
                        ch.link(add_to_x(n, t, zs[t], tgf[:, 0:1]))
                ch.leave(B)
                V.memset(idle[:, 0:1], 0.0).then_inc(g["phase"], 1)

            def attention(s, gi):
                m = ph[s.name]
                ch = Chain(dve, m["dve"])
                U = s.units
                groups = s.groups + (1 if s.split else 0)
                vh = v[:, :, 0:NH * s.vs].rearrange("p t (h e) -> p t h e", h=NH)
                if s.ones:
                    for t in range(T):
                        ch.link(V.memset(vh[:, t, :, s.d:s.d + 1], 1.0))

                def front(n):
                    dve.wait_ge(g["xnT"], entries(s.name, n))
                    layernorm(ch, m, n, n + 1)
                    if s.split:
                        V.tensor_copy(qk2[:, :, 0:2], qp[:, bass.ds(n * T, T), :])
                        V.tensor_copy(qk2[:, :, 2:4], kp[:, bass.ds(n * T, T), :]).then_inc(m["cols"], 1)

                def mask_rows(n):
                    if s.split:
                        dve.wait_ge(m["mrow"], n + 1)
                        V.tensor_copy(mrow[0:2, :, :], bank[7][0:2, :].rearrange("p (k s) -> p k s", k=2))\
                            .then_inc(m["mrowc"], 1)

                def projected(n):
                    for j in range(s.qjobs):
                        dve.wait_ge(m["q"], n * s.qjobs + j + 1)
                        src = bank[s.jobs[j]][:, :].rearrange("p (k s) -> p k s", k=2)
                        for w in range(2 if s.ones else 1):
                            dst = qT[w][:, 2 * j:2 * j + 2, :]
                            if s.mask:
                                for k in range(2):
                                    ins = stt(dst[:, k, :], src[:, k, :], evens[:, w:w + 1],
                                              mask_u8[:, bass.ds(n * S, S)], ALU.mult, ALU.mult)
                            elif s.bias:
                                for k in range(2):
                                    ins = ts(dst[:, k, :], src[:, k, :], bq3[:, 2 * j + k:2 * j + k + 1],
                                             evens[:, w:w + 1], ALU.add, ALU.mult)
                            elif s.ones:
                                ins = ts(dst, src, evens[:, w:w + 1], None, ALU.mult)
                            else:
                                ins = ts(dst, src, s.qscale, None, ALU.mult)
                        ins.then_inc(m["qc"], 1)
                    if s.bias:
                        dve.wait_ge(m["v"], n + 1)
                        for t in range(T):
                            ins = tt(vh[:, t, :, 0:s.d],
                                     bank[s.jobs[-1]][:, t * D:(t + 1) * D].rearrange("p (h e) -> p h e", h=NH),
                                     bv3[:, :].rearrange("p (h e) -> p h e", h=NH), ALU.add)
                        ins.then_inc(m["vc"], 1)
                    if s.split:
                        dve.wait_ge(m["k"], (n + 1) * s.kjobs)
                        ch.link(ts(qxs[:, :], bank[7][:, 0:4 * NREG], s.qscale, None, ALU.mult))
                        qv = qxs[:, :].rearrange("p (g r) -> p g r", g=4)
                        for r in range(NREG):
                            ins = tt(qx[:, :, r * NH:(r + 1) * NH], hm[:, :, :],
                                     qv[:, :, r:r + 1].broadcast_to([P, 4, NH]), ALU.mult)
                        ins.then_inc(m["xs"], 1)

                def heads(n, ahead):
                    for h in range(U + LAG):
                        if h < U:
                            dve.wait_ge(m["s"], n * U + h + 1)
                            if h == NH:
                                V.tensor_reduce(nmax[0:NX, h, 0:1], bank[h % 3][0:NX, 0:S], AXX, ALU.max, negate=True)\
                                    .then_inc(m["mx"], 1)
                            else:
                                src = bank[h % 3][:, :]
                                if s.clip:
                                    if h >= 3:
                                        dve.wait_ge(m["e"], n * NH + h - 2)
                                    ch.link(ts(sc[h % 3][:, :], src, CLAMP, -CLAMP, ALU.min, ALU.max))
                                    src = sc[h % 3][:, :]
                                V.tensor_reduce(nmax[:, h, :], src.rearrange("p (t k) -> p t k", t=T),
                                                AXX, ALU.max, negate=True).then_inc(m["mx"], 1)
                        if h >= LAG and not s.clip:
                            k = h - LAG
                            dve.wait_ge(m["pT"], n * U + k + 1)
                            if k >= 8:
                                dve.wait_ge(m["pv"], n * groups + (k - 8) // s.per + 1)
                            w = 2 * NX if k == NH else 512
                            V.tensor_copy(probT[k % 8][:, 0:w], bank[3 + k % 2][:, 0:w]).then_inc(m["pTc"], 1)
                        if h == FRONT and ahead:
                            front(n + 1)
                        if h == FRONT + 3 and ahead:
                            mask_rows(n + 1)

                def outputs(n):
                    if s.split:
                        dve.wait_ge(m["pv"], (n + 1) * groups)
                        ov = bank[7][0:NX, 0:NH * s.vs].rearrange("p (h e) -> p h e", h=NH)
                        ch.link(V.reciprocal(rec[0:NX, :], ov[:, :, s.d]))
                        ch.link(tt(rec[0:NX, :], rec[0:NX, :], bm[0:NX, :], ALU.mult))
                        tt(onx[0:NX, :].rearrange("p (h e) -> p h e", h=NH), ov[:, :, 0:s.d],
                           rec[0:NX, :].rearrange("p (h o) -> p h o", o=1).broadcast_to([NX, NH, s.d]),
                           ALU.mult).then_inc(m["xs"], 1)
                    for t in range(T):
                        dve.wait_ge(m["z"], n * T + t + 1)
                        z4 = bank[3 + t][:, :].rearrange("p (h e) -> p h e", h=NH)
                        ch.link(V.reciprocal(recs[:, t, :], z4[:, :, s.d]))
                        dst = (on[t][:, :] if s.proj else tmp).rearrange("p (h e) -> p h e", h=NH)
                        ins = tt(dst, z4[:, :, 0:s.d],
                                 recs[:, t, :].rearrange("p (h o) -> p h o", o=1).broadcast_to([P, NH, s.d]),
                                 ALU.mult)
                        if s.split and t == 0:
                            ch.link(ins)
                            dve.wait_ge(m["reg"], n + 1)
                            ins = stt(on[0][:, :], on[0][:, :], wcol[:, 0:1], bank[7][:, 0:D], ALU.mult, ALU.add)
                        if s.proj:
                            ins.then_inc(m["on"], 1)
                        else:
                            ch.link(ins)
                            ch.link(add_to_x(n, t, tmp, tgx[:, gi:gi + 1]))

                def finish(n):
                    for t in range(T):
                        dve.wait_ge(m["y"], n * T + (t + 1 if s.ones else T))
                        y = bank[3 + t][:, S:2 * S] if s.ones else bank[7][:, t * S:(t + 1) * S]
                        ch.link(tt(tmp, y, bo[s.name][:, :], ALU.add))
                        ch.link(add_to_x(n, t, tmp, (tgf if s.split else tgx)[:, gi:gi + 1]))

                front_links = LN
                proj_links = 1 if s.split else 0
                body = (2 * NH // 2 if s.clip else 0)
                if s.ones:
                    body += T * (1 if s.proj else 3) + (3 if s.split else 0)
                body += 2 * T if s.proj else 0
                ch.link(ts(evens[:, :], even[:, :], s.qscale, None, ALU.mult))
                front(0)
                mask_rows(0)
                projected(0)
                with dve.Fori(0, B - 1) as n:
                    ch.loop(n, body + front_links + proj_links)
                    heads(n, True)
                    if s.ones:
                        outputs(n)
                    projected(n + 1)
                    if s.proj:
                        finish(n)
                ch.leave(B - 1)
                heads(B - 1, False)
                if s.ones:
                    outputs(B - 1)
                if s.proj:
                    finish(B - 1)
                V.memset(idle[:, 0:1], 0.0).then_inc(g["phase"], 1)

            def mixture(name, gi, ne):
                m = moe[name]
                ch = Chain(dve, m["dve"])
                f = F1 if name == "l1f" else F2
                ft = -(-f // P)
                all_stats(ch, m)

                def high_part(c):
                    dve.wait_ge(g["xt"], entries(name, 2 * c + 2))
                    cols = bass.ds(c * 512, 512)
                    V.tensor_copy(xth[:, :, cols], xtw[:, :, cols]).then_inc(m["xh"], 1)

                def two_entries(j):
                    for b in range(2):
                        dve.wait_ge(g["xnT"], entries(name, j * 2 + b) - 1)
                        normalise(j * 2 + b, b)

                two_entries(0)
                with dve.Fori(1, B // 2) as j:
                    two_entries(j)
                    high_part(j - 1)
                high_part(NBLK - 1)
                dve.wait_ge(m["lg"], 1)
                full = [P, NT, NE]
                per_tok = [P, NT, 1]
                gmv = gm[:, :].rearrange("p (t o) -> p t o", o=1)
                ch.link(V.tensor_copy(lg[:, :, :], bank[0][:, 0:NT * NE].rearrange("p (t e) -> p t e", t=NT)))
                ch.link(V.tensor_reduce(gm[:, :], lg[:, :, :], AXX, ALU.max))
                ch.link(tt(sel[:, :, :], lg[:, :, :], gmv.broadcast_to(full), ALU.subtract))
                V.memset(idle[:, 0:1], 0.0).then_inc(m["gd"], 1)
                dve.wait_ge(m["ga"], 1)
                if name == "l2f":
                    ch.link(V.tensor_reduce(gm[:, :], sel[:, :, :], AXX, ALU.add))
                    ch.link(V.reciprocal(gm[:, :], gm[:, :]))
                    ch.link(tt(sel[:, :, :], sel[:, :, :], gmv.broadcast_to(full), ALU.mult))
                    ch.link(tt(lg[:, :, :], sel[:, :, :],
                               gb2[:, :].rearrange("p (o e) -> p o e", o=1).broadcast_to(full), ALU.add))
                rank = scr[:, 0:NT * NE * NE].rearrange("p (t e j) -> p t e j", e=NE, j=NE)
                for e in range(NE):
                    ch.link(tt(rank[:, :, e, :], lg[:, :, :], lg[:, :, e:e + 1].broadcast_to(full), ALU.is_equal))
                    ch.link(tt(rank[:, :, e, :], rank[:, :, e, :],
                               tri[:, e:e + 1, :].broadcast_to(full), ALU.mult))
                    ch.link(tt(larger[:, :, :], lg[:, :, :], lg[:, :, e:e + 1].broadcast_to(full), ALU.is_gt))
                    ch.link(tt(rank[:, :, e, :], rank[:, :, e, :], larger[:, :, :], ALU.add))
                ch.link(V.tensor_reduce(lg[:, :, :], rank, AXX, ALU.add))
                ch.link(ts(lg[:, :, :], lg[:, :, :], 1.5, None, ALU.is_lt))
                ch.link(tt(sel[:, :, :], sel[:, :, :], lg[:, :, :], ALU.mult))
                if name == "l1f":
                    ch.link(V.tensor_reduce(gm[:, :], sel[:, :, :], AXX, ALU.add))
                    ch.link(V.reciprocal(gm[:, :], gm[:, :]))
                    ch.link(tt(sel[:, :, :], sel[:, :, :], gmv.broadcast_to(full), ALU.mult))
                else:
                    ch.link(V.memset(gate[:, :, NE:NE + 2], 1.0))
                    ch.link(ts(gate[:, :, NE:NE + 2], gate[:, :, NE:NE + 2], tgf[:, gi:gi + 1], None, ALU.mult))
                ch.link(ts(gate[:, :, 0:NE], sel[:, :, :], tgf[:, gi:gi + 1], None, ALU.mult))
                V.memset(idle[:, 0:1], 0.0).then_inc(m["yc"], 1)
                with dve.Fori(0, ne // 2) as i:
                    ch.loop(i, 2 * NBLK * ft * 2)
                    for u in range(2):
                        for blk in range(NBLK + 1):
                            blocks = (i * 2 + u) * NBLK + blk
                            if blk < NBLK:
                                for h in range(ft):
                                    if h == 1 and blk >= 1:
                                        expert_out(m, i, u, blk - 1, 4 * (blocks - 1))
                                    r = min(P, f - h * P)
                                    dve.wait_ge(m["sil"], blocks * ft + h + 1)
                                    slot = ((u * NBLK + blk) * ft + h) % HS[name]
                                    hi, lo, whole = (t[slot][0:r, :] for t in hid[name])
                                    ch.link(tt(whole, sil[h % 2][0:r, :], bank[2 + h % 2][0:r, :], ALU.mult))
                                    ch.link(V.tensor_copy(hi, whole))
                                    tt(lo, whole, hi, ALU.subtract).then_inc(m["hid"], 1)
                            else:
                                expert_out(m, i, u, blk - 1, 4 * (blocks - 1))
                ch.leave(ne // 2)
                dve.wait_ge(m["hid"], ne * NBLK * ft)
                dve.wait_ge(m["yc"], ne * NBLK * 4 + 1)
                V.memset(idle[:, 0:1], 0.0).then_inc(g["phase"], 1)

            def expert_out(m, i, u, blk, before):
                for k in range(4):
                    t = blk * 4 + k
                    dve.wait_ge(m["y"], before + k + 1)
                    stt(x[:, t, :], bank[4 + k % 4][:, 0:D], gate[:, t, bass.ds(i * 2 + u, 1)], x[:, t, :],
                        ALU.mult, ALU.add).then_inc(m["yc"], 1)


            def guide():
                ch = Chain(dve, sm["dve"])
                q16 = lambda t: t.rearrange("p (h e) -> p h e", h=NH)
                ch.link(tt(tmp, qg[:, :], qg[:, :], ALU.mult))
                root(sm, 1, V.tensor_reduce(ss[:, 0:NH], q16(tmp), AXX, ALU.add))
                ch.link(tt(q16(qg[:, :]), q16(qg[:, :]),
                           ss[:, 0:NH].rearrange("p (h o) -> p h o", o=1).broadcast_to([P, NH, 16]), ALU.mult))
                with dve.Fori(0, B) as n:
                    ch.loop(n, LN + T * 5 + 2)
                    layernorm(ch, sm, n, n * 2 + 2)
                    for t in range(T):
                        dve.wait_ge(sm["q"], n * T + t + 1)
                        ch.link(V.tensor_copy(z, bank[t][:, 0:D]))
                        ch.link(tt(tmp, z, z, ALU.mult))
                        ins = V.tensor_reduce(ss[:, t * NH:(t + 1) * NH], q16(tmp), AXX, ALU.add)
                        ch.link(ins)
                        ch.link(tt(tmp, z, qg[:, :], ALU.mult))
                        ch.link(V.tensor_reduce(ss[:, (2 + t) * NH:(3 + t) * NH], q16(tmp), AXX, ALU.add))
                    root(sm, n * 2 + 3, V.memset(idle[:, 0:1], 0.0))
                    ch.link(tt(ss[:, 2 * NH:4 * NH], ss[:, 0:2 * NH], ss[:, 2 * NH:4 * NH], ALU.mult))
                    ch.link(V.tensor_reduce(sim[:, bass.ds(n * T, T)],
                                            ss[:, 2 * NH:4 * NH].rearrange("p (t h) -> p t h", h=NH), AXX, ALU.add))
                ch.leave(B)
                ch.link(ts(sim[:, :], sim[:, :], 1.0 / NH, None, ALU.mult))
                nreg = scr[:, 0:NT]
                t0 = scr[:, NT:2 * NT]
                t1 = scr[:, 2 * NT:3 * NT]
                ch.link(ts(nreg, regm[:, :], -1.0, 1.0, ALU.mult, ALU.add))
                ch.link(tt(t0, sim[:, :], nreg, ALU.mult))
                ch.link(stt(t1, regm[:, :], -FAR, t0, ALU.mult, ALU.add))
                ch.link(V.tensor_reduce(ss[:, 0:1], t1, AXX, ALU.max))
                ch.link(stt(t1, regm[:, :], FAR, t0, ALU.mult, ALU.add))
                ch.link(ts(t1, t1, -1.0, None, ALU.mult))
                ch.link(V.tensor_reduce(ss[:, 1:2], t1, AXX, ALU.max))
                assert ch.base + ch.k == SIM_STEPS_BEFORE, ch.base + ch.k
                dve.wait_ge(sm["pool"], 1)
                ch.link(ts(t0, sim[:, :], ss[:, 3:4], None, ALU.add))
                ch.link(tt(ss[:, 4:5], ss[:, 2:3], ss[:, 3:4], ALU.add))
                ch.link(V.reciprocal(ss[:, 4:5], ss[:, 4:5]))
                ch.link(ts(t0, t0, ss[:, 4:5], None, ALU.mult))
                ch.link(ts(t0, t0, 0.9, None, ALU.is_gt))
                ch.link(tt(qp[:, :, 0], t0, regm[:, :], ALU.max))
                ch.link(ts(qp[:, :, 1], qp[:, :, 0], -1.0, 1.0, ALU.mult, ALU.add))
                ch.link(ts(t1, t0, -1.0, 1.0, ALU.mult, ALU.add))
                ch.link(stt(kp[:, :, 0], t1, -FAR, nreg, ALU.mult, ALU.mult))
                ch.link(stt(kp[:, :, 1], t0, -FAR, nreg, ALU.mult, ALU.mult))
                V.memset(idle[:, 0:1], 0.0).then_inc(g["phase"], 1)

            dve.wait_ge(g["x_in"], 16)
            dve.wait_ge(g["tanh"], 2)
            dve.wait_ge(g["consts"], g["n_consts"])
            similarity()
            dve.wait_ge(g["att_in"], 16 * g["n_loads"])
            for name in run[1:]:
                if name == "l0f":
                    feed_forward()
                elif name == "l1x":
                    attention(L1X, 1)
                elif name == "l1f":
                    mixture("l1f", 1, NE)
                elif name == "l2x":
                    attention(L2X, 2)
                elif name == "l2f":
                    mixture("l2f", 2, NE + 2)
                elif name == "l3x":
                    attention(L3X, 3)
                elif name == "sim":
                    guide()
                else:
                    attention(L3F, 3)

        @block.scalar
        def _(act):
            A = nc.scalar.activation

            def copy(dst, src):
                return A(dst, src, ACT.Copy)

            def turned(name, n):
                act.wait_ge(g["xnT"], entries(name, n) + 1)
                copy(xt[:, :, :], bank[6][:, :].rearrange("p (c s) -> p c s", c=DC)).then_inc(g["xt"], 1)

            def similarity():
                with act.Fori(0, B) as n:
                    turned("l0x", n)
                    act.wait_ge(l0x["vt"], n + 1)
                    A(qT[0][:, 0, :], bank[0][:, 0:S], ACT.Identity, bias=b0v[:, 0:1]).then_inc(l0x["act"], 1)
                    A(qT[0][:, 1, :], bank[1][:, 0:S], ACT.Identity, bias=b0t[:, 0:1]).then_inc(l0x["act"], 1)
                    act.wait_ge(l0x["act"], n * 2 + 2)
                    A(kT[:, 0, :], qT[0][:, 0, :], ACT.Square)
                    A(kT[:, 1, :], qT[0][:, 1, :], ACT.Square).then_inc(l0x["vtc"], 1)

            def feed_forward():
                with act.Fori(0, B) as n:
                    turned("l0f", n)
                    for j in range(F0 // P):
                        act.wait_ge(l0f["h"], n * (F0 // P) + j + 1)
                        A(hid0[:, j, :], bank[j % 4][:, 0:S], ACT.Relu, bias=b01[:, j:j + 1]).then_inc(l0f["hc"], 1)

            def attention(s):
                m = ph[s.name]
                U = s.units
                vh = v[:, :, 0:NH * s.vs].rearrange("p t (h e) -> p t h e", h=NH)

                def front(n):
                    act.wait_ge(g["xnT"], entries(s.name, n) + 1)
                    copy(xt[:, :, :], bank[7][:, :].rearrange("p (c s) -> p c s", c=DC)).then_inc(g["xt"], 1)

                def projected(n):
                    for j in range(s.qjobs):
                        act.wait_ge(m["k"], n * s.kjobs + j + 1)
                        dst = kT[:, 2 * j:2 * j + 2, :]
                        src = bank[s.jobs[s.qjobs + j]][:, :].rearrange("p (k s) -> p k s", k=2)
                        if s.bias:
                            for k in range(2):
                                ins = A(dst[:, k, :], src[:, k, :], ACT.Identity, bias=bk3[:, 2 * j + k:2 * j + k + 1])
                        else:
                            ins = copy(dst, src)
                        ins.then_inc(m["kc"], 1)
                    if not s.bias:
                        for j in range(s.vjobs):
                            act.wait_ge(m["v"], n * s.vjobs + j + 1)
                            src = bank[s.jobs[2 * s.qjobs + j]]
                            if s.ones:
                                for t in range(T):
                                    ins = copy(vh[:, t, :, 0:s.d],
                                               src[:, t * D:(t + 1) * D].rearrange("p (h e) -> p h e", h=NH))
                            else:
                                ins = copy(v[:, j // 2, (j % 2) * 512:(j % 2 + 1) * 512], src[:, :])
                            ins.then_inc(m["vc"], 1)

                def gathered(n, f):
                    groups = s.groups + (1 if s.split else 0)
                    act.wait_ge(m["pv"], n * groups + 2 * f + 2)
                    copy(oTs[:, 2 * f:2 * f + 2, :], bank[5 + f % 2][:, :].rearrange("p (k s) -> p k s", k=2))\
                        .then_inc(m["oc"], 1)

                def heads(n, ahead):
                    nf = 0
                    for h in range(U + LAG + 2):
                        if h < U:
                            act.wait_ge(m["mx"], n * U + h + 1)
                            if h >= 3:
                                act.wait_ge(m["pT"], n * U + h - 2)
                        if h < NH:
                            src = (sc[h % 3] if s.clip else bank[h % 3])
                            for t in range(T):
                                kw = {} if s.ones else {"accum_out": esum[:, h, t:t + 1]}
                                ins = A(prob[h % 3][:, t * S:(t + 1) * S], src[:, t * S:(t + 1) * S], ACT.Exp,
                                        bias=nmax[:, h, t:t + 1], **kw)
                            ins.then_inc(m["e"], 1)
                        elif h < U:
                            A(prob[h % 3][0:NX, 0:S], bank[h % 3][0:NX, 0:S], ACT.Exp, bias=nmax[0:NX, h, 0:1])\
                                .then_inc(m["e"], 1)
                        if s.clip and LAG <= h < U + LAG:
                            k = h - LAG
                            act.wait_ge(m["pT"], n * U + k + 1)
                            if k >= 8:
                                act.wait_ge(m["pv"], n * s.groups + (k - 8) // s.per + 1)
                            copy(probT[k % 8][:, :], bank[3 + k % 2][:, :]).then_inc(m["pTc"], 1)
                        if h == FRONT + 1 and ahead:
                            front(n + 1)
                        if nf < s.fills and h == min((nf + 1) * 2 * s.per - 1 + LAG + 2, U + LAG + 1):
                            gathered(n, nf)
                            nf += 1
                    assert nf == s.fills

                def finish(n):
                    for t in range(T):
                        act.wait_ge(m["onT"], n * T + t + 1)
                        copy(oT[t][:, :, :], bank[3 + t][:, 0:DC * P].rearrange("p (c s) -> p c s", s=P))\
                            .then_inc(m["oT"], 1)

                if s.ones:
                    act.wait_ge(m["dve"], T)
                front(0)
                projected(0)
                with act.Fori(0, B - 1) as n:
                    heads(n, True)
                    projected(n + 1)
                    if s.ones and s.proj:
                        finish(n)
                heads(B - 1, False)
                if s.ones and s.proj:
                    finish(B - 1)

            def mixture(name, ne):
                m = moe[name]
                f = F1 if name == "l1f" else F2
                ft = -(-f // P)
                with act.Fori(0, B // 2) as j:
                    for b in range(2):
                        n = j * 2 + b
                        act.wait_ge(g["xnT"], entries(name, n) + 1)
                        copy(xtw[:, :, bass.ds(n * S, S)], bank[6 + b][:, :].rearrange("p (c s) -> p c s", c=DC))\
                            .then_inc(g["xt"], 1)
                act.wait_ge(m["gd"], 1)
                A(sel[:, :, :], sel[:, :, :], ACT.Exp).then_inc(m["ga"], 1)
                with act.Fori(0, ne // 2) as i:
                    for u in range(2):
                        for blk in range(NBLK):
                            blocks = (i * 2 + u) * NBLK + blk
                            for h in range(ft):
                                r = min(P, f - h * P)
                                act.wait_ge(m["a"], blocks * ft + h + 1)
                                if h >= 2:
                                    act.wait_ge(m["hid"], blocks * ft + h - 1)
                                A(sil[h % 2][0:r, :], bank[h % 2][0:r, :], ACT.Silu).then_inc(m["sil"], 1)

            def guide():
                with act.Fori(0, B) as n:
                    turned("sim", n)

            act.wait_ge(g["w0_in"], 16 * 6)
            A(tgx[:, :], gates_x[:, :], ACT.Tanh).then_inc(g["tanh"], 1)
            A(tgf[:, :], gates_f[:, :], ACT.Tanh).then_inc(g["tanh"], 1)
            similarity()
            act.wait_ge(g["att_in"], 16 * g["n_loads"])
            for name in run[1:]:
                if name == "l0f":
                    feed_forward()
                elif name in attn:
                    attention(attn[name])
                elif name == "l1f":
                    mixture("l1f", NE)
                elif name == "l2f":
                    mixture("l2f", NE + 2)
                else:
                    guide()

        @block.tensor
        def _(pe):
            mm, tr = nc.tensor.matmul, nc.tensor.transpose

            def mm3(out_, ab, cd, start, stop):
                (ah, al), (bh, bl) = ab, cd
                mm(out_, al, bh, start=start, stop=False)
                mm(out_, ah, bl, start=False, stop=False)
                return mm(out_, ah, bh, start=False, stop=stop)

            def turn(name, n, b=0):
                pe.wait_ge(g["xn"], entries(name, n) * T + T)
                for t in range(T):
                    for c in range(DC):
                        ins = tr(bank[6 + b][:, c * S + t * P:c * S + (t + 1) * P],
                                 xnb(b, t)[:, c * P:(c + 1) * P], ident[:, :])
                ins.then_inc(g["xnT"], 1)

            def similarity():
                with pe.Fori(0, B) as n:
                    turn("l0x", n)
                    pe.wait_ge(g["xt"], entries("l0x", n) + 1)
                    pe.wait_ge(l0x["ct"], n * 16 + 16)
                    for c in range(DC):
                        mm(bank[0][:, 0:S], w0v[:, c, :], xt[:, c, :], start=c == 0, stop=c == DC - 1)
                    for c in range(2):
                        ins = mm(bank[1][:, 0:S], w0t[:, c, :], ct[:, c, :], start=c == 0, stop=c == 1)
                    ins.then_inc(l0x["vt"], 1)
                    pe.wait_ge(l0x["vtc"], n + 1)
                    for t in range(T):
                        mm(bank[2][:, t * S:(t + 1) * S], qT[0][:, 0, t * P:(t + 1) * P], qT[0][:, 1, :], start=True, stop=True)
                    for k in range(2):
                        for t in range(T):
                            c = k * T + t
                            ins = mm(bank[4][:, c:c + 1], kT[:, k, t * P:(t + 1) * P], ones[:, 0:1], start=True, stop=True)
                    ins.then_inc(l0x["dots"], 1)
                    pe.wait_ge(l0x["dg"], n + 1)
                    for t in range(T):
                        ins = mm(bank[3][:, t * P:(t + 1) * P], ones[:, :], diag[:, t, :], start=True, stop=True)
                    ins.then_inc(l0x["rows"], 1)

            def feed_forward():
                nj = F0 // P
                with pe.Fori(0, B) as n:
                    turn("l0f", n)
                    pe.wait_ge(g["xt"], entries("l0f", n) + 1)
                    for j in range(nj):
                        if j >= 4:
                            pe.wait_ge(l0f["hc"], n * nj + j - 3)
                        for c in range(DC):
                            ins = mm(bank[j % 4][:, 0:S], w01[:, c, j * P:(j + 1) * P], xt[:, c, :],
                                     start=c == 0, stop=c == DC - 1)
                        ins.then_inc(l0f["h"], 1)
                    pe.wait_ge(l0f["hc"], n * nj + nj)
                    for t in range(T):
                        for j in range(nj):
                            ins = mm(bank[6 + t][:, 0:D], hid0[:, j, t * P:(t + 1) * P], w02[:, j, :],
                                     start=j == 0, stop=j == nj - 1)
                        ins.then_inc(l0f["y"], 1)

            def attention(s):
                m = ph[s.name]
                U = s.units
                groups = s.groups + (1 if s.split else 0)
                src = xt if s.split else ct
                w_q, w_k, w_v = wq[s.name], wk[s.name], wv[s.name]

                def front(n):
                    pe.wait_ge(g["xn"], entries(s.name, n) * T + T)
                    for t in range(T):
                        for c in range(DC):
                            ins = tr(bank[7][:, c * S + t * P:c * S + (t + 1) * P], xn[:, t, c * P:(c + 1) * P],
                                     ident[:, :])
                    ins.then_inc(g["xnT"], 1)
                    if s.split:
                        pe.wait_ge(m["cols"], n + 1)
                        pe.wait_ge(g["xt"], entries(s.name, n) + 1)
                        for k in range(2):
                            for t in range(T):
                                ins = mm(bank[7][0:2, k * S + t * P:k * S + (t + 1) * P],
                                         qk2[:, t, 2 * k:2 * k + 2], ident[:, :], start=True, stop=True)
                        ins.then_inc(m["mrow"], 1)

                def project(n):
                    pe.wait_ge(g["xt"], entries(s.name, n) + 1)
                    if s.split:
                        pe.wait_ge(m["mrowc"], n + 1)
                    else:
                        pe.wait_ge(m["ct"], n * 16 + 16)
                    for w, what, kt_, of, mk in ((w_q, "q", DC, xt, 0), (w_k, "k", s.kt, src, 1)):
                        for j in range(s.qjobs):
                            job = mk * s.qjobs + j
                            if job >= 7:
                                pe.wait_ge(m["qc"], n * s.qjobs + job - 6)
                            for k in range(2):
                                gr = 2 * j + k
                                dst = bank[s.jobs[job]][:, k * S:(k + 1) * S]
                                for c in range(kt_):
                                    ins = mm(dst, w[:, c, gr * P:(gr + 1) * P], of[:, c, :], start=c == 0,
                                             stop=c == kt_ - 1 and not s.split)
                                if s.split:
                                    ins = mm(dst, selw[:, :], mrow[:, mk, :], start=False, stop=True)
                            ins.then_inc(m[what], 1)
                    for j in range(s.vjobs):
                        job = 2 * s.qjobs + j
                        if s.ones:
                            parts = [(bank[s.jobs[job]][:, t * D:(t + 1) * D], t, 0, D) for t in range(T)]
                        else:
                            if job - 7 < s.qjobs:
                                pe.wait_ge(m["qc"], n * s.qjobs + job - 6)
                            else:
                                pe.wait_ge(m["kc"], n * s.qjobs + job - 6 - s.qjobs)
                            parts = [(bank[s.jobs[job]][:, :], j // 2, (j % 2) * 512, 512)]
                        for dst, t, c0, w in parts:
                            for c in range(s.kt):
                                ins = mm(dst, src[:, c, t * P:(t + 1) * P], w_v[:, c, c0:c0 + w],
                                         start=c == 0, stop=c == s.kt - 1)
                        ins.then_inc(m["v"], 1)

                def project_registers(n):
                    for gr in range(4):
                        dst = bank[7][:, gr * NREG:(gr + 1) * NREG]
                        for c in range(DC):
                            mm(dst, w_q[:, c, gr * P:(gr + 1) * P], xt[:, c, 0:NREG], start=c == 0, stop=False)
                        ins = mm(dst, selw[:, :], mregq[:, :], start=False, stop=True)
                    ins.then_inc(m["k"], 1)

                def scores(n, h):
                    if h >= 3:
                        pe.wait_ge(m["e"], n * U + h - 2)
                    if h == NH:
                        pe.wait_ge(m["xs"], n * 2 + 1)
                        for gr in range(4):
                            ins = mm(bank[h % 3][0:NX, 0:S], qx[:, gr, :], kT[:, gr, :], start=gr == 0, stop=gr == 3)
                    else:
                        gr = h // s.per
                        r0 = 64 * (h % s.per // (s.per // 2))
                        q = qT[h % 2 if s.ones else 0]
                        for t in range(T):
                            ins = mm(bank[h % 3][:, t * S:(t + 1) * S], q[r0:r0 + 64, gr, t * P:(t + 1) * P],
                                     kT[r0:r0 + 64, gr, :], start=True, stop=True)
                    ins.then_inc(m["s"], 1)

                def turn_probs(n, k):
                    pe.wait_ge(m["e" if s.ones else "pn"], n * U + k + 1)
                    if k >= 2:
                        pe.wait_ge(m["pTc"], n * U + k - 1)
                    for kt in range(T):
                        if k == NH:
                            ins = tr(bank[3 + k % 2][:, kt * NX:(kt + 1) * NX],
                                     prob[k % 3][0:NX, kt * P:(kt + 1) * P], ident[0:NX, 0:NX])
                        else:
                            for t in range(T):
                                c0 = (kt * T + t) * P
                                ins = tr(bank[3 + k % 2][:, c0:c0 + P],
                                         prob[k % 3][:, t * S + kt * P:t * S + (kt + 1) * P], ident[:, :])
                    ins.then_inc(m["pT"], 1)

                def values(n, gr, ahead):
                    if gr == s.groups:
                        pe.wait_ge(m["pTc"], (n + 1) * U)
                        if ahead:
                            pe.wait_ge(m["mrowc"], n + 2)
                        for kt in range(T):
                            ins = mm(bank[7][0:NX, 0:NH * s.vs], probT[NH % 8][:, kt * NX:(kt + 1) * NX],
                                     v[:, kt, 0:NH * s.vs], start=kt == 0, stop=kt == T - 1)
                        ins.then_inc(m["pv"], 1)
                        return
                    pe.wait_ge(m["pTc"], n * U + (gr + 1) * s.per)
                    if gr == 0:
                        pe.wait_ge(m["vc"], (n + 1) * s.vjobs)
                    if gr >= 4 and gr % 2 == 0:
                        pe.wait_ge(m["oc"], n * s.fills + gr // 2 - 1)
                    for kt in range(T):
                        for j in range(s.per):
                            h = gr * s.per + j
                            r0 = j * s.rows
                            ins = mm(bank[5 + gr // 2 % 2][r0:r0 + s.vs, gr % 2 * S:(gr % 2 + 1) * S],
                                     v[:, kt, h * s.vs:(h + 1) * s.vs], probT[h % 8][:, kt * S:(kt + 1) * S],
                                     start=kt == 0, stop=kt == T - 1)
                    ins.then_inc(m["pv"], 1)

                def heads(n, ahead):
                    pe.wait_ge(m["qc"], (n + 1) * s.qjobs)
                    pe.wait_ge(m["kc"], (n + 1) * s.qjobs)
                    if not s.ones:
                        pe.wait_ge(m["vc"], (n + 1) * s.vjobs)
                    gr = 0
                    for h in range(U + LAG + 1):
                        if h < U:
                            scores(n, h)
                        if LAG <= h < U + LAG:
                            turn_probs(n, h - LAG)
                        if h == FRONT + 1 and ahead:
                            front(n + 1)
                        while gr < groups and min((gr + 1) * s.per, U) - 1 + LAG + 1 <= h:
                            values(n, gr, ahead)
                            gr += 1
                    assert gr == groups

                def outputs(n):
                    if s.split:
                        pe.wait_ge(m["xs"], n * 2 + 2)
                        mm(bank[7][:, 0:D], rsel[0:NX, :], onx[0:NX, :], start=True, stop=True).then_inc(m["reg"], 1)
                    pe.wait_ge(m["oc"], (n + 1) * s.fills)
                    pe.wait_ge(m["pTc"], (n + 1) * U)
                    for t in range(T):
                        for gr in range(4):
                            ins = tr(bank[3 + t][:, gr * P:(gr + 1) * P], oTs[:, gr, t * P:(t + 1) * P], ident[:, :])
                        ins.then_inc(m["z"], 1)

                def finish(n):
                    if s.ones:
                        for t in range(T):
                            pe.wait_ge(m["on"], n * T + t + 1)
                            for c in range(DC):
                                ins = tr(bank[3 + t][:, c * P:(c + 1) * P], on[t][:, c * P:(c + 1) * P], ident[:, :])
                            ins.then_inc(m["onT"], 1)
                        for t in range(T):
                            pe.wait_ge(m["oT"], n * T + t + 1)
                            for c in range(DC):
                                ins = mm(bank[3 + t][:, S:2 * S], oT[t][:, c, :], wo[s.name][:, c, :],
                                         start=c == 0, stop=c == DC - 1)
                            ins.then_inc(m["y"], 1)
                    else:
                        pe.wait_ge(m["oc"], (n + 1) * s.fills)
                        for t in range(T):
                            for c in range(s.groups):
                                ins = mm(bank[7][:, t * S:(t + 1) * S], oTs[:, c, t * P:(t + 1) * P],
                                         wo[s.name][:, c, :], start=c == 0, stop=c == s.groups - 1)
                            ins.then_inc(m["y"], 1)

                pe.wait_ge(g["phase"], n_phase[s.name] - 1)
                if s is L3X:
                    pe.wait_ge(g["w3_in"], 16 * 3)
                if s is L2X:
                    pe.wait_ge(g["w2a_in"], 16 * 2)
                    pe.wait_ge(g["w2b_in"], 16 * 2)
                front(0)
                project(0)
                if s.split:
                    project_registers(0)
                with pe.Fori(0, B - 1) as n:
                    heads(n, True)
                    if s.ones:
                        outputs(n)
                    else:
                        pe.wait_ge(m["oc"], (n + 1) * s.fills)
                    project(n + 1)
                    if s.proj:
                        finish(n)
                    if s.split:
                        project_registers(n + 1)
                heads(B - 1, False)
                if s.ones:
                    outputs(B - 1)
                if s.proj:
                    finish(B - 1)

            def mixture(name, wg, ne):
                m = moe[name]
                f = F1 if name == "l1f" else F2
                ft = -(-f // P)
                with pe.Fori(0, B // 2) as j:
                    for b in range(2):
                        pe.wait_ge(g["xt"], entries(name, j * 2 + b) - 1)
                        turn(name, j * 2 + b, b)
                pe.wait_ge(g["xt"], entries(name, B))
                for t in range(NT):
                    for c in range(DC):
                        ins = mm(bank[0][:, t * NE:(t + 1) * NE], xtw[:, c, t * P:(t + 1) * P], wg[:, c, :],
                                 start=c == 0, stop=c == DC - 1)
                ins.then_inc(m["lg"], 1)
                pe.wait_ge(m["gd"], 1)

                def down(u, w3, blk, before):
                    pe.wait_ge(m["yc"], before + 1)
                    for k in range(4):
                        for h in range(ft):
                            r = min(P, f - h * P)
                            slot = ((u * NBLK + blk) * ft + h) % HS[name]
                            ins = mm3(bank[4 + k][:, 0:D],
                                      [t[slot][0:r, k * P:(k + 1) * P] for t in hid[name][0:2]],
                                      [w[0:r, h, :] for w in w3], h == 0, h == ft - 1)
                        ins.then_inc(m["y"], 1)

                with pe.Fori(0, ne // 2) as i:
                    for u in range(2):
                        w1, w2, w3 = zip(*expert(u, f))
                        pe.wait_ge(m["ws"], i * 2 + u + 1)
                        for blk in range(NBLK + 1):
                            blocks = (i * 2 + u) * NBLK + blk
                            if blk == NBLK:
                                pe.wait_ge(m["hid"], blocks * ft)
                                down(u, w3, blk - 1, 4 * (blocks - 1))
                                break
                            for h in range(ft):
                                if h == 1 and blk >= 1:
                                    pe.wait_ge(m["hid"], blocks * ft)
                                    down(u, w3, blk - 1, 4 * (blocks - 1))
                                r = min(P, f - h * P)
                                if h >= 2:
                                    pe.wait_ge(m["hid"], blocks * ft + h - 1)
                                elif blk >= 1:
                                    pe.wait_ge(m["hid"], blocks * ft + h - 1)
                                pe.wait_ge(m["xs"], blk + 1)
                                for k, w in ((0, w1), (2, w2)):
                                    for c in range(DC):
                                        ins = mm3(bank[k + h % 2][0:r, :], [t[:, c, h * P:h * P + r] for t in w],
                                                  [t[:, c, blk * 512:(blk + 1) * 512] for t in (xth, xtl)],
                                                  c == 0, c == DC - 1)
                                ins.then_inc(m["a"], 1)

            def guide():
                with pe.Fori(0, B) as n:
                    turn("sim", n)
                    pe.wait_ge(g["xt"], entries("sim", n) + 1)
                    for t in range(T):
                        for c in range(DC):
                            ins = mm(bank[t][:, 0:D], xt[:, c, t * P:(t + 1) * P], wqs[:, c, :],
                                     start=c == 0, stop=c == DC - 1)
                        ins.then_inc(sm["q"], 1)

            pe.wait_ge(g["consts"], g["n_consts"])
            pe.wait_ge(g["w0_in"], 16 * 6)
            similarity()
            pe.wait_ge(g["w0f_in"], 32)
            pe.wait_ge(g["att_in"], 16 * g["n_loads"])
            for name in run[1:]:
                if name == "l0f":
                    feed_forward()
                elif name in attn:
                    attention(attn[name])
                elif name == "l1f":
                    mixture("l1f", wg1, NE)
                elif name == "l2f":
                    mixture("l2f", wg2, NE + 2)
                else:
                    guide()


SIM_STEPS_BEFORE = 2 + B * (2 + T * 5 + 2) + 8


def kernel(**inputs):
    import numpy as np
    import concourse.bacc as bacc
    from concourse.bass_utils import run_bass_kernel_spmd

    def rows(w, k):
        return w.reshape(k, w.shape[0] // k, w.shape[1]).transpose(1, 0, 2)

    def heads32(w):
        r = np.zeros((w.shape[0], NH, 32), w.dtype)
        r[:, :, 0:16] = w.reshape(w.shape[0], NH, 16)
        return r.reshape(w.shape[0], NH * 32)

    def columns(b):
        return heads32(b.reshape(1, D)).reshape(4, P).T

    def per_expert(w1, w2, w3):
        f = w1.shape[0]
        ft = -(-f // P)
        down = np.zeros((ft * P, D), w1.dtype)
        down[0:f] = w3.T
        return np.concatenate([rows(w1.T, DC).reshape(P, -1), rows(w2.T, DC).reshape(P, -1),
                               rows(down, ft).reshape(P, -1)], axis=1)

    n = {k: np.asarray(v) for k, v in inputs.items()}
    wkv = n["L1_xattn_Wkv"].T
    qkv = n["L3_ffn_W_qkv"]
    we1 = np.stack([per_expert(n["L1_ffn_W1"][e], n["L1_ffn_W2"][e], n["L1_ffn_W3"][e]) for e in range(NE)])
    shared = [(n["L2_ffn_sw1"][F2 * e:F2 * e + F2], n["L2_ffn_sw3"][F2 * e:F2 * e + F2],
               n["L2_ffn_sw2"][:, F2 * e:F2 * e + F2]) for e in range(2)]
    we2 = np.stack([per_expert(n["L2_ffn_w1"][e], n["L2_ffn_w3"][e], n["L2_ffn_w2"][e]) for e in range(NE)]
                   + [per_expert(*t) for t in shared])
    arrays = {
        "x": n["x"],
        "ctxT": n["ctx_768"].reshape(B, S, 2, CK).transpose(0, 3, 2, 1),
        "mask": n["mask_BxS_bk0"].reshape(B * S),
        "g_xattn": n["g_xattn"], "g_ffn": n["g_ffn"],
        "w0v": rows(n["L0_xattn_Wv"].T, DC), "w0t": rows(n["L0_xattn_Wt"].T, 2),
        "b0v": n["L0_xattn_bv"].reshape(P, 1), "b0t": n["L0_xattn_bt"].reshape(P, 1),
        "w01": rows(n["L0_ffn_w1"][0], DC), "w02": rows(n["L0_ffn_w2"][0], F0 // P),
        "b01": n["L0_ffn_b1"][0].reshape(F0 // P, P).T, "b02": n["L0_ffn_b2"][0],
        "gamma": n["L0_ffn_gamma"], "beta": n["L0_ffn_beta"],
        "wq_l1x": rows(heads32(n["L1_xattn_Wq"].T), DC),
        "wk_l1x": rows(heads32(wkv[:, 0:D]), 2), "wv_l1x": rows(wkv[:, D:2 * D], 2),
        "wg1": rows(n["L1_ffn_Wg"].T, DC), "we1": we1,
        "wq_l2x": rows(n["L2_xattn_w_q"], DC), "wk_l2x": rows(n["L2_xattn_w_k"], 2),
        "wv_l2x": rows(n["L2_xattn_w_v"], 2), "wo_l2x": rows(n["L2_xattn_w_o"], 8), "bo_l2x": n["L2_xattn_b_o"],
        "wg2": rows(n["L2_ffn_gate_w"].T, DC), "gb2": n["L2_ffn_gate_bias"], "we2": we2,
        "wq_l3x": rows(heads32(n["L3_xattn_Wq"]), DC), "bq3": columns(n["L3_xattn_bq"]),
        "wk_l3x": rows(heads32(n["L3_xattn_Wk"]), 2), "bk3": columns(n["L3_xattn_bk"]),
        "wv_l3x": rows(n["L3_xattn_Wv"], 2), "bv3": n["L3_xattn_bv"],
        "wo_l3x": rows(n["L3_xattn_Wo"], DC), "bo_l3x": n["L3_xattn_bo"],
        "qg": n["L3_ffn_g_info"][0, 0],
        "wqs": rows(qkv[:, 0:D], DC), "wq_l3f": rows(heads32(qkv[:, 0:D]), DC),
        "wk_l3f": rows(heads32(qkv[:, D:2 * D]), DC), "wv_l3f": rows(qkv[:, 2 * D:3 * D], DC),
        "wo_l3f": rows(n["L3_ffn_W_proj"], DC), "bo_l3f": n["L3_ffn_b_proj"],
    }
    arrays = {k: np.ascontiguousarray(v) for k, v in arrays.items()}
    nc = bacc.Bacc("TRN2", target_bir_lowering=False, num_devices=1)
    aps = {k: nc.dram_tensor(f"in_{k}", v.shape, mybir.dt.from_np(v.dtype), kind="ExternalInput").ap()
           for k, v in arrays.items()}
    out = nc.dram_tensor("out", (B, S, D), F32, kind="ExternalOutput").ap()
    build(nc, aps, out)
    r = run_bass_kernel_spmd(nc, [{f"in_{k}": v for k, v in arrays.items()}], core_ids=[0])
    return r.results[0]["out"]
```

```python
from contextlib import ExitStack

import concourse.bass as bass
from concourse import mybir

F32 = mybir.dt.float32
U8 = mybir.dt.uint8
F32R = mybir.dt.float32r
ALU = mybir.AluOpType
ACT = mybir.ActivationFunctionType
AXX = mybir.AxisListType.X
RMAX = bass.bass_isa.ReduceOp.max

P = 128
B, S, D = 8, 256, 256
T = S // P
NT = B * T
DC = D // P
CTX, CK = 192, 96
NH = 16
HV = 128
F0 = 1024
F1 = 682
NBLK = NT * P // 512
HS = {"l1f": 8, "l2f": 4}
F1T = -(-F1 // P)
F2 = 256
NE = 8
NREG = 5
NX = NREG * NH
LN_EPS = 1e-5
COS_EPS = 1e-8
CLAMP = 10000.0
FAR = 1e30


FRONT = 5
LAG = 2


class Attn:

    def __init__(self, name, d, qscale, proj=False, bias=False, mask=False, clip=False, split=False):
        self.name, self.d, self.qscale = name, d, qscale
        self.proj, self.bias, self.mask, self.clip, self.split = proj, bias, mask, clip, split
        self.rows = 32 if d == 16 else 64
        self.per = P // self.rows
        self.groups = NH // self.per
        self.width = NH * d
        self.vs = d + 1 if d == 16 else d
        self.ones = self.vs > d
        self.kdim, self.kt = (P, DC) if split else (CK, 2)
        self.units = NH + (1 if split else 0)
        self.qjobs = self.groups // 2
        self.vjobs = T * self.width // 512
        self.kjobs = self.qjobs + (1 if split else 0)
        self.jobs = [0, 1, 2, 5, 6] if d == 16 else [j % 7 for j in range(12)]
        self.fills = self.groups // 2


L1X = Attn("l1x", 16, 0.25, mask=True)
L2X = Attn("l2x", 64, 0.125, proj=True, bias=False)
L3X = Attn("l3x", 16, 0.25, proj=True, bias=True, clip=True)
L3F = Attn("l3f", 16, 0.25, proj=True, split=True)


def expert_size(f):
    return 2 * DC * (f // P * P) + (DC * P if f % P else 0) + -(-f // P) * D


def hidden_rows(f, h):
    return slice(0, P) if (h + 1) * P <= f else slice(P // 2, P)


def steps(eng, step, chain=None, links=0):
    step(0, 0, True, False)
    with eng.Fori(0, B // 2 - 1) as j:
        if chain:
            chain.loop(j, 2 * links)
        for b in range(2):
            step(j * 2 + 1 + b, 1 - b, False, False)
    if chain:
        chain.leave(B // 2 - 1)
    step(B - 1, 1, False, True)


class Chain:

    def __init__(self, eng, sem):
        self.eng, self.sem, self.base, self.k, self.total = eng, sem, 0, 0, 0

    def loop(self, i, per):
        self.total = self.base = self.total + self.k
        self.base = self.total + i * per
        self.k, self.per = 0, per

    def leave(self, n):
        assert self.k == self.per, f"{self.sem}: {self.k} increments in the body, {self.per} said"
        self.total += n * self.per
        self.base, self.k = self.total, 0

    def link(self, ins):
        self.k += 1
        ins.then_inc(self.sem, 1)
        self.eng.wait_ge(self.sem, self.base + self.k)


def build(nc, a, out, layers=8):
    ctx = ExitStack()
    with ctx:
        def sb(name, shape, dt=F32):
            return ctx.enter_context(nc.sbuf_tensor(name, shape, dt))

        def under(name, shape, dt=F32):
            with nc.sbuf_tensor(name, shape, dt) as t:
                return t

        def sem(name):
            return ctx.enter_context(nc.semaphore(name))

        bank = [ctx.enter_context(nc.psum_tensor(f"bank{k}", [P, 512], F32)) for k in range(8)]

        x = sb("x", [P, NT, D])
        ident = sb("ident", [P, P])
        ones = sb("ones", [P, P])
        gates_x = sb("gates_x", [P, 4])
        gates_f = sb("gates_f", [P, 4])
        tgx = sb("tgx", [P, 4])
        tgf = sb("tgf", [P, 4])
        mask_u8 = sb("mask_u8", [P, B * S], U8)
        w0v = sb("w0v", [P, DC, HV]); w0t = sb("w0t", [CK, 2, HV])
        b0v = sb("b0v", [P, 1]); b0t = sb("b0t", [P, 1])
        n1q, n1k, n1v = DC * L1X.groups * P, L1X.kt * L1X.groups * P, L1X.kt * L1X.width
        w13 = under("w13", [P, n1q + n1k + n1v])
        rows13 = sb("rows13", [P, n1q + n1k + n1v], F32R)
        wq = {"l1x": w13[:, 0:n1q].rearrange("p (c f) -> p c f", c=DC), "l3f": sb("wq_l3f", [P, DC, L3F.groups * P])}
        wk = {"l1x": w13[0:L1X.kdim, n1q:n1q + n1k].rearrange("p (c f) -> p c f", c=L1X.kt),
              "l3f": sb("wk_l3f", [L3F.kdim, L3F.kt, L3F.groups * P])}
        wv = {"l1x": w13[0:L1X.kdim, n1q + n1k:n1q + n1k + n1v].rearrange("p (c f) -> p c f", c=L1X.kt),
              "l3f": sb("wv_l3f", [L3F.kdim, L3F.kt, L3F.width])}
        for w in (wq, wk, wv):
            w["l3x"] = w["l1x"]
        wo = {s.name: sb(f"wo_{s.name}", [P, s.width // P, D]) for s in (L3X, L3F)}
        bo = {s.name: sb(f"bo_{s.name}", [P, D]) for s in (L2X, L3X, L3F)}
        bq3 = sb("bq3", [P, 4]); bk3 = sb("bk3", [P, 4]); bv3 = sb("bv3", [P, D])
        b01 = sb("b01", [P, F0 // P]); b02 = sb("b02", [P, D])
        gam = sb("gam", [P, D]); bet = sb("bet", [P, D])
        wg1 = sb("wg1", [P, DC, NE]); wg2 = sb("wg2", [P, DC, NE]); gb2 = sb("gb2", [P, NE])
        wqs = sb("wqs", [P, DC, D]); qg = sb("qg", [P, D])
        EW = expert_size(F1)
        ew = under("ew", [P, 2, EW])
        ewl = sb("ewl", [P, 2, EW], F32R)
        w2 = under("w2", [P, 2, EW])
        ewh = sb("ewh", [P, 2, EW], F32R)
        n2q, n2k = DC * L2X.groups * P, L2X.kt * L2X.groups * P
        n2v, n2o = L2X.kt * L2X.width, L2X.width // P * D
        wq["l2x"] = w2[:, 0, 0:n2q].rearrange("p (c f) -> p c f", c=DC)
        wk["l2x"] = w2[0:L2X.kdim, 0, n2q:n2q + n2k].rearrange("p (c f) -> p c f", c=L2X.kt)
        wv["l2x"] = w2[0:L2X.kdim, 1, 0:n2v].rearrange("p (c f) -> p c f", c=L2X.kt)
        wo["l2x"] = w2[:, 1, n2v:n2v + n2o].rearrange("p (c f) -> p c f", c=L2X.width // P)
        w01 = ew[:, 0, 0:DC * F0 // 2 * 2].rearrange("p (c f) -> p c f", c=DC)
        w02 = ew[:, 1, 0:F0 // P * D].rearrange("p (c f) -> p c f", c=F0 // P)

        def expert(u, f):
            full, part = f // P * P, DC * P if f % P else 0
            n, cuts = DC * full, []
            for e in (ewh, ewl):
                cuts.append((e[:, u, 0:n].rearrange("p (c f) -> p c f", c=DC),
                             e[:, u, n:2 * n].rearrange("p (c f) -> p c f", c=DC),
                             e[:, u, 2 * n:2 * n + part].rearrange("p (c f) -> p c f", c=DC) if part else None,
                             e[:, u, 2 * n + part:expert_size(f)].rearrange("p (c f) -> p c f", c=-(-f // P))))
            return cuts

        xn = sb("xn", [P, T, D])
        xt = sb("xt", [P, DC, S])
        ct = sb("ct", [CK, 2, S])
        bst = sb("bst", [P, T, 6]); mv = sb("mv", [P, T, 2]); rstd = sb("rstd", [P, T])
        ARENA = 16 * S + T * NH * 64 + (3 + 8) * 512 + 8 * S
        arena = under("arena", [P, ARENA])
        split = sb("split", [P, ARENA], F32R)
        o = [0]

        def cut(n):
            o[0] += n
            return arena[:, o[0] - n:o[0]]

        q8 = cut(8 * S).rearrange("p (g s) -> p g s", g=8)
        qT = [q8, q8[:, 4:8, :]]
        kT = cut(8 * S).rearrange("p (g s) -> p g s", g=8)
        v = cut(T * NH * 64).rearrange("p (t n) -> p t n", t=T)
        prob = [cut(512) for _ in range(3)]
        probT = [cut(512) for _ in range(8)]
        oTs = cut(8 * S).rearrange("p (g s) -> p g s", g=8)
        on = [sb(f"on{t}", [P, D]) for t in range(T)]
        oT = [sb(f"oT{t}", [P, DC, P]) for t in range(T)]
        xt2 = arena[:, ARENA - DC * S:ARENA].rearrange("p (c s) -> p c s", c=DC)
        xtb = [xt, xt2]
        sq = [arena[:, k * 512:(k + 1) * 512] for k in range(2)]
        gprod = arena[:, 1024:1536]
        ssq, ssg, inv, inv2 = (arena[:, 2048 + k * NT * NH:2048 + (k + 1) * NT * NH] for k in range(4))
        hid0 = arena[:, 0:F0 // P * S].rearrange("p (c s) -> p c s", s=S)
        n_xt = DC * NT * P
        xth, xtl, xtw = (t[:, c:c + n_xt].rearrange("p (c s) -> p c s", c=DC)
                         for t, c in ((split, 0), (split, n_xt), (arena, n_xt)))
        tiles = [(split, arena, c) for c in range(2 * n_xt, ARENA - 511, 512)]
        tiles += [(rows13, w13, k * 512) for k in range(2 * HS["l1f"] - len(tiles))]
        hid = {}
        for n, hs in HS.items():
            high, low, whole = ([t[k][:, t[2]:t[2] + 512] for t in tiles[c:c + hs]]
                                for k, c in ((0, 0), (0, hs), (1, hs)))
            hid[n] = (high, low, whole)
        assert o[0] <= ARENA, (o[0], ARENA)
        scr = sb("scr", [P, NT * NE * NE])
        sil = [sb(f"sil{k}", [P, 512]) for k in range(2)]
        sc = sil + [scr[:, 512:1024]]
        evens = sb("evens", [P, 2])
        even = sb("even", [P, 2])
        tmp = scr[:, 0:D]
        z = scr[:, D:2 * D]
        nmax = sb("nmax", [P, NH + 1, T])
        esum = sb("esum", [P, NH, T])
        rec = sb("rec", [P, NH])
        recs = sb("recs", [P, T, NH])
        idle = sb("idle", [P, 3])
        pidle = sb("pidle", [P, 1])
        norms = sb("norms", [P, 2 * T])
        diag = probT[0][:, 0:T * P].rearrange("p (t q) -> p t q", t=T)
        mhalf = sb("mhalf", [P, 2 * NH]); minus1 = sb("minus1", [P, T])
        gate = sb("gate", [P, NT, 10])
        lg = sb("lg", [P, NT, NE]); sel = sb("sel", [P, NT, NE]); gm = sb("gm", [P, NT])
        larger = sb("larger", [P, NT, NE])
        bsta = sb("bsta", [P, NT, 6]); mva = sb("mva", [P, NT, 2]); rstda = sb("rstda", [P, NT])
        tri = sb("tri", [P, NE, NE])
        sim = sb("sim", [P, NT]); regm = sb("regm", [P, NT]); ss = sb("ss", [P, 4 * NH])
        qp = sb("qp", [P, NT, 2]); kp = sb("kp", [P, NT, 2]); qk2 = sb("qk2", [P, T, 4])
        mrow = sb("mrow", [P, 2, S]); mregq = sb("mregq", [P, NREG]); selw = sb("selw", [P, P])
        qxs = sb("qxs", [P, 4 * NREG]); qx = sb("qx", [P, 4, NX])
        hm = sb("hm", [P, 4, NH]); bm = sb("bm", [P, NH]); rsel = sb("rsel", [P, P]); wcol = sb("wcol", [P, 1])
        onx = sb("onx", [P, D])

        def xnb(b, t):
            return xn[:, t, :] if b == 0 else on[t][:, :]

        names = ("x_in", "w0_in", "w0f_in", "att_in", "consts", "tanh", "phase", "out_done", "w3_in", "w2a_in", "w2b_in",
                 "xn", "xnT", "xt", "rq", "rd")
        g = {n: sem(n) for n in names}

        def group(p, *ns):
            return {n: sem(f"{p}_{n}") for n in ns}

        ph = {}
        for s in (L1X, L2X, L3X, L3F):
            ph[s.name] = group(s.name, "ct", "q", "k", "v", "qc", "kc", "vc", "s", "mx", "e", "pT", "pTc", "pv",
                               "oc", "dve",
                               *(("y", "yr") if s.proj else ()),
                               *(("z",) if s.ones else ("pn", "psum")),
                               *(("on", "onT", "oT") if s.ones and s.proj else ()),
                               *(("cols", "mrow", "mrowc", "xs", "reg") if s.split else ()))
        l0x = group("l0x", "fin", "ct", "vt", "vtc", "dots", "dg", "rows", "dve")
        l0f = group("l0f", "yc", "h", "hc", "y", "dve")
        moe = {}
        for n in ("l1f", "l2f"):
            moe[n] = group(n, "lg", "lr", "gd", "ga", "w0", "w1", "wh", "ws", "xh", "xs",
                           "a", "sil", "prod", "hid", "y", "yc", "dve")
        sm = group("sim", "q", "sq", "qc", "prod", "sums", "sqrt", "dve", "pool")

        block = ctx.enter_context(nc.Block())
        n_phase = {"l0x": 1, "l0f": 2, "l1x": 3, "l1f": 4, "l2x": 5, "l2f": 6, "l3x": 7, "sim": 8, "l3f": 9}
        order = [["l0x"], ["l0f"], ["l1x"], ["l1f"], ["l2x"], ["l2f"], ["l3x"], ["sim", "l3f"]]
        run = [n for l in order[:layers] for n in l]
        attn = {s.name: s for s in (L1X, L2X, L3X, L3F)}

        asked, requests = {}, 0
        for n, one in (("l0x", 1 + B), ("l0f", 1 + B), ("l1x", B), ("l1f", 1), ("l2x", B), ("l2f", 1), ("l3x", B),
                       ("sim", 2), ("l3f", B)):
            asked[n] = requests
            requests += one
        for n, m in (("l0x", l0x), ("l0f", l0f), ("sim", sm), *ph.items(), *moe.items()):
            m["asked"] = asked[n]

        def entries(name, n):
            return n + (n_phase[name] - 1) * B

        @block.sync
        def _(sp):
            sp.dma_start(x[:, :, :], a["x"].rearrange("b (t p) d -> p (b t) d", p=P)).then_inc(g["x_in"], 16)
            for dst, src in ((w0v[:, :, :], a["w0v"]), (w0t[:, :, :], a["w0t"]), (b0v[:, :], a["b0v"]),
                             (b0t[:, :], a["b0t"]), (gates_x[:, :], a["g_xattn"].partition_broadcast(P)),
                             (gates_f[:, :], a["g_ffn"].partition_broadcast(P))):
                sp.dma_start(dst, src).then_inc(g["w0_in"], 16)

            def contexts(name, sem_in, sem_used, per):
                if n_phase[name] > 1:
                    sp.wait_ge(g["phase"], n_phase[name] - 1)
                sp.dma_start(ct[:, :, :], a["ctxT"][0, :, :, :]).then_inc(sem_in, 16)
                with sp.Fori(1, B) as n:
                    sp.wait_ge(sem_used, n * per)
                    sp.dma_start(ct[:, :, :], a["ctxT"][n, :, :, :]).then_inc(sem_in, 16)

            contexts("l0x", l0x["ct"], l0x["vt"], 1)
            def first_experts(name, f, src):
                sp.wait_ge(g["phase"], 2 if name == "l1f" else 4)
                for u in range(2):
                    sp.dma_start(ew[:, u, 0:expert_size(f)], src[u, :, :]).then_inc(moe[name][f"w{u}"], 16)

            def more_experts(name, f, src, ne):
                with sp.Fori(1, ne // 2) as i:
                    for u in range(2):
                        sp.wait_ge(moe[name]["y"], (i * 2 + u - 1) * NT)
                        sp.dma_start(ew[:, u, 0:expert_size(f)], src[i * 2 + u, :, :])\
                            .then_inc(moe[name][f"w{u}"], 16)

            if "l1f" in run:
                first_experts("l1f", F1, a["we1"])
            if "l1x" in run:
                contexts("l1x", ph["l1x"]["ct"], ph["l1x"]["v"], L1X.vjobs)
            if "l1f" in run:
                more_experts("l1f", F1, a["we1"], NE)
            if "l2f" in run:
                first_experts("l2f", F2, a["we2"])
            if "l2x" in run:
                contexts("l2x", ph["l2x"]["ct"], ph["l2x"]["v"], L2X.vjobs)
            if "l2f" in run:
                more_experts("l2f", F2, a["we2"], NE + 2)
            if "l3x" in run:
                contexts("l3x", ph["l3x"]["ct"], ph["l3x"]["v"], L3X.vjobs)
            sp.wait_ge(g["phase"], len(run))
            sp.dma_start(out.rearrange("b (t p) d -> p (b t) d", p=P), x[:, :, :]).then_inc(g["out_done"], 16)
            sp.wait_ge(g["out_done"], 16)

        @block.gpsimd
        def _(pool):
            nc.gpsimd.memset(ident[:, :], 0.0).then_inc(g["consts"], 1)
            nc.gpsimd.memset(ones[:, :], 1.0).then_inc(g["consts"], 1)
            nc.gpsimd.memset(tri[:, :, :], 1.0).then_inc(g["consts"], 1)
            nc.gpsimd.memset(regm[:, :], 0.0).then_inc(g["consts"], 1)
            nc.gpsimd.memset(mrow[:, :, :], 0.0).then_inc(g["consts"], 1)
            nc.gpsimd.memset(mregq[:, :], 0.0).then_inc(g["consts"], 1)
            nc.gpsimd.memset(selw[:, :], 0.0).then_inc(g["consts"], 1)
            nc.gpsimd.memset(hm[:, :, :], 0.0).then_inc(g["consts"], 1)
            nc.gpsimd.memset(bm[:, :], 0.0).then_inc(g["consts"], 1)
            nc.gpsimd.memset(rsel[:, :], 0.5).then_inc(g["consts"], 1)
            nc.gpsimd.memset(wcol[:, :], 1.0).then_inc(g["consts"], 1)
            nc.gpsimd.memset(mhalf[:, :], -0.5).then_inc(g["consts"], 1)
            nc.gpsimd.memset(even[:, :], 0.0).then_inc(g["consts"], 1)
            nc.gpsimd.memset(minus1[:, :], -1.0).then_inc(g["consts"], 1)
            pool.wait_ge(g["consts"], 14)
            for k in range(2):
                for base in (0, 64):
                    r0 = base + 32 * k
                    nc.gpsimd.memset(even[r0:r0 + 32, k:k + 1], 1.0).then_inc(g["consts"], 1)
            done = [18]

            def select(t, fill, base, pattern, cm, op=ALU.not_equal):
                pool.wait_ge(g["consts"], done[0])
                nc.gpsimd.affine_select(out=t, in_=t, compare_op=op, fill=fill, base=base,
                                        pattern=pattern, channel_multiplier=cm).then_inc(g["consts"], 1)
                done[0] += 1

            select(ident[:, :], 1.0, 0, [[-1, P]], 1)
            select(tri[:, :, :], 0.0, 0, [[1, NE], [-1, NE]], 0, ALU.is_gt)
            reg = regm[:, :].rearrange("p (b t) -> p b t", t=T)[:, :, 0:1]
            select(reg, 1.0, -NREG, [[0, B], [0, 1]], 1, ALU.is_ge)
            select(mregq[:, :], 1.0, -1, [[0, NREG]], 1)
            select(selw[:, :].rearrange("p (h r) -> p h r", r=32), 1.0, -16, [[0, 4], [1, 32]], -1)
            select(selw[:, :], 0.0, 1, [[0, P]], -1, ALU.is_ge)
            pool.wait_ge(g["consts"], done[0])
            nc.gpsimd.memset(hm[:, :, :], 1.0).then_inc(g["consts"], 1)
            done[0] += 1
            select(hm[:, :, :], 0.0, 0, [[128, 4], [-32, NH]], 1, ALU.is_ge)
            select(hm[:, :, :], 0.0, 31, [[-128, 4], [32, NH]], -1, ALU.is_ge)
            for r in range(NREG):
                select(bm[:, :], 1.0, -NH * r, [[-1, NH]], 1)
            select(rsel[:, :], 0.0, 0, [[-NH, P]], 1, ALU.is_ge)
            select(rsel[:, :], 0.0, NH - 1, [[NH, P]], -1, ALU.is_ge)
            select(wcol[:, :], 0.5, -NREG, [[0, 1]], 1, ALU.is_ge)
            g["n_consts"] = done[0]

            pool.dma_start(w01, a["w01"]).then_inc(g["w0f_in"], 16)
            pool.dma_start(w02, a["w02"]).then_inc(g["w0f_in"], 16)
            loads = [(b01[:, :], a["b01"]), (b02[:, :], a["b02"].partition_broadcast(P)),
                     (gam[:, :], a["gamma"].partition_broadcast(P)), (bet[:, :], a["beta"].partition_broadcast(P)),
                     (mask_u8[:, :], a["mask"].partition_broadcast(P))]
            for s in (L1X, L2X, L3X, L3F):
                qkv = [(wq[s.name][:, :, :], a[f"wq_{s.name}"]), (wk[s.name][:, :, :], a[f"wk_{s.name}"]),
                       (wv[s.name][:, :, :], a[f"wv_{s.name}"])]
                if s is L3X:
                    later = qkv
                elif s is L2X:
                    later2 = qkv + [(wo["l2x"], a["wo_l2x"])]
                    loads += [(bo["l2x"][:, :], a["bo_l2x"].partition_broadcast(P))]
                    continue
                else:
                    loads += qkv
                if s.proj:
                    loads += [(wo[s.name][:, :, :], a[f"wo_{s.name}"]),
                              (bo[s.name][:, :], a[f"bo_{s.name}"].partition_broadcast(P))]
            loads += [(bq3[:, :], a["bq3"]), (bk3[:, :], a["bk3"]), (bv3[:, :], a["bv3"].partition_broadcast(P)),
                      (wg1[:, :, :], a["wg1"]), (wg2[:, :, :], a["wg2"]), (gb2[:, :], a["gb2"].partition_broadcast(P)),
                      (wqs[:, :, :], a["wqs"]), (qg[:, :], a["qg"].partition_broadcast(P))]
            for dst, src in loads:
                pool.dma_start(dst, src).then_inc(g["att_in"], 16)
            g["n_loads"] = len(loads)

            def root(m, k, out_, in_, power):
                pool.wait_ge(g["rq"], m["asked"] + k)
                nc.gpsimd.tensor_tensor(out_, in_, power, ALU.pow).then_inc(g["rd"], 1)

            for name in run:
                if name == "l0x":
                    root(l0x, 1, rstda[:, :], rstda[:, :], mhalf[:, 0:NT])
                    with pool.Fori(0, B) as n:
                        root(l0x, n + 2, norms[:, :], norms[:, :], mhalf[:, 0:2 * T])
                elif name == "l0f":
                    root(l0f, 1, rstda[:, :], rstda[:, :], mhalf[:, 0:NT])
                    with pool.Fori(0, B) as n:
                        root(l0f, n + 2, rstd[:, :], rstd[:, :], mhalf[:, 0:T])
                elif name == "sim":
                    root(sm, 1, rstda[:, :], rstda[:, :], mhalf[:, 0:NT])
                    root(sm, 2, ss[:, 0:NH], ss[:, 0:NH], mhalf[:, 0:NH])
                    pool.wait_ge(sm["dve"], SIM_STEPS_BEFORE)
                    nc.gpsimd.partition_all_reduce(ss[:, 2:4], ss[:, 0:2], P, RMAX).then_inc(sm["pool"], 1)
                else:
                    m = ph[name] if name in ph else moe[name]
                    if name in moe:
                        ne, f = (NE, F1) if name == "l1f" else (NE + 2, F2)
                        size = expert_size(f)
                        def split_weights(u, expert_no, rounds):
                            pool.wait_ge(m[f"w{u}"], rounds * 16)
                            w, wl, wh = (t[:, u, 0:size] for t in (ew, ewl, ewh))
                            nc.gpsimd.tensor_tensor(pidle[:, :], minus1[:, 0:1], minus1[:, 0:1], ALU.mult)
                            nc.gpsimd.tensor_copy(wh, w).then_inc(m["wh"], 1)
                            pool.wait_ge(m["wh"], expert_no + 1)
                            nc.gpsimd.tensor_tensor(wl, w, wh, ALU.subtract).then_inc(m["ws"], 1)

                        if name == "l1f":
                            split_weights(0, 0, 1)
                        root(m, 1, rstda[:, :], rstda[:, :], mhalf[:, 0:NT])
                        if name == "l2f":
                            split_weights(0, 0, 1)
                        for c in range(NBLK):
                            pool.wait_ge(m["xh"], c + 1)
                            if c == 0:
                                pool.wait_ge(m["lg"], 1)
                            cols = slice(c * 512, c * 512 + 512)
                            nc.gpsimd.tensor_tensor(xtl[:, :, cols], xtw[:, :, cols], xth[:, :, cols],
                                                    ALU.subtract).then_inc(m["xs"], 1)
                        with pool.Fori(0, ne // 2 - 1) as i:
                            split_weights(1, i * 2 + 1, i + 1)
                            split_weights(0, i * 2 + 2, i + 2)
                        split_weights(1, ne - 1, ne // 2)
                        if name == "l1f":
                            for sem_, y, pairs in (("w2a_in", (NE - 1) * NT, later2[0:2]),
                                                   ("w2b_in", NE * NT, later2[2:4]), ("w3_in", NE * NT, later)):
                                pool.wait_ge(m["y"], y)
                                for dst, src in pairs:
                                    pool.dma_start(dst, src).then_inc(g[sem_], 16)
                        continue
                    if name != "l2x":
                        with pool.Fori(0, B) as n:
                            root(m, n + 1, rstd[:, :], rstd[:, :], mhalf[:, 0:T])
                        continue

                    def normalise(n, ahead):
                        for h in range(NH):
                            pool.wait_ge(m["e"], n * NH + h + 1)
                            nc.gpsimd.tensor_tensor(esum[:, h, :], esum[:, h, :], minus1[:, 0:T], ALU.pow)\
                                .then_inc(m["psum"], 1)
                            pool.wait_ge(m["psum"], n * NH + h + 1)
                            p3 = prob[h % 3].rearrange("p (t k) -> p t k", t=T)
                            nc.gpsimd.tensor_tensor(p3, p3, esum[:, h, :].rearrange("p (t o) -> p t o", o=1)
                                                    .broadcast_to([P, T, S]), ALU.mult).then_inc(m["pn"], 1)
                            if h == 0 and ahead:
                                root(m, n + 2, rstd[:, :], rstd[:, :], mhalf[:, 0:T])

                    root(m, 1, rstd[:, :], rstd[:, :], mhalf[:, 0:T])
                    with pool.Fori(0, B - 1) as n:
                        normalise(n, True)
                    normalise(B - 1, False)

        @block.vector
        def _(dve):
            V = nc.vector
            stt, ts, tt = V.scalar_tensor_tensor, V.tensor_scalar, V.tensor_tensor

            def root(m, k, ins):
                ins.then_inc(g["rq"], 1)
                dve.wait_ge(g["rd"], m["asked"] + k)

            def stats(ch, m, k, srcs):
                for t, src in enumerate(srcs):
                    ins = V.bn_stats(bst[:, t, :], src)
                ch.link(ins)
                V.memset(idle[:, 0:1], 0.0)
                for t in range(T):
                    ins = V.bn_aggr(mv[:, t, :], bst[:, t, :])
                ch.link(ins)
                root(m, k, ts(rstd[:, :], mv[:, :, 1], LN_EPS, None, ALU.add))

            LN = 2

            def stats_of(n):
                for t in range(T):
                    ins = V.bn_stats(bsta[:, n * T + t, :], x[:, n * T + t, :])
                return ins

            def all_stats(ch, m, first=B - 1):
                for n in range(first, B):
                    ins = stats_of(n)
                ch.link(ins)
                V.memset(idle[:, 0:1], 0.0)
                for t in range(NT):
                    ins = V.bn_aggr(mva[:, t, :], bsta[:, t, :])
                ch.link(ins)
                root(m, 1, ts(rstda[:, :], mva[:, :, 1], LN_EPS, None, ALU.add))

            def normalise(n, b):
                for t in range(T):
                    r = bass.ds(n * T + t, 1)
                    ts(xnb(b, t), x[:, n * T + t, :], mva[:, r, 0], rstda[:, r],
                       ALU.subtract, ALU.mult).then_inc(g["xn"], 1)

            def add_to_x(n, t, branch, scalar):
                return stt(x[:, n * T + t, :], branch, scalar, x[:, n * T + t, :], ALU.mult, ALU.add)

            def similarity():
                ch = Chain(dve, l0x["dve"])
                all_stats(ch, l0x, 0)
                V.memset(idle[:, 2:3], 0.0).then_inc(l0x["fin"], 1)
                normalise(0, 0)

                def finish(n, b):
                    dve.wait_ge(l0x["rows"], n + 1)
                    for t in range(T):
                        ch.link(ts(tmp, bank[5][:, 0:S], norms[:, t:t + 1], 1.0 / COS_EPS, ALU.mult, ALU.min))
                        ch.link(tt(tmp, bank[2 + b][:, t * S:(t + 1) * S], tmp, ALU.mult))
                        ch.link(add_to_x(n, t, tmp, tgx[:, 0:1]))
                    V.memset(idle[:, 1:2], 0.0).then_inc(l0x["fin"], 1)

                def step(n, b, first, last):
                    if not last:
                        if not first:
                            dve.wait_ge(g["xnT"], n)
                        normalise(n + 1, 1 - b)
                    if not first:
                        finish(n - 1, 1 - b)
                    dve.wait_ge(l0x["dots"], n + 1)
                    root(l0x, n + 2, V.tensor_copy(norms[:, :], bank[4][:, 0:2 * T]))
                    ch.link(ts(norms[:, :], norms[:, :], FAR, None, ALU.min))
                    for t in range(T):
                        ins = ts(diag[:, t, :], ident[:, :], norms[:, T + t:T + t + 1], None, ALU.mult)
                    ins.then_inc(l0x["dg"], 1)

                steps(dve, step, ch, 1 + 3 * T)
                finish(B - 1, 1)
                V.memset(idle[:, 0:1], 0.0).then_inc(g["phase"], 1)

            def feed_forward():
                ch = Chain(dve, l0f["dve"])
                all_stats(ch, l0f, 0)
                normalise(0, 0)

                def step(n, b, first, last):
                    if not last:
                        dve.wait_ge(g["xnT"], entries("l0f", n))
                        normalise(n + 1, 1 - b)
                    zs = [scr[:, (1 + t) * D:(2 + t) * D] for t in range(T)]
                    for t in range(T):
                        dve.wait_ge(l0f["y"], n * T + t + 1)
                        ch.link(tt(zs[t], bank[6 + t][:, 0:D], b02[:, :], ALU.add))
                        ch.link(tt(zs[t], zs[t], xnb(b, t), ALU.add))
                    V.memset(idle[:, 1:2], 0.0).then_inc(l0f["yc"], 1)
                    stats(ch, l0f, n + 2, zs)
                    for t in range(T):
                        ch.link(ts(zs[t], zs[t], mv[:, t, 0:1], rstd[:, t:t + 1], ALU.subtract, ALU.mult))
                        ch.link(tt(zs[t], zs[t], gam[:, :], ALU.mult))
                        ch.link(tt(zs[t], zs[t], bet[:, :], ALU.add))
                        ch.link(add_to_x(n, t, zs[t], tgf[:, 0:1]))

                steps(dve, step, ch, 2 + 6 * T)
                V.memset(idle[:, 0:1], 0.0).then_inc(g["phase"], 1)

            def attention(s, gi):
                m = ph[s.name]
                ch = Chain(dve, m["dve"])
                U = s.units
                groups = s.groups + (1 if s.split else 0)
                vh = v[:, :, 0:NH * s.vs].rearrange("p t (h e) -> p t h e", h=NH)
                if s.ones:
                    for t in range(T):
                        ch.link(V.memset(vh[:, t, :, s.d:s.d + 1], 1.0))

                def statistics(n):
                    for t in range(T):
                        ins = V.bn_stats(bst[:, t, :], x[:, n * T + t, :])
                    ch.link(ins)
                    V.memset(idle[:, 0:1], 0.0)
                    for t in range(T):
                        ins = V.bn_aggr(mv[:, t, :], bst[:, t, :])
                    ch.link(ins)
                    ts(rstd[:, :], mv[:, :, 1], LN_EPS, None, ALU.add).then_inc(g["rq"], 1)

                def front(n):
                    dve.wait_ge(g["rd"], m["asked"] + n + 1)
                    dve.wait_ge(g["xnT"], entries(s.name, n))
                    for t in range(T):
                        ts(xn[:, t, :], x[:, n * T + t, :], mv[:, t, 0:1], rstd[:, t:t + 1],
                           ALU.subtract, ALU.mult).then_inc(g["xn"], 1)
                    if s.split:
                        V.tensor_copy(qk2[:, :, 0:2], qp[:, bass.ds(n * T, T), :])
                        V.tensor_copy(qk2[:, :, 2:4], kp[:, bass.ds(n * T, T), :]).then_inc(m["cols"], 1)

                def mask_rows(n):
                    if s.split:
                        dve.wait_ge(m["mrow"], n + 1)
                        V.tensor_copy(mrow[0:2, :, :], bank[7][0:2, :].rearrange("p (k s) -> p k s", k=2))\
                            .then_inc(m["mrowc"], 1)

                def projected(n):
                    for j in range(s.qjobs):
                        dve.wait_ge(m["q"], n * s.qjobs + j + 1)
                        src = bank[s.jobs[j]][:, :].rearrange("p (k s) -> p k s", k=2)
                        for w in range(2 if s.ones else 1):
                            dst = qT[w][:, 2 * j:2 * j + 2, :]
                            if s.mask:
                                for k in range(2):
                                    ins = stt(dst[:, k, :], src[:, k, :], evens[:, w:w + 1],
                                              mask_u8[:, bass.ds(n * S, S)], ALU.mult, ALU.mult)
                            elif s.bias:
                                for k in range(2):
                                    ins = ts(dst[:, k, :], src[:, k, :], bq3[:, 2 * j + k:2 * j + k + 1],
                                             evens[:, w:w + 1], ALU.add, ALU.mult)
                            elif s.ones:
                                ins = ts(dst, src, evens[:, w:w + 1], None, ALU.mult)
                            else:
                                ins = ts(dst, src, s.qscale, None, ALU.mult)
                        ins.then_inc(m["qc"], 1)
                    if s.bias:
                        dve.wait_ge(m["v"], n + 1)
                        for t in range(T):
                            ins = tt(vh[:, t, :, 0:s.d],
                                     bank[s.jobs[-1]][:, t * D:(t + 1) * D].rearrange("p (h e) -> p h e", h=NH),
                                     bv3[:, :].rearrange("p (h e) -> p h e", h=NH), ALU.add)
                        ins.then_inc(m["vc"], 1)
                    if s.split:
                        dve.wait_ge(m["k"], (n + 1) * s.kjobs)
                        ch.link(ts(qxs[:, :], bank[7][:, 0:4 * NREG], s.qscale, None, ALU.mult))
                        qv = qxs[:, :].rearrange("p (g r) -> p g r", g=4)
                        for r in range(NREG):
                            ins = tt(qx[:, :, r * NH:(r + 1) * NH], hm[:, :, :],
                                     qv[:, :, r:r + 1].broadcast_to([P, 4, NH]), ALU.mult)
                        ins.then_inc(m["xs"], 1)

                def heads(n, ahead, steps_=None):
                    for h in steps_ or range(LAG, U + LAG):
                        if h < U:
                            dve.wait_ge(m["s"], n * U + h + 1)
                            if h == NH:
                                V.tensor_reduce(nmax[0:NX, h, 0:1], bank[h % 3][0:NX, 0:S], AXX, ALU.max, negate=True)\
                                    .then_inc(m["mx"], 1)
                            else:
                                src = bank[h % 3][:, :]
                                if s.clip:
                                    if h >= 3:
                                        dve.wait_ge(m["e"], n * NH + h - 2)
                                    ch.link(ts(sc[h % 3][:, :], src, CLAMP, -CLAMP, ALU.min, ALU.max))
                                    src = sc[h % 3][:, :]
                                V.tensor_reduce(nmax[:, h, :], src.rearrange("p (t k) -> p t k", t=T),
                                                AXX, ALU.max, negate=True).then_inc(m["mx"], 1)
                        if h >= LAG and not s.clip:
                            k = h - LAG
                            dve.wait_ge(m["pT"], n * U + k + 1)
                            if k >= 8:
                                dve.wait_ge(m["pv"], n * groups + (k - 8) // s.per + 1)
                            w = 2 * NX if k == NH else 512
                            V.tensor_copy(probT[k % 8][:, 0:w], bank[3 + k % 2][:, 0:w]).then_inc(m["pTc"], 1)
                        if h == LAG and ahead:
                            statistics(n + 1)
                        if isinstance(n, int) and n == B - 1 and not s.split and 0 <= h - 4 < B - 1 and not steps_:
                            stats_of(h - 4)
                        if h == FRONT and ahead:
                            front(n + 1)
                        if h == FRONT + 3 and ahead:
                            mask_rows(n + 1)

                def outputs(n):
                    if s.split:
                        dve.wait_ge(m["pv"], (n + 1) * groups)
                        ov = bank[7][0:NX, 0:NH * s.vs].rearrange("p (h e) -> p h e", h=NH)
                        ch.link(V.reciprocal(rec[0:NX, :], ov[:, :, s.d]))
                        ch.link(tt(rec[0:NX, :], rec[0:NX, :], bm[0:NX, :], ALU.mult))
                        tt(onx[0:NX, :].rearrange("p (h e) -> p h e", h=NH), ov[:, :, 0:s.d],
                           rec[0:NX, :].rearrange("p (h o) -> p h o", o=1).broadcast_to([NX, NH, s.d]),
                           ALU.mult).then_inc(m["xs"], 1)
                    for t in range(T):
                        dve.wait_ge(m["z"], n * T + t + 1)
                        z4 = bank[3 + t][:, :].rearrange("p (h e) -> p h e", h=NH)
                        ch.link(V.reciprocal(recs[:, t, :], z4[:, :, s.d]))
                        dst = (on[t][:, :] if s.proj else tmp).rearrange("p (h e) -> p h e", h=NH)
                        ins = tt(dst, z4[:, :, 0:s.d],
                                 recs[:, t, :].rearrange("p (h o) -> p h o", o=1).broadcast_to([P, NH, s.d]),
                                 ALU.mult)
                        if s.split and t == 0:
                            ch.link(ins)
                            dve.wait_ge(m["reg"], n + 1)
                            ins = stt(on[0][:, :], on[0][:, :], wcol[:, 0:1], bank[7][:, 0:D], ALU.mult, ALU.add)
                        if s.proj:
                            ins.then_inc(m["on"], 1)
                        else:
                            ch.link(ins)
                            ch.link(add_to_x(n, t, tmp, tgx[:, gi:gi + 1]))

                def finish(n):
                    for t in range(T):
                        dve.wait_ge(m["y"], n * T + (t + 1 if s.ones else T))
                        y = bank[3 + t][:, S:2 * S] if s.ones else bank[7][:, t * S:(t + 1) * S]
                        ch.link(tt(tmp, y, bo[s.name][:, :], ALU.add))
                        if t == T - 1:
                            V.memset(idle[:, 1:2], 0.0).then_inc(m["yr"], 1)
                        ch.link(add_to_x(n, t, tmp, (tgf if s.split else tgx)[:, gi:gi + 1]))

                front_links = LN
                proj_links = 1 if s.split else 0
                body = (2 * NH // 2 if s.clip else 0)
                if s.ones:
                    body += T * (1 if s.proj else 3) + (3 if s.split else 0)
                body += 2 * T if s.proj else 0
                ch.link(ts(evens[:, :], even[:, :], s.qscale, None, ALU.mult))
                if s.proj:
                    V.memset(idle[:, 2:3], 0.0).then_inc(m["yr"], 1)
                statistics(0)
                front(0)
                mask_rows(0)
                projected(0)
                heads(0, False, range(LAG))
                with dve.Fori(0, B - 1) as n:
                    ch.loop(n, body + front_links + proj_links)
                    heads(n, True)
                    if s.ones:
                        outputs(n)
                    projected(n + 1)
                    heads(n + 1, False, range(LAG))
                    if s.proj:
                        finish(n)
                ch.leave(B - 1)
                heads(B - 1, False)
                if s.ones:
                    outputs(B - 1)
                if s.proj:
                    finish(B - 1)
                V.memset(idle[:, 0:1], 0.0).then_inc(g["phase"], 1)

            def mixture(name, gi, ne):
                m = moe[name]
                ch = Chain(dve, m["dve"])
                f = F1 if name == "l1f" else F2
                ft = -(-f // P)
                all_stats(ch, m)

                def high_part(c):
                    dve.wait_ge(g["xt"], entries(name, 2 * c + 2))
                    cols = bass.ds(c * 512, 512)
                    V.tensor_copy(xth[:, :, cols], xtw[:, :, cols]).then_inc(m["xh"], 1)

                def two_entries(j):
                    for b in range(2):
                        dve.wait_ge(g["xnT"], entries(name, j * 2 + b) - 1)
                        normalise(j * 2 + b, b)

                two_entries(0)
                with dve.Fori(1, B // 2) as j:
                    two_entries(j)
                    high_part(j - 1)
                high_part(NBLK - 1)
                dve.wait_ge(m["lg"], 1)
                full = [P, NT, NE]
                per_tok = [P, NT, 1]
                gmv = gm[:, :].rearrange("p (t o) -> p t o", o=1)
                ch.link(V.tensor_copy(lg[:, :, :], bank[0][:, 0:NT * NE].rearrange("p (t e) -> p t e", t=NT)))
                V.memset(idle[:, 0:1], 0.0).then_inc(m["lr"], 1)
                ch.link(V.tensor_reduce(gm[:, :], lg[:, :, :], AXX, ALU.max))
                ch.link(tt(sel[:, :, :], lg[:, :, :], gmv.broadcast_to(full), ALU.subtract))
                V.memset(idle[:, 0:1], 0.0).then_inc(m["gd"], 1)
                def hidden(i, u, blk, h):
                    tile = ((i * 2 + u) * NBLK + blk) * ft + h
                    slot = ((u * NBLK + blk) * ft + h) % HS[name]
                    r = hidden_rows(f, h)
                    dve.wait_ge(m["sil"], tile + 1)
                    hi, lo, whole = (t[slot][r, :] for t in hid[name])
                    tt(whole, sil[h % 2][r, :], bank[(2 if r.start == 0 else 0) + h % 2][r, :], ALU.mult)\
                        .then_inc(m["prod"], 1)
                    dve.wait_ge(m["prod"], tile + 1)
                    ch.link(V.tensor_copy(hi, whole))
                    tt(lo, whole, hi, ALU.subtract).then_inc(m["hid"], 1)

                for h in range(ft):
                    hidden(0, 0, 0, h)
                dve.wait_ge(m["ga"], 1)
                if name == "l2f":
                    ch.link(V.tensor_reduce(gm[:, :], sel[:, :, :], AXX, ALU.add))
                    ch.link(V.reciprocal(gm[:, :], gm[:, :]))
                    ch.link(tt(sel[:, :, :], sel[:, :, :], gmv.broadcast_to(full), ALU.mult))
                    ch.link(tt(lg[:, :, :], sel[:, :, :],
                               gb2[:, :].rearrange("p (o e) -> p o e", o=1).broadcast_to(full), ALU.add))
                rank = scr[:, 0:NT * NE * NE].rearrange("p (t e j) -> p t e j", e=NE, j=NE)
                four = [P, NT, NE, NE]
                of_e = lg[:, :, :].rearrange("p t (e o) -> p t e o", o=1).broadcast_to(four)
                of_j = lg[:, :, :].rearrange("p t (o j) -> p t o j", o=1).broadcast_to(four)
                lower = tri[:, :, :].rearrange("p (o e) j -> p o e j", o=1).broadcast_to(four)
                ch.link(tt(rank, of_j, of_e, ALU.is_gt))
                ch.link(V.tensor_reduce(larger[:, :, :], rank, AXX, ALU.add))
                ch.link(tt(rank, of_j, of_e, ALU.is_equal))
                ch.link(tt(rank, rank, lower, ALU.mult))
                ch.link(V.tensor_reduce(lg[:, :, :], rank, AXX, ALU.add))
                ch.link(tt(lg[:, :, :], lg[:, :, :], larger[:, :, :], ALU.add))
                ch.link(ts(lg[:, :, :], lg[:, :, :], 1.5, None, ALU.is_lt))
                ch.link(tt(sel[:, :, :], sel[:, :, :], lg[:, :, :], ALU.mult))
                if name == "l1f":
                    ch.link(V.tensor_reduce(gm[:, :], sel[:, :, :], AXX, ALU.add))
                    ch.link(V.reciprocal(gm[:, :], gm[:, :]))
                    ch.link(tt(sel[:, :, :], sel[:, :, :], gmv.broadcast_to(full), ALU.mult))
                else:
                    ch.link(V.memset(gate[:, :, NE:NE + 2], 1.0))
                    ch.link(ts(gate[:, :, NE:NE + 2], gate[:, :, NE:NE + 2], tgf[:, gi:gi + 1], None, ALU.mult))
                ch.link(ts(gate[:, :, 0:NE], sel[:, :, :], tgf[:, gi:gi + 1], None, ALU.mult))
                V.memset(idle[:, 0:1], 0.0).then_inc(m["yc"], 1)

                def pair(i, last):
                    for u in range(2):
                        for blk in range(NBLK):
                            after = (i, u, blk + 1) if blk < NBLK - 1 else (i, 1, 0) if u == 0 else (i + 1, 0, 0)
                            more = not (last and u == 1 and blk == NBLK - 1)
                            if more:
                                hidden(*after, 0)
                            expert_out(m, i, u, blk, 4 * ((i * 2 + u) * NBLK + blk))
                            if more:
                                for h in range(1, ft):
                                    hidden(*after, h)

                with dve.Fori(0, ne // 2 - 1) as i:
                    ch.loop(i, 2 * NBLK * ft)
                    pair(i, False)
                ch.leave(ne // 2 - 1)
                pair(ne // 2 - 1, True)
                dve.wait_ge(m["hid"], ne * NBLK * ft)
                dve.wait_ge(m["yc"], ne * NBLK * 4 + 1)
                V.memset(idle[:, 0:1], 0.0).then_inc(g["phase"], 1)

            def expert_out(m, i, u, blk, before):
                for k in range(4):
                    t = blk * 4 + k
                    dve.wait_ge(m["y"], before + k + 1)
                    stt(x[:, t, :], bank[4 + k % 4][:, 0:D], gate[:, t, bass.ds(i * 2 + u, 1)], x[:, t, :],
                        ALU.mult, ALU.add).then_inc(m["yc"], 1)


            def guide():
                ch = Chain(dve, sm["dve"])
                q16 = lambda t: t.rearrange("p (h e) -> p h e", h=NH)
                all_stats(ch, sm)
                V.memset(idle[:, 2:3], 0.0).then_inc(sm["qc"], 1)
                normalise(0, 0)
                ch.link(tt(tmp, qg[:, :], qg[:, :], ALU.mult))
                root(sm, 2, V.tensor_reduce(ss[:, 0:NH], q16(tmp), AXX, ALU.add))
                ch.link(tt(q16(qg[:, :]), q16(qg[:, :]),
                           ss[:, 0:NH].rearrange("p (h o) -> p h o", o=1).broadcast_to([P, NH, 16]), ALU.mult))
                by_head = lambda t: t.rearrange("p (h e) -> p h e", e=16)

                def step(n, b, first, last):
                    if not last:
                        dve.wait_ge(g["xnT"], entries("sim", n))
                        normalise(n + 1, 1 - b)
                    dve.wait_ge(sm["q"], n + 1)
                    heads = bass.ds(n * T * NH, T * NH)
                    tt(gprod.rearrange("p (t d) -> p t d", t=T), bank[b][:, :].rearrange("p (t d) -> p t d", t=T),
                       qg[:, :].rearrange("p (o d) -> p o d", o=1).broadcast_to([P, T, D]), ALU.mult)                        .then_inc(sm["prod"], 1)
                    dve.wait_ge(sm["prod"], n + 1)
                    ch.link(V.tensor_reduce(ssg[:, heads], by_head(gprod), AXX, ALU.add))
                    dve.wait_ge(sm["sq"], n + 1)
                    V.tensor_reduce(ssq[:, heads], by_head(sq[b]), AXX, ALU.add).then_inc(sm["qc"], 1)

                steps(dve, step, ch, 1)
                dve.wait_ge(sm["qc"], B + 1)
                V.memset(idle[:, 0:1], 0.0).then_inc(sm["sums"], 1)
                dve.wait_ge(sm["sqrt"], 1)
                ch.link(V.reciprocal(inv, inv))
                ch.link(tt(inv2, inv, inv, ALU.mult))
                ch.link(tt(inv2, inv2, ssq, ALU.mult))
                ch.link(ts(inv2, inv2, -0.5, 1.5, ALU.mult, ALU.add))
                ch.link(tt(inv, inv, inv2, ALU.mult))
                ch.link(tt(inv, inv, ssg, ALU.mult))
                ch.link(V.tensor_reduce(sim[:, :], inv.rearrange("p (t h) -> p t h", h=NH), AXX, ALU.add))
                ch.link(ts(sim[:, :], sim[:, :], 1.0 / NH, None, ALU.mult))
                nreg = scr[:, 0:NT]
                t0 = scr[:, NT:2 * NT]
                t1 = scr[:, 2 * NT:3 * NT]
                ch.link(ts(nreg, regm[:, :], -1.0, 1.0, ALU.mult, ALU.add))
                ch.link(tt(t0, sim[:, :], nreg, ALU.mult))
                ch.link(stt(t1, regm[:, :], -FAR, t0, ALU.mult, ALU.add))
                ch.link(V.tensor_reduce(ss[:, 0:1], t1, AXX, ALU.max))
                ch.link(stt(t1, regm[:, :], FAR, t0, ALU.mult, ALU.add))
                ch.link(ts(t1, t1, -1.0, None, ALU.mult))
                ch.link(V.tensor_reduce(ss[:, 1:2], t1, AXX, ALU.max))
                assert ch.base + ch.k == SIM_STEPS_BEFORE, ch.base + ch.k
                dve.wait_ge(sm["pool"], 1)
                ch.link(ts(t0, sim[:, :], ss[:, 3:4], None, ALU.add))
                ch.link(tt(ss[:, 4:5], ss[:, 2:3], ss[:, 3:4], ALU.add))
                ch.link(V.reciprocal(ss[:, 4:5], ss[:, 4:5]))
                ch.link(ts(t0, t0, ss[:, 4:5], None, ALU.mult))
                ch.link(ts(t0, t0, 0.9, None, ALU.is_gt))
                ch.link(tt(qp[:, :, 0], t0, regm[:, :], ALU.max))
                ch.link(ts(qp[:, :, 1], qp[:, :, 0], -1.0, 1.0, ALU.mult, ALU.add))
                ch.link(ts(t1, t0, -1.0, 1.0, ALU.mult, ALU.add))
                ch.link(stt(kp[:, :, 0], t1, -FAR, nreg, ALU.mult, ALU.mult))
                ch.link(stt(kp[:, :, 1], t0, -FAR, nreg, ALU.mult, ALU.mult))
                V.memset(idle[:, 0:1], 0.0).then_inc(g["phase"], 1)

            dve.wait_ge(g["x_in"], 16)
            dve.wait_ge(g["tanh"], 2)
            dve.wait_ge(g["consts"], g["n_consts"])
            similarity()
            dve.wait_ge(g["att_in"], 16 * g["n_loads"])
            for name in run[1:]:
                if name == "l0f":
                    feed_forward()
                elif name == "l1x":
                    attention(L1X, 1)
                elif name == "l1f":
                    mixture("l1f", 1, NE)
                elif name == "l2x":
                    attention(L2X, 2)
                elif name == "l2f":
                    mixture("l2f", 2, NE + 2)
                elif name == "l3x":
                    attention(L3X, 3)
                elif name == "sim":
                    guide()
                else:
                    attention(L3F, 3)

        @block.scalar
        def _(act):
            A = nc.scalar.activation

            def copy(dst, src):
                return A(dst, src, ACT.Copy)

            def turned(name, n, b=0, first_bank=6):
                act.wait_ge(g["xnT"], entries(name, n) + 1)
                copy(xtb[b][:, :, :], bank[first_bank + b][:, :].rearrange("p (c s) -> p c s", c=DC))\
                    .then_inc(g["xt"], 1)

            def similarity():
                turned("l0x", 0)

                def step(n, b, first, last):
                    if not last:
                        turned("l0x", n + 1, 1 - b)
                    act.wait_ge(l0x["vt"], n + 1)
                    for k, bias in enumerate((b0v, b0t)):
                        A(qT[0][:, k, :], bank[k][:, 0:S], ACT.Identity, bias=bias[:, 0:1]).then_inc(l0x["vtc"], 1)
                    for k, bias in enumerate((b0v, b0t)):
                        A(kT[:, k, :], bank[k][:, 0:S], ACT.Square, bias=bias[:, 0:1]).then_inc(l0x["vtc"], 1)

                steps(act, step)

            def feed_forward():
                turned("l0f", 0, 0, 4)

                def step(n, b, first, last):
                    for j in range(F0 // P):
                        act.wait_ge(l0f["h"], n * (F0 // P) + j + 1)
                        A(hid0[:, j, :], bank[j % 4][:, 0:S], ACT.Relu, bias=b01[:, j:j + 1]).then_inc(l0f["hc"], 1)
                    if not last:
                        turned("l0f", n + 1, 1 - b, 4)

                steps(act, step)

            def attention(s):
                m = ph[s.name]
                U = s.units
                vh = v[:, :, 0:NH * s.vs].rearrange("p t (h e) -> p t h e", h=NH)

                def front(n):
                    act.wait_ge(g["xnT"], entries(s.name, n) + 1)
                    copy(xt[:, :, :], bank[7][:, :].rearrange("p (c s) -> p c s", c=DC)).then_inc(g["xt"], 1)

                def projected(n):
                    for j in range(s.qjobs):
                        act.wait_ge(m["k"], n * s.kjobs + j + 1)
                        dst = kT[:, 2 * j:2 * j + 2, :]
                        src = bank[s.jobs[s.qjobs + j]][:, :].rearrange("p (k s) -> p k s", k=2)
                        if s.bias:
                            for k in range(2):
                                ins = A(dst[:, k, :], src[:, k, :], ACT.Identity, bias=bk3[:, 2 * j + k:2 * j + k + 1])
                        else:
                            ins = copy(dst, src)
                        ins.then_inc(m["kc"], 1)
                    if not s.bias:
                        for j in range(s.vjobs):
                            act.wait_ge(m["v"], n * s.vjobs + j + 1)
                            src = bank[s.jobs[2 * s.qjobs + j]]
                            if s.ones:
                                for t in range(T):
                                    ins = copy(vh[:, t, :, 0:s.d],
                                               src[:, t * D:(t + 1) * D].rearrange("p (h e) -> p h e", h=NH))
                            else:
                                ins = copy(v[:, j // 2, (j % 2) * 512:(j % 2 + 1) * 512], src[:, :])
                            ins.then_inc(m["vc"], 1)

                def gathered(n, f):
                    groups = s.groups + (1 if s.split else 0)
                    act.wait_ge(m["pv"], n * groups + 2 * f + 2)
                    copy(oTs[:, 2 * f:2 * f + 2, :], bank[5 + f % 2][:, :].rearrange("p (k s) -> p k s", k=2))\
                        .then_inc(m["oc"], 1)

                def heads(n, ahead, steps_=None):
                    nf = 0
                    for h in steps_ or range(LAG, U + LAG + 2):
                        if h < U:
                            act.wait_ge(m["mx"], n * U + h + 1)
                            if h >= 3:
                                act.wait_ge(m["pT"], n * U + h - 2)
                        if h < NH:
                            src = (sc[h % 3] if s.clip else bank[h % 3])
                            for t in range(T):
                                kw = {} if s.ones else {"accum_out": esum[:, h, t:t + 1]}
                                ins = A(prob[h % 3][:, t * S:(t + 1) * S], src[:, t * S:(t + 1) * S], ACT.Exp,
                                        bias=nmax[:, h, t:t + 1], **kw)
                            ins.then_inc(m["e"], 1)
                        elif h < U:
                            A(prob[h % 3][0:NX, 0:S], bank[h % 3][0:NX, 0:S], ACT.Exp, bias=nmax[0:NX, h, 0:1])\
                                .then_inc(m["e"], 1)
                        if s.clip and LAG <= h < U + LAG:
                            k = h - LAG
                            act.wait_ge(m["pT"], n * U + k + 1)
                            if k >= 8:
                                act.wait_ge(m["pv"], n * s.groups + (k - 8) // s.per + 1)
                            copy(probT[k % 8][:, :], bank[3 + k % 2][:, :]).then_inc(m["pTc"], 1)
                        if h == FRONT + 1 and ahead:
                            front(n + 1)
                        if nf < s.fills and h == min((nf + 1) * 2 * s.per - 1 + LAG + 2, U + LAG + 1):
                            gathered(n, nf)
                            nf += 1
                    assert steps_ or nf == s.fills

                def finish(n):
                    for t in range(T):
                        act.wait_ge(m["onT"], n * T + t + 1)
                        copy(oT[t][:, :, :], bank[3 + t][:, 0:DC * P].rearrange("p (c s) -> p c s", s=P))\
                            .then_inc(m["oT"], 1)

                if s.ones:
                    act.wait_ge(m["dve"], T)
                front(0)
                projected(0)
                heads(0, False, range(LAG))
                with act.Fori(0, B - 1) as n:
                    heads(n, True)
                    projected(n + 1)
                    heads(n + 1, False, range(LAG))
                    if s.ones and s.proj:
                        finish(n)
                heads(B - 1, False)
                if s.ones and s.proj:
                    finish(B - 1)

            def mixture(name, ne):
                m = moe[name]
                f = F1 if name == "l1f" else F2
                ft = -(-f // P)
                with act.Fori(0, B // 2) as j:
                    for b in range(2):
                        n = j * 2 + b
                        act.wait_ge(g["xnT"], entries(name, n) + 1)
                        copy(xtw[:, :, bass.ds(n * S, S)], bank[6 + b][:, :].rearrange("p (c s) -> p c s", c=DC))\
                            .then_inc(g["xt"], 1)
                act.wait_ge(m["gd"], 1)
                A(sel[:, :, :], sel[:, :, :], ACT.Exp).then_inc(m["ga"], 1)
                with act.Fori(0, ne // 2) as i:
                    for u in range(2):
                        for blk in range(NBLK):
                            blocks = (i * 2 + u) * NBLK + blk
                            for h in range(ft):
                                r = hidden_rows(f, h)
                                act.wait_ge(m["a"], blocks * ft + h + 1)
                                if h >= 2:
                                    act.wait_ge(m["prod"], blocks * ft + h - 1)
                                A(sil[h % 2][r, :], bank[h % 2][0:r.stop - r.start, :], ACT.Silu).then_inc(m["sil"], 1)

            def guide():
                turned("sim", 0)

                def step(n, b, first, last):
                    if not last:
                        turned("sim", n + 1, 1 - b)
                    act.wait_ge(sm["prod"], n + 1)
                    if not first:
                        act.wait_ge(sm["qc"], n + 1)
                    A(sq[b], bank[b][:, :], ACT.Square).then_inc(sm["sq"], 1)

                steps(act, step)
                act.wait_ge(sm["sums"], 1)
                A(inv, ssq, ACT.Sqrt).then_inc(sm["sqrt"], 1)

            act.wait_ge(g["w0_in"], 16 * 6)
            A(tgx[:, :], gates_x[:, :], ACT.Tanh).then_inc(g["tanh"], 1)
            A(tgf[:, :], gates_f[:, :], ACT.Tanh).then_inc(g["tanh"], 1)
            similarity()
            act.wait_ge(g["att_in"], 16 * g["n_loads"])
            for name in run[1:]:
                if name == "l0f":
                    feed_forward()
                elif name in attn:
                    attention(attn[name])
                elif name == "l1f":
                    mixture("l1f", NE)
                elif name == "l2f":
                    mixture("l2f", NE + 2)
                else:
                    guide()

        @block.tensor
        def _(pe):
            mm, tr = nc.tensor.matmul, nc.tensor.transpose

            def mm3(out_, ab, cd, start, stop):
                (ah, al), (bh, bl) = ab, cd
                mm(out_, al, bh, start=start, stop=False)
                mm(out_, ah, bl, start=False, stop=False)
                return mm(out_, ah, bh, start=False, stop=stop)

            def turn(name, n, b=0, first_bank=6):
                pe.wait_ge(g["xn"], entries(name, n) * T + T)
                for t in range(T):
                    for c in range(DC):
                        ins = tr(bank[first_bank + b][:, c * S + t * P:c * S + (t + 1) * P],
                                 xnb(b, t)[:, c * P:(c + 1) * P], ident[:, :])
                ins.then_inc(g["xnT"], 1)

            def similarity():
                turn("l0x", 0)

                def rows(n):
                    pe.wait_ge(l0x["dg"], n + 1)
                    for t in range(T):
                        ins = mm(bank[5][:, t * P:(t + 1) * P], ones[:, :], diag[:, t, :], start=True, stop=True)
                    ins.then_inc(l0x["rows"], 1)

                def step(n, b, first, last):
                    if not last:
                        if not first:
                            pe.wait_ge(g["xt"], n)
                        turn("l0x", n + 1, 1 - b)
                    pe.wait_ge(g["xt"], n + 1)
                    pe.wait_ge(l0x["ct"], n * 16 + 16)
                    for c in range(DC):
                        mm(bank[0][:, 0:S], w0v[:, c, :], xtb[b][:, c, :], start=c == 0, stop=c == DC - 1)
                    for c in range(2):
                        ins = mm(bank[1][:, 0:S], w0t[:, c, :], ct[:, c, :], start=c == 0, stop=c == 1)
                    ins.then_inc(l0x["vt"], 1)
                    if not first:
                        pe.wait_ge(l0x["fin"], n)
                        rows(n - 1)
                    pe.wait_ge(l0x["vtc"], n * 4 + 4)
                    for t in range(T):
                        mm(bank[2 + b][:, t * S:(t + 1) * S], qT[0][:, 0, t * P:(t + 1) * P], qT[0][:, 1, :],
                           start=True, stop=True)
                    for k in range(2):
                        for t in range(T):
                            c = k * T + t
                            ins = mm(bank[4][:, c:c + 1], kT[:, k, t * P:(t + 1) * P], ones[:, 0:1], start=True, stop=True)
                    ins.then_inc(l0x["dots"], 1)

                steps(pe, step)
                rows(B - 1)

            def feed_forward():
                nj = F0 // P
                turn("l0f", 0, 0, 4)

                def step(n, b, first, last):
                    pe.wait_ge(g["xt"], entries("l0f", n) + 1)
                    for j in range(nj):
                        if j >= 4:
                            pe.wait_ge(l0f["hc"], n * nj + j - 3)
                        for c in range(DC):
                            ins = mm(bank[j % 4][:, 0:S], w01[:, c, j * P:(j + 1) * P], xtb[b][:, c, :],
                                     start=c == 0, stop=c == DC - 1)
                        ins.then_inc(l0f["h"], 1)
                    if not last:
                        turn("l0f", n + 1, 1 - b, 4)
                    pe.wait_ge(l0f["hc"], n * nj + nj)
                    if not first:
                        pe.wait_ge(l0f["yc"], n)
                    for t in range(T):
                        for j in range(nj):
                            ins = mm(bank[6 + t][:, 0:D], hid0[:, j, t * P:(t + 1) * P], w02[:, j, :],
                                     start=j == 0, stop=j == nj - 1)
                        ins.then_inc(l0f["y"], 1)

                steps(pe, step)

            def attention(s):
                m = ph[s.name]
                U = s.units
                groups = s.groups + (1 if s.split else 0)
                src = xt if s.split else ct
                w_q, w_k, w_v = wq[s.name], wk[s.name], wv[s.name]

                def front(n):
                    pe.wait_ge(g["xn"], entries(s.name, n) * T + T)
                    for t in range(T):
                        for c in range(DC):
                            ins = tr(bank[7][:, c * S + t * P:c * S + (t + 1) * P], xn[:, t, c * P:(c + 1) * P],
                                     ident[:, :])
                    ins.then_inc(g["xnT"], 1)
                    if s.split:
                        pe.wait_ge(m["cols"], n + 1)
                        pe.wait_ge(g["xt"], entries(s.name, n) + 1)
                        for k in range(2):
                            for t in range(T):
                                ins = mm(bank[7][0:2, k * S + t * P:k * S + (t + 1) * P],
                                         qk2[:, t, 2 * k:2 * k + 2], ident[:, :], start=True, stop=True)
                        ins.then_inc(m["mrow"], 1)

                def project(n):
                    pe.wait_ge(g["xt"], entries(s.name, n) + 1)
                    if s.split:
                        pe.wait_ge(m["mrowc"], n + 1)
                    else:
                        pe.wait_ge(m["ct"], n * 16 + 16)
                    for w, what, kt_, of, mk in ((w_q, "q", DC, xt, 0), (w_k, "k", s.kt, src, 1)):
                        for j in range(s.qjobs):
                            job = mk * s.qjobs + j
                            if job >= 7:
                                pe.wait_ge(m["qc"], n * s.qjobs + job - 6)
                            for k in range(2):
                                gr = 2 * j + k
                                dst = bank[s.jobs[job]][:, k * S:(k + 1) * S]
                                for c in range(kt_):
                                    ins = mm(dst, w[:, c, gr * P:(gr + 1) * P], of[:, c, :], start=c == 0,
                                             stop=c == kt_ - 1 and not s.split)
                                if s.split:
                                    ins = mm(dst, selw[:, :], mrow[:, mk, :], start=False, stop=True)
                            ins.then_inc(m[what], 1)
                    if s is L2X and isinstance(n, int):
                        pe.wait_ge(g["w2b_in"], 16 * 2)
                    for j in range(s.vjobs):
                        job = 2 * s.qjobs + j
                        if s.ones:
                            parts = [(bank[s.jobs[job]][:, t * D:(t + 1) * D], t, 0, D) for t in range(T)]
                        else:
                            if job - 7 < s.qjobs:
                                pe.wait_ge(m["qc"], n * s.qjobs + job - 6)
                            else:
                                pe.wait_ge(m["kc"], n * s.qjobs + job - 6 - s.qjobs)
                            parts = [(bank[s.jobs[job]][:, :], j // 2, (j % 2) * 512, 512)]
                        for dst, t, c0, w in parts:
                            for c in range(s.kt):
                                ins = mm(dst, src[:, c, t * P:(t + 1) * P], w_v[:, c, c0:c0 + w],
                                         start=c == 0, stop=c == s.kt - 1)
                        ins.then_inc(m["v"], 1)

                def project_registers(n):
                    for gr in range(4):
                        dst = bank[7][:, gr * NREG:(gr + 1) * NREG]
                        for c in range(DC):
                            mm(dst, w_q[:, c, gr * P:(gr + 1) * P], xt[:, c, 0:NREG], start=c == 0, stop=False)
                        ins = mm(dst, selw[:, :], mregq[:, :], start=False, stop=True)
                    ins.then_inc(m["k"], 1)

                def scores(n, h):
                    if h >= 3:
                        pe.wait_ge(m["e"], n * U + h - 2)
                    if h == NH:
                        pe.wait_ge(m["xs"], n * 2 + 1)
                        for gr in range(4):
                            ins = mm(bank[h % 3][0:NX, 0:S], qx[:, gr, :], kT[:, gr, :], start=gr == 0, stop=gr == 3)
                    else:
                        gr = h // s.per
                        r0 = 64 * (h % s.per // (s.per // 2))
                        q = qT[h % 2 if s.ones else 0]
                        for t in range(T):
                            ins = mm(bank[h % 3][:, t * S:(t + 1) * S], q[r0:r0 + 64, gr, t * P:(t + 1) * P],
                                     kT[r0:r0 + 64, gr, :], start=True, stop=True)
                    ins.then_inc(m["s"], 1)

                def turn_probs(n, k):
                    pe.wait_ge(m["e" if s.ones else "pn"], n * U + k + 1)
                    if s.proj and k == 0:
                        pe.wait_ge(m["yr"], n + 1)
                    if k >= 2:
                        pe.wait_ge(m["pTc"], n * U + k - 1)
                    for kt in range(T):
                        if k == NH:
                            ins = tr(bank[3 + k % 2][:, kt * NX:(kt + 1) * NX],
                                     prob[k % 3][0:NX, kt * P:(kt + 1) * P], ident[0:NX, 0:NX])
                        else:
                            for t in range(T):
                                c0 = (kt * T + t) * P
                                ins = tr(bank[3 + k % 2][:, c0:c0 + P],
                                         prob[k % 3][:, t * S + kt * P:t * S + (kt + 1) * P], ident[:, :])
                    ins.then_inc(m["pT"], 1)

                def values(n, gr, ahead):
                    if gr == s.groups:
                        pe.wait_ge(m["pTc"], (n + 1) * U)
                        if ahead:
                            pe.wait_ge(m["mrowc"], n + 2)
                        for kt in range(T):
                            ins = mm(bank[7][0:NX, 0:NH * s.vs], probT[NH % 8][:, kt * NX:(kt + 1) * NX],
                                     v[:, kt, 0:NH * s.vs], start=kt == 0, stop=kt == T - 1)
                        ins.then_inc(m["pv"], 1)
                        return
                    pe.wait_ge(m["pTc"], n * U + (gr + 1) * s.per)
                    if gr == 0:
                        pe.wait_ge(m["vc"], (n + 1) * s.vjobs)
                    if gr >= 4 and gr % 2 == 0:
                        pe.wait_ge(m["oc"], n * s.fills + gr // 2 - 1)
                    for kt in range(T):
                        for j in range(s.per):
                            h = gr * s.per + j
                            r0 = j * s.rows
                            ins = mm(bank[5 + gr // 2 % 2][r0:r0 + s.vs, gr % 2 * S:(gr % 2 + 1) * S],
                                     v[:, kt, h * s.vs:(h + 1) * s.vs], probT[h % 8][:, kt * S:(kt + 1) * S],
                                     start=kt == 0, stop=kt == T - 1)
                    ins.then_inc(m["pv"], 1)

                def first_heads(n):
                    pe.wait_ge(m["qc"], (n + 1) * s.qjobs)
                    pe.wait_ge(m["kc"], (n + 1) * s.qjobs)
                    if not s.ones:
                        pe.wait_ge(m["vc"], (n + 1) * s.vjobs)
                    for h in range(LAG):
                        scores(n, h)

                def heads(n, ahead):
                    gr = 0
                    for h in range(LAG, U + LAG + 1):
                        if h < U:
                            scores(n, h)
                        if h < U + LAG:
                            turn_probs(n, h - LAG)
                        if h == FRONT + 1 and ahead:
                            front(n + 1)
                        while gr < groups and min((gr + 1) * s.per, U) - 1 + LAG + 1 <= h:
                            values(n, gr, ahead)
                            gr += 1
                    assert gr == groups

                def outputs(n):
                    if s.split:
                        pe.wait_ge(m["xs"], n * 2 + 2)
                        mm(bank[7][:, 0:D], rsel[0:NX, :], onx[0:NX, :], start=True, stop=True).then_inc(m["reg"], 1)
                    pe.wait_ge(m["oc"], (n + 1) * s.fills)
                    pe.wait_ge(m["pTc"], (n + 1) * U)
                    for t in range(T):
                        for gr in range(4):
                            ins = tr(bank[3 + t][:, gr * P:(gr + 1) * P], oTs[:, gr, t * P:(t + 1) * P], ident[:, :])
                        ins.then_inc(m["z"], 1)

                def finish(n):
                    if s.ones:
                        for t in range(T):
                            pe.wait_ge(m["on"], n * T + t + 1)
                            for c in range(DC):
                                ins = tr(bank[3 + t][:, c * P:(c + 1) * P], on[t][:, c * P:(c + 1) * P], ident[:, :])
                            ins.then_inc(m["onT"], 1)
                        for t in range(T):
                            pe.wait_ge(m["oT"], n * T + t + 1)
                            for c in range(DC):
                                ins = mm(bank[3 + t][:, S:2 * S], oT[t][:, c, :], wo[s.name][:, c, :],
                                         start=c == 0, stop=c == DC - 1)
                            ins.then_inc(m["y"], 1)
                    else:
                        pe.wait_ge(m["oc"], (n + 1) * s.fills)
                        for t in range(T):
                            for c in range(s.groups):
                                ins = mm(bank[7][:, t * S:(t + 1) * S], oTs[:, c, t * P:(t + 1) * P],
                                         wo[s.name][:, c, :], start=c == 0, stop=c == s.groups - 1)
                            ins.then_inc(m["y"], 1)

                pe.wait_ge(g["phase"], n_phase[s.name] - 1)
                if s is L3X:
                    pe.wait_ge(g["w3_in"], 16 * 3)
                if s is L2X:
                    pe.wait_ge(g["w2a_in"], 16 * 2)
                front(0)
                project(0)
                if s.split:
                    project_registers(0)
                first_heads(0)
                with pe.Fori(0, B - 1) as n:
                    heads(n, True)
                    if s.ones:
                        outputs(n)
                    else:
                        pe.wait_ge(m["oc"], (n + 1) * s.fills)
                    project(n + 1)
                    if s.split:
                        pe.wait_ge(m["on"], n * T + 1)
                        project_registers(n + 1)
                    first_heads(n + 1)
                    if s.proj:
                        finish(n)
                heads(B - 1, False)
                if s.ones:
                    outputs(B - 1)
                if s.proj:
                    finish(B - 1)

            def mixture(name, wg, ne):
                m = moe[name]
                f = F1 if name == "l1f" else F2
                ft = -(-f // P)
                def logits(n):
                    pe.wait_ge(g["xt"], entries(name, n) + 1)
                    for t in range(n * T, n * T + T):
                        for c in range(DC):
                            ins = mm(bank[0][:, t * NE:(t + 1) * NE], xtw[:, c, t * P:(t + 1) * P], wg[:, c, :],
                                     start=c == 0, stop=c == DC - 1)
                    return ins

                for n in range(B):
                    pe.wait_ge(g["xt"], entries(name, n) - 1)
                    turn(name, n, n % 2)
                    if n >= 2:
                        logits(n - 2)
                logits(B - 2)
                logits(B - 1).then_inc(m["lg"], 1)
                pe.wait_ge(m["lr"], 1)

                def down(u, w3, blk, before):
                    pe.wait_ge(m["yc"], before + 1)
                    for k in range(4):
                        for h in range(ft):
                            r = hidden_rows(f, h)
                            slot = ((u * NBLK + blk) * ft + h) % HS[name]
                            ins = mm3(bank[4 + k][:, 0:D],
                                      [t[slot][r, k * P:(k + 1) * P] for t in hid[name][0:2]],
                                      [w[r, h, :] for w in w3], h == 0, h == ft - 1)
                        ins.then_inc(m["y"], 1)

                def up(i, u, blk, h):
                    w1, w2, ends, _ = zip(*expert(u, f))
                    tile = ((i * 2 + u) * NBLK + blk) * ft + h
                    if h == 0 and blk == 0:
                        pe.wait_ge(m["ws"], i * 2 + u + 1)
                    pe.wait_ge(m["xs"], blk + 1)
                    if not isinstance(i, int) or tile >= 2:
                        pe.wait_ge(m["prod"], tile - 1)
                    full = hidden_rows(f, h).start == 0
                    for k, w, w0 in ((0, w1, h * P), (2, w2, h * P)) if full else ((0, ends, 0),):
                        for c in range(DC):
                            ins = mm3(bank[k + h % 2][:, :], [t[:, c, w0:w0 + P] for t in w],
                                      [t[:, c, blk * 512:(blk + 1) * 512] for t in (xth, xtl)],
                                      c == 0, c == DC - 1)
                    ins.then_inc(m["a"], 1)

                def pair(i, last):
                    for u in range(2):
                        for blk in range(NBLK):
                            for h in range(1, ft):
                                up(i, u, blk, h)
                            if blk < NBLK - 1:
                                up(i, u, blk + 1, 0)
                            elif u == 0:
                                up(i, 1, 0, 0)
                            elif not last:
                                up(i + 1, 0, 0, 0)
                            blocks = (i * 2 + u) * NBLK + blk
                            pe.wait_ge(m["hid"], (blocks + 1) * ft)
                            down(u, list(zip(*expert(u, f)))[3], blk, 4 * blocks)

                up(0, 0, 0, 0)
                with pe.Fori(0, ne // 2 - 1) as i:
                    pair(i, False)
                pair(ne // 2 - 1, True)

            def guide():
                turn("sim", 0)

                def step(n, b, first, last):
                    if not last:
                        pe.wait_ge(g["xt"], entries("sim", n))
                        turn("sim", n + 1, 1 - b)
                    pe.wait_ge(g["xt"], entries("sim", n) + 1)
                    if not first:
                        pe.wait_ge(sm["qc"], n)
                    for t in range(T):
                        for c in range(DC):
                            ins = mm(bank[b][:, t * D:(t + 1) * D], xtb[b][:, c, t * P:(t + 1) * P], wqs[:, c, :],
                                     start=c == 0, stop=c == DC - 1)
                    ins.then_inc(sm["q"], 1)

                steps(pe, step)

            pe.wait_ge(g["consts"], g["n_consts"])
            pe.wait_ge(g["w0_in"], 16 * 6)
            similarity()
            pe.wait_ge(g["w0f_in"], 32)
            pe.wait_ge(g["att_in"], 16 * g["n_loads"])
            for name in run[1:]:
                if name == "l0f":
                    feed_forward()
                elif name in attn:
                    attention(attn[name])
                elif name == "l1f":
                    mixture("l1f", wg1, NE)
                elif name == "l2f":
                    mixture("l2f", wg2, NE + 2)
                else:
                    guide()


SIM_STEPS_BEFORE = 2 + 2 + B + 6 + 9


def kernel(**inputs):
    import numpy as np
    import concourse.bacc as bacc
    from concourse.bass_utils import run_bass_kernel_spmd

    def rows(w, k):
        return w.reshape(k, w.shape[0] // k, w.shape[1]).transpose(1, 0, 2)

    def heads32(w):
        r = np.zeros((w.shape[0], NH, 32), w.dtype)
        r[:, :, 0:16] = w.reshape(w.shape[0], NH, 16)
        return r.reshape(w.shape[0], NH * 32)

    def columns(b):
        return heads32(b.reshape(1, D)).reshape(4, P).T

    def per_expert(w1, w2, w3):
        f = w1.shape[0]
        full, end, half = f // P * P, f % P, P // 2
        down = np.zeros((-(-f // P) * P, D), w1.dtype)
        down[0:full] = w3.T[0:full]
        parts = [rows(w1[0:full].T, DC), rows(w2[0:full].T, DC)]
        if end:
            ends = np.zeros((P, D), w1.dtype)
            ends[0:end], ends[half:half + end] = w1[full:], w2[full:]
            down[full + half:full + half + end] = w3.T[full:]
            parts.append(rows(ends.T, DC))
        return np.concatenate([p.reshape(P, -1) for p in parts + [rows(down, -(-f // P))]], axis=1)

    n = {k: np.asarray(v) for k, v in inputs.items()}
    wkv = n["L1_xattn_Wkv"].T
    qkv = n["L3_ffn_W_qkv"]
    we1 = np.stack([per_expert(n["L1_ffn_W1"][e], n["L1_ffn_W2"][e], n["L1_ffn_W3"][e]) for e in range(NE)])
    shared = [(n["L2_ffn_sw1"][F2 * e:F2 * e + F2], n["L2_ffn_sw3"][F2 * e:F2 * e + F2],
               n["L2_ffn_sw2"][:, F2 * e:F2 * e + F2]) for e in range(2)]
    we2 = np.stack([per_expert(n["L2_ffn_w1"][e], n["L2_ffn_w3"][e], n["L2_ffn_w2"][e]) for e in range(NE)]
                   + [per_expert(*t) for t in shared])
    arrays = {
        "x": n["x"],
        "ctxT": n["ctx_768"].reshape(B, S, 2, CK).transpose(0, 3, 2, 1),
        "mask": n["mask_BxS_bk0"].reshape(B * S),
        "g_xattn": n["g_xattn"], "g_ffn": n["g_ffn"],
        "w0v": rows(n["L0_xattn_Wv"].T, DC), "w0t": rows(n["L0_xattn_Wt"].T, 2),
        "b0v": n["L0_xattn_bv"].reshape(P, 1), "b0t": n["L0_xattn_bt"].reshape(P, 1),
        "w01": rows(n["L0_ffn_w1"][0], DC), "w02": rows(n["L0_ffn_w2"][0], F0 // P),
        "b01": n["L0_ffn_b1"][0].reshape(F0 // P, P).T, "b02": n["L0_ffn_b2"][0],
        "gamma": n["L0_ffn_gamma"], "beta": n["L0_ffn_beta"],
        "wq_l1x": rows(heads32(n["L1_xattn_Wq"].T), DC),
        "wk_l1x": rows(heads32(wkv[:, 0:D]), 2), "wv_l1x": rows(wkv[:, D:2 * D], 2),
        "wg1": rows(n["L1_ffn_Wg"].T, DC), "we1": we1,
        "wq_l2x": rows(n["L2_xattn_w_q"], DC), "wk_l2x": rows(n["L2_xattn_w_k"], 2),
        "wv_l2x": rows(n["L2_xattn_w_v"], 2), "wo_l2x": rows(n["L2_xattn_w_o"], 8), "bo_l2x": n["L2_xattn_b_o"],
        "wg2": rows(n["L2_ffn_gate_w"].T, DC), "gb2": n["L2_ffn_gate_bias"], "we2": we2,
        "wq_l3x": rows(heads32(n["L3_xattn_Wq"]), DC), "bq3": columns(n["L3_xattn_bq"]),
        "wk_l3x": rows(heads32(n["L3_xattn_Wk"]), 2), "bk3": columns(n["L3_xattn_bk"]),
        "wv_l3x": rows(n["L3_xattn_Wv"], 2), "bv3": n["L3_xattn_bv"],
        "wo_l3x": rows(n["L3_xattn_Wo"], DC), "bo_l3x": n["L3_xattn_bo"],
        "qg": n["L3_ffn_g_info"][0, 0],
        "wqs": rows(qkv[:, 0:D], DC), "wq_l3f": rows(heads32(qkv[:, 0:D]), DC),
        "wk_l3f": rows(heads32(qkv[:, D:2 * D]), DC), "wv_l3f": rows(qkv[:, 2 * D:3 * D], DC),
        "wo_l3f": rows(n["L3_ffn_W_proj"], DC), "bo_l3f": n["L3_ffn_b_proj"],
    }
    arrays = {k: np.ascontiguousarray(v) for k, v in arrays.items()}
    nc = bacc.Bacc("TRN2", target_bir_lowering=False, num_devices=1)
    aps = {k: nc.dram_tensor(f"in_{k}", v.shape, mybir.dt.from_np(v.dtype), kind="ExternalInput").ap()
           for k, v in arrays.items()}
    out = nc.dram_tensor("out", (B, S, D), F32, kind="ExternalOutput").ap()
    build(nc, aps, out)
    r = run_bass_kernel_spmd(nc, [{f"in_{k}": v for k, v in arrays.items()}], core_ids=[0])
    return r.results[0]["out"]
```
